# Optimizing a Trainium2 kernel written in Bass

```python
import numpy as np
import jax
import jax.numpy as jnp

def _softmax(x, axis=-1):
    return jax.nn.softmax(x, axis=axis)

def _gelu(x):
    return jax.nn.gelu(x, approximate=True)

def _silu(x):
    return jax.nn.silu(x)

def _sigmoid(x):
    return jax.nn.sigmoid(x)

def _layernorm(x, axis=-1, eps=1e-05):
    m = jnp.mean(x, axis=axis, keepdims=True)
    v = jnp.var(x, axis=axis, keepdims=True)
    return (x - m) / jnp.sqrt(v + eps)

def _scatter_add(tgt, idx, src, axis=0):
    return tgt.at[idx].add(src)

def _segment_sum(src, seg, n):
    return jax.ops.segment_sum(src, seg, n)
kernel_name = 'mk_gnn_resnorm_d4_gnn_r32_49a471'

def setup_inputs(seed: int=0):
    np.random.seed(seed)
    _w = jnp.asarray

    def _rec_inputs():
        import jax
        import jax.numpy as jnp
        _gk = jax.random.key(seed)
        x = -0.0002117 + 1 * jax.random.normal(jax.random.fold_in(_gk, 1), (3125, 256), jnp.float32)
        src = jax.random.randint(jax.random.fold_in(_gk, 2), (50000,), 0, 3125, jnp.int32)
        dst = jax.random.randint(jax.random.fold_in(_gk, 3), (50000,), 0, 3125, jnp.int32)
        _o = jnp.argsort(dst, stable=True)
        src = src[_o]
        dst = dst[_o]
        edge_weight = jax.random.uniform(jax.random.fold_in(_gk, 13), (50000,), jnp.float32, 0.0, 1)
        return (x, src, dst, edge_weight)
    x, src, dst, edge_weight = _rec_inputs()

    def _L0_gnn_setup():
        import jax, jax.numpy as jnp
        import numpy as np
        N = 3125
        E = 100000
        IN_F = 256
        OUT_F = 256
        key = jax.random.key(seed)
        k1, k2, k3, k4, k5 = jax.random.split(key, 5)
        stdv = 1.0 / np.sqrt(OUT_F)
        x = jax.random.normal(k1, (N, IN_F), dtype=jnp.float32)
        edge_index = jax.random.randint(k2, (2, E), 0, N, dtype=jnp.int64)
        edge_weight = jax.random.uniform(k3, (E,), dtype=jnp.float32)
        weight = jax.random.uniform(k4, (IN_F, OUT_F), dtype=jnp.float32, minval=-stdv, maxval=stdv)
        bias = jax.random.uniform(k5, (OUT_F,), dtype=jnp.float32, minval=-stdv, maxval=stdv)
        return {'x': x, 'edge_index': edge_index, 'edge_weight': edge_weight, 'weight': weight, 'bias': bias}
    _L0_gnn_all = _L0_gnn_setup()
    _L0_gnn_in = {k: v for k, v in _L0_gnn_all.items() if k in ('weight', 'bias')}
    del _L0_gnn_all

    def _L1_gnn_setup():
        import jax, jax.numpy as jnp
        import numpy as np
        N = 3125
        E = 100000
        F_IN = 256
        F_OUT = 256
        key = jax.random.key(seed)
        k1, k2, k3, k4, k5 = jax.random.split(key, 5)
        x = jax.random.normal(k1, (N, F_IN), dtype=jnp.float32)
        edge_row = jax.random.randint(k2, (E,), 0, N, dtype=jnp.int32)
        edge_col = jax.random.randint(k3, (E,), 0, N, dtype=jnp.int32)
        edge_val = jax.random.uniform(k4, (E,), dtype=jnp.float32)
        W = jax.random.normal(k5, (2 * F_IN, F_OUT), dtype=jnp.float32) * (1.0 / np.sqrt(2 * F_IN))
        b = jnp.zeros((F_OUT,), dtype=jnp.float32)
        return {'x': x, 'edge_row': edge_row, 'edge_col': edge_col, 'edge_val': edge_val, 'W': W, 'b': b}
    _L1_gnn_all = _L1_gnn_setup()
    _L1_gnn_in = {k: v for k, v in _L1_gnn_all.items() if k in ('W', 'b')}
    del _L1_gnn_all

    def _L2_gnn_setup():
        import jax, jax.numpy as jnp
        import numpy as np
        N = 3125
        E = 100000
        DI = 256
        DO = 256
        BN_EPS = 1e-05

        def _bn_relu(h, gamma, beta):
            mean = jnp.mean(h, axis=0)
            var = jnp.var(h, axis=0)
            hn = (h - mean) * jax.lax.rsqrt(var + BN_EPS)
            return jax.nn.relu(hn * gamma + beta)
        key = jax.random.key(seed)
        ks = jax.random.split(key, 6)
        x = jax.random.normal(ks[0], (N, DI), dtype=jnp.float32)
        edge_row = jax.random.randint(ks[1], (E,), 0, N, dtype=jnp.int32)
        edge_col = jax.random.randint(ks[2], (E,), 0, N, dtype=jnp.int32)
        edge_vals = jnp.ones((E,), dtype=jnp.float32)
        eps = jnp.zeros((1,), dtype=jnp.float32)
        W1 = jax.random.normal(ks[3], (DI, DO), dtype=jnp.float32) * 0.05
        b1 = jnp.zeros((DO,), dtype=jnp.float32)
        g1 = jnp.ones((DO,), dtype=jnp.float32)
        be1 = jnp.zeros((DO,), dtype=jnp.float32)
        W2 = jax.random.normal(ks[4], (DO, DO), dtype=jnp.float32) * 0.05
        b2 = jnp.zeros((DO,), dtype=jnp.float32)
        g2 = jnp.ones((DO,), dtype=jnp.float32)
        be2 = jnp.zeros((DO,), dtype=jnp.float32)
        return {'x': x, 'edge_row': edge_row, 'edge_col': edge_col, 'edge_vals': edge_vals, 'eps': eps, 'W1': W1, 'b1': b1, 'g1': g1, 'be1': be1, 'W2': W2, 'b2': b2, 'g2': g2, 'be2': be2}
    _L2_gnn_all = _L2_gnn_setup()
    _L2_gnn_in = {k: v for k, v in _L2_gnn_all.items() if k in ('eps', 'W1', 'b1', 'g1', 'be1', 'W2', 'b2', 'g2', 'be2')}
    del _L2_gnn_all

    def _L3_gnn_setup():
        import jax, jax.numpy as jnp
        import numpy as np
        N = 3125
        E = 25000
        EMB = 256
        HID = 256
        EPS = 1e-05

        def _pool_max(h, edge_src, edge_dst):
            pooled = jax.ops.segment_max(h[edge_src], edge_dst, num_segments=N)
            cnt = jax.ops.segment_sum(jnp.ones((edge_dst.shape[0],), h.dtype), edge_dst, num_segments=N)
            return jnp.where((cnt > 0)[:, None], pooled, jnp.zeros((), h.dtype))

        def _layernorm(x, g, b):
            mu = jnp.mean(x, axis=-1, keepdims=True)
            var = jnp.mean(jnp.square(x - mu), axis=-1, keepdims=True)
            return (x - mu) * jax.lax.rsqrt(var + EPS) * g + b
        key = jax.random.key(seed)
        ks = jax.random.split(key, 12)
        s = 0.05
        return {'embeddings': jax.random.normal(ks[0], (N, EMB), jnp.float32), 'edge_src': jax.random.randint(ks[1], (E,), 0, N, jnp.int32), 'edge_dst': jax.random.randint(ks[2], (E,), 0, N, jnp.int32), 'Wp1': jax.random.normal(ks[3], (HID, EMB), jnp.float32) * s, 'bp1': jnp.zeros((HID,), jnp.float32), 'Wm1': jax.random.normal(ks[4], (HID, EMB + HID), jnp.float32) * s, 'bm1': jnp.zeros((HID,), jnp.float32), 'Wm2': jax.random.normal(ks[5], (HID, 2 * HID), jnp.float32) * s, 'bm2': jnp.zeros((HID,), jnp.float32), 'Wm3': jax.random.normal(ks[6], (HID, 2 * HID), jnp.float32) * s, 'bm3': jnp.zeros((HID,), jnp.float32), 'ln2_g': jnp.ones((HID,), jnp.float32), 'ln2_b': jnp.zeros((HID,), jnp.float32), 'ln3_g': jnp.ones((HID,), jnp.float32), 'ln3_b': jnp.zeros((HID,), jnp.float32)}
    _L3_gnn_all = _L3_gnn_setup()
    _L3_gnn_in = {k: v for k, v in _L3_gnn_all.items() if k in ('Wp1', 'bp1', 'Wm1', 'bm1', 'Wm2', 'bm2', 'Wm3', 'bm3', 'ln2_g', 'ln2_b', 'ln3_g', 'ln3_b')}
    del _L3_gnn_all
    return {'x': x, 'src': src, 'dst': dst, 'edge_weight': edge_weight, 'L0_gnn_weight': _L0_gnn_in['weight'], 'L0_gnn_bias': _L0_gnn_in['bias'], 'L1_gnn_W': _L1_gnn_in['W'], 'L1_gnn_b': _L1_gnn_in['b'], 'L2_gnn_eps': _L2_gnn_in['eps'], 'L2_gnn_W1': _L2_gnn_in['W1'], 'L2_gnn_b1': _L2_gnn_in['b1'], 'L2_gnn_g1': _L2_gnn_in['g1'], 'L2_gnn_be1': _L2_gnn_in['be1'], 'L2_gnn_W2': _L2_gnn_in['W2'], 'L2_gnn_b2': _L2_gnn_in['b2'], 'L2_gnn_g2': _L2_gnn_in['g2'], 'L2_gnn_be2': _L2_gnn_in['be2'], 'L3_gnn_Wp1': _L3_gnn_in['Wp1'], 'L3_gnn_bp1': _L3_gnn_in['bp1'], 'L3_gnn_Wm1': _L3_gnn_in['Wm1'], 'L3_gnn_bm1': _L3_gnn_in['bm1'], 'L3_gnn_Wm2': _L3_gnn_in['Wm2'], 'L3_gnn_bm2': _L3_gnn_in['bm2'], 'L3_gnn_Wm3': _L3_gnn_in['Wm3'], 'L3_gnn_bm3': _L3_gnn_in['bm3'], 'L3_gnn_ln2_g': _L3_gnn_in['ln2_g'], 'L3_gnn_ln2_b': _L3_gnn_in['ln2_b'], 'L3_gnn_ln3_g': _L3_gnn_in['ln3_g'], 'L3_gnn_ln3_b': _L3_gnn_in['ln3_b']}

def reference(x, src, dst, edge_weight, L0_gnn_weight, L0_gnn_bias, L1_gnn_W, L1_gnn_b, L2_gnn_eps, L2_gnn_W1, L2_gnn_b1, L2_gnn_g1, L2_gnn_be1, L2_gnn_W2, L2_gnn_b2, L2_gnn_g2, L2_gnn_be2, L3_gnn_Wp1, L3_gnn_bp1, L3_gnn_Wm1, L3_gnn_bm1, L3_gnn_Wm2, L3_gnn_bm2, L3_gnn_Wm3, L3_gnn_bm3, L3_gnn_ln2_g, L3_gnn_ln2_b, L3_gnn_ln3_g, L3_gnn_ln3_b):
    import jax
    import jax.numpy as jnp

    def _L0_gnn_ref(x, edge_index, edge_weight, weight, bias):
        import jax, jax.numpy as jnp
        import numpy as np
        N = 3125
        E = 100000
        IN_F = 256
        OUT_F = 256
        support = x @ weight
        row, col = (edge_index[0], edge_index[1])
        messages = edge_weight[:, None] * support[col]
        output = jax.ops.segment_sum(messages, row, num_segments=N)
        return output + bias

    def _L1_gnn_ref(x, edge_row, edge_col, edge_val, W, b):
        import jax, jax.numpy as jnp
        import numpy as np
        N = 3125
        E = 100000
        F_IN = 256
        F_OUT = 256
        gathered = edge_val[:, None] * x[edge_col]
        support = jax.ops.segment_sum(gathered, edge_row, num_segments=N)
        h = jnp.concatenate([x, support], axis=1)
        out = h @ W + b
        return jax.nn.relu(out)

    def _L2_gnn_ref(x, edge_row, edge_col, edge_vals, eps, W1, b1, g1, be1, W2, b2, g2, be2):
        import jax, jax.numpy as jnp
        import numpy as np
        N = 3125
        E = 100000
        DI = 256
        DO = 256
        BN_EPS = 1e-05

        def _bn_relu(h, gamma, beta):
            mean = jnp.mean(h, axis=0)
            var = jnp.var(h, axis=0)
            hn = (h - mean) * jax.lax.rsqrt(var + BN_EPS)
            return jax.nn.relu(hn * gamma + beta)
        n = x.shape[0]
        msgs = edge_vals[:, None] * x[edge_col]
        agg = jax.ops.segment_sum(msgs, edge_row, num_segments=n)
        h = (1.0 + eps[0]) * x + agg
        h = _bn_relu(h @ W1 + b1, g1, be1)
        h = _bn_relu(h @ W2 + b2, g2, be2)
        return h

    def _L3_gnn_ref(embeddings, edge_src, edge_dst, Wp1, bp1, Wm1, bm1, Wm2, bm2, Wm3, bm3, ln2_g, ln2_b, ln3_g, ln3_b):
        import jax, jax.numpy as jnp
        import numpy as np
        N = 3125
        E = 25000
        EMB = 256
        HID = 256
        EPS = 1e-05

        def _pool_max(h, edge_src, edge_dst):
            pooled = jax.ops.segment_max(h[edge_src], edge_dst, num_segments=N)
            cnt = jax.ops.segment_sum(jnp.ones((edge_dst.shape[0],), h.dtype), edge_dst, num_segments=N)
            return jnp.where((cnt > 0)[:, None], pooled, jnp.zeros((), h.dtype))

        def _layernorm(x, g, b):
            mu = jnp.mean(x, axis=-1, keepdims=True)
            var = jnp.mean(jnp.square(x - mu), axis=-1, keepdims=True)
            return (x - mu) * jax.lax.rsqrt(var + EPS) * g + b
        h1 = jax.nn.relu(embeddings @ Wp1.T + bp1)
        p1 = _pool_max(h1, edge_src, edge_dst)
        x = jax.nn.relu(jnp.concatenate([embeddings, p1], axis=1) @ Wm1.T + bm1)
        p2 = _pool_max(x, edge_src, edge_dst)
        y2 = jax.nn.relu(jnp.concatenate([x, p2], axis=1) @ Wm2.T + bm2)
        x = _layernorm(y2 + x, ln2_g, ln2_b)
        p3 = _pool_max(x, edge_src, edge_dst)
        y3 = jax.nn.relu(jnp.concatenate([x, p3], axis=1) @ Wm3.T + bm3)
        x = _layernorm(y3 + x, ln3_g, ln3_b)
        return x
    edge_index = jnp.stack([src, dst])
    x = _layernorm(x + _L0_gnn_ref(x, edge_index, edge_weight, L0_gnn_weight, L0_gnn_bias), axis=-1)
    x = _layernorm(x + _L1_gnn_ref(x, src, dst, edge_weight, L1_gnn_W, L1_gnn_b), axis=-1)
    x = _layernorm(x + _L2_gnn_ref(x, src, dst, edge_weight, L2_gnn_eps, L2_gnn_W1, L2_gnn_b1, L2_gnn_g1, L2_gnn_be1, L2_gnn_W2, L2_gnn_b2, L2_gnn_g2, L2_gnn_be2), axis=-1)
    x = _layernorm(x + _L3_gnn_ref(x, src, dst, L3_gnn_Wp1, L3_gnn_bp1, L3_gnn_Wm1, L3_gnn_bm1, L3_gnn_Wm2, L3_gnn_bm2, L3_gnn_Wm3, L3_gnn_bm3, L3_gnn_ln2_g, L3_gnn_ln2_b, L3_gnn_ln3_g, L3_gnn_ln3_b), axis=-1)
    return x

_drawn_inputs = setup_inputs


def setup_inputs(seed=0):
    import zlib

    import numpy as np

    out = dict(_drawn_inputs(seed))
    spreads = {'L1_gnn_b': (0.0, 0.1),
     'L2_gnn_b1': (0.0, 0.1),
     'L2_gnn_g1': (1.0, 0.2),
     'L2_gnn_be1': (0.0, 0.1),
     'L2_gnn_b2': (0.0, 0.1),
     'L2_gnn_g2': (1.0, 0.2),
     'L2_gnn_be2': (0.0, 0.1),
     'L3_gnn_bp1': (0.0, 0.1),
     'L3_gnn_bm1': (0.0, 0.1),
     'L3_gnn_bm2': (0.0, 0.1),
     'L3_gnn_bm3': (0.0, 0.1),
     'L3_gnn_ln2_g': (1.0, 0.2),
     'L3_gnn_ln2_b': (0.0, 0.1),
     'L3_gnn_ln3_g': (1.0, 0.2),
     'L3_gnn_ln3_b': (0.0, 0.1)}
    factors = {}
    for name, (base, spread) in spreads.items():
        noise = np.random.default_rng([zlib.crc32(name.encode()), seed]).standard_normal(out[name].shape)
        drawn = base * np.exp(spread * noise) if base else spread * noise
        out[name] = jnp.asarray(drawn.astype(out[name].dtype))
    for name, factor in factors.items():
        out[name] = (out[name] * factor).astype(out[name].dtype)
    return out
```

```python
from contextlib import ExitStack

import numpy as np

import concourse.bass as bass
from concourse import mybir

P = 128
ALU = mybir.AluOpType
ACT = mybir.ActivationFunctionType
AX = mybir.AxisListType
F32 = mybir.dt.float32
BF16 = mybir.dt.bfloat16
I32 = mybir.dt.int32

N, E, D = 3125, 50000, 256
FH = D // P
NT = -(-N // P)
NP = NT * P
GT = 5
NG = NT // GT
GC = GT * P
PIECE = GC // 2
STREAMS = 4
STEPS = 98
CH = STREAMS * STEPS
EP = CH * P
FAR = (STEPS - 2) * P
PAD_DST = N
END_DST = N + 1
JUNK = NP * NP
A_ROWS = NP + 1
ZERO_ROW = EP
BIG = float(np.finfo(np.float32).max)
EPS = 1e-5
RING = 8
HALF = RING // 2
ROUNDS = CH // RING
LAYERS3 = 3


def build(nc, src_steps, dst_steps, w_steps, src_chunks, dst_flat, x, W0, b0, W1L, b1L, eps, W1, b1, g1, be1,
          W2, b2, g2, be2, Wp, bp, Wm1, bm1, Wm2, bm2, Wm3, bm3, lg2, lb2, lg3, lb3, out):
    A = nc.dram_tensor("adjacency", (A_ROWS * NP, 1), F32, kind="Internal").ap()
    A_rows = A.rearrange("(r c) o -> r (c o)", c=NP)
    H = [nc.dram_tensor(f"pool_in_{l}", (NP, D), F32, kind="Internal").ap() for l in range(LAYERS3)]
    S = [nc.dram_tensor(f"running_max_{l}", (EP + P, D), F32, kind="Internal").ap() for l in range(LAYERS3)]

    with ExitStack() as ctx:
        def sb(name, shape, dt=F32):
            return ctx.enter_context(nc.sbuf_tensor(name, shape, dt))

        def sem(name):
            return ctx.enter_context(nc.semaphore(name))

        XA, XB = sb("XA", [P, NT, D]), sb("XB", [P, NT, D])
        xT = sb("xT", [P, FH, NP])
        BT = sb("BT", [P, FH, NP])
        PG = BT[:, :, :].rearrange("p h n -> p (h n)").rearrange("p (t d) -> p t d", d=D)
        a_ring = sb("a_ring", [P, GT, GC])
        g_ring = sb("g_ring", [P, RING, D])
        s_ring = sb("s_ring", [P, RING, D])
        p_ring = a_ring[:, 0:2, :].rearrange("p a n -> p (a n)").rearrange("p (t d) -> p t d", d=D)
        pT = a_ring[:, 2:4, :].rearrange("p a n -> p (a n)").rearrange("p (t h n) -> p t h n", h=FH, n=P)
        tmp = sb("tmp", [P, GT, D])
        tmpf = tmp[:, :, :].rearrange("p t d -> p (t d)")

        srcS, dstS, wS = sb("srcS", [P, CH], I32), sb("dstS", [P, CH], I32), sb("wS", [P, CH])
        key, junk = sb("key", [P, CH]), sb("junk", [P, CH])
        node_lo, node_hi = sb("node_lo", [P, CH]), sb("node_hi", [P, CH])
        srcC, dstC = sb("srcC", [P, CH], I32), sb("dstC", [P, CH], I32)
        dst_next, dst_far = sb("dst_next", [P, CH], I32), sb("dst_far", [P, CH], I32)
        seg = sb("seg", [P, CH])
        eq = sb("eq", [P, CH])
        last_before = sb("last_before", [P, 1], I32)
        carry_mask = sb("carry_mask", [P, 1])
        whole_mask = sb("whole_mask", [P, 1])
        whole_row = sb("whole_row", [P, P])
        col = sb("col", [P, 16])
        fix_row = sb("fix_row", [P, 1], I32)
        end_row = sb("end_row", [P, NT], I32)
        cnt, incl, ends = sb("cnt", [P, NT]), sb("incl", [P, NT]), sb("ends", [P, NT])
        flag = sb("flag", [1, 1], I32)
        flagf = sb("flagf", [1, 1])

        ident, ones = sb("ident", [P, P]), sb("ones", [P, P])
        before = sb("before", [P, P])
        upto = sb("upto", [P, P])
        row0 = sb("row0", [P, P])
        iota_i = sb("iota_i", [P, P], I32)
        iota_f = sb("iota_f", [P, P])
        key_cols, w_cols = sb("key_cols", [P, 2, STREAMS]), sb("w_cols", [P, 2, STREAMS])
        w_rows = sb("w_rows", [P, 2, STREAMS, P])
        unused = sb("unused", [P, 2 * STREAMS, P], BF16)
        hot_lo = sb("hot_lo", [P, 2, STREAMS, P], BF16)
        hot_hi = sb("hot_hi", [P, 2, STREAMS, NT], BF16)
        w_out = sb("w_out", [P, 2, STREAMS])
        repeats = sb("repeats", [P, 2, STREAMS])
        moved = sb("moved", [P, 2, STREAMS])
        idx_out = sb("idx_out", [P, 2, STREAMS], I32)
        src_idx = sb("src_idx", [P, RING], I32)

        stats = sb("stats", [P, GT, 6])
        mv = sb("mv", [P, GT, 2])
        sd, rstd = sb("sd", [P, GT]), sb("rstd", [P, GT])
        bn_stat = sb("bn_stat", [P, FH, 7, 6])
        bn_mv = sb("bn_mv", [P, FH, 2])
        bn_sd, bn_scale, bn_shift, bn_ms = (sb(n, [P, FH]) for n in ("bn_sd", "bn_scale", "bn_shift", "bn_ms"))
        eps_col = sb("eps_col", [P, 1])
        eps1 = sb("eps1", [P, 1])

        RT = sb("RT", [P, FH, P + 1])
        fix_old, fix_new = sb("fix_old", [P, D]), sb("fix_new", [P, D])

        def weight(name, w):
            return sb(name, [P, w.shape[0] // P, D]), w.rearrange("(h p) n -> p h n", p=P)

        W0s, W1Ls, W1s, W2s, Wps, Wm1s, Wm2s, Wm3s = weights = [
            weight(n, w) for n, w in (("W0s", W0), ("W1Ls", W1L), ("W1s", W1), ("W2s", W2), ("Wps", Wp),
                                      ("Wm1s", Wm1), ("Wm2s", Wm2), ("Wm3s", Wm3))]
        W0s, W1Ls, W1s, W2s, Wps, Wm1s, Wm2s, Wm3s = (w[0] for w in weights)
        rows = {}
        for name, v in (("b0", b0), ("b1L", b1L), ("bp", bp), ("bm1", bm1), ("bm2", bm2), ("bm3", bm3),
                        ("lg2", lg2), ("lb2", lb2), ("lg3", lg3), ("lb3", lb3)):
            rows[name] = (sb(f"row_{name}", [P, D]), v)
        cols = {}
        for name, v in (("b1", b1), ("g1", g1), ("be1", be1), ("b2", b2), ("g2", g2), ("be2", be2)):
            cols[name] = (sb(f"col_{name}", [P, FH]), v)

        bank = [ctx.enter_context(nc.psum_tensor(f"bank{i}", [P, 512], F32)) for i in range(8)]

        def row_group(name):
            return rows[name][0][:, :].unsqueeze(1).to_broadcast([P, GT, D])

        edges_in = sem("edges_in")
        x_in, x_zero = sem("x_in"), sem("x_zero")
        weights_in = sem("weights_in")
        eps_in = sem("eps_in")
        zeros_ready, a_zeroed = sem("zeros_ready"), sem("a_zeroed")
        zero_row_in = sem("zero_row_in")
        pool_const = sem("pool_const")
        dve = sem("dve")
        cols_ready, rows_ready, w_rows_ready, rows_read = (
            sem(n) for n in ("cols_ready", "rows_ready", "w_rows_ready", "rows_read"))
        hot_ready, hist_done = sem("hot_ready"), sem("hist_done")
        merged, scatter_ready = sem("merged"), sem("scatter_ready")
        scattered = [sem(f"scattered{q}") for q in range(STREAMS)]
        pe_small = sem("pe_small")
        small_ready = sem("small_ready")
        flag_ready = sem("flag_ready")
        a_in = [sem(f"a_in{j}") for j in range(GT)]
        a_used = sem("a_used")
        y_out = sem("y_out")
        t_ready, t_free = sem("t_ready"), sem("t_free")
        z_ready, z_free = sem("z_ready"), sem("z_free")
        tp_ready, tp_free, tp_copied = sem("tp_ready"), sem("tp_free"), sem("tp_copied")
        back_ready, back_free = sem("back_ready"), sem("back_free")
        x_ready = sem("x_ready")
        var_ready, sd_ready = sem("var_ready"), sem("sd_ready")
        bn_var, bn_sd_ready, bn_ready = sem("bn_var"), sem("bn_sd_ready"), sem("bn_ready")
        r_ready = sem("r_ready")
        h_ready, h_stored = sem("h_ready"), sem("h_stored")
        idx_ready = sem("idx_ready")
        gathered = [sem(f"gathered{u}") for u in range(RING)]
        max_done = sem("max_done")
        max_stored = [sem("max_stored0"), sem("max_stored1")]
        fix_read, fix_T, fix_scan, fix_back, fix_ready, fix_written = (
            sem(n) for n in ("fix_read", "fix_T", "fix_scan", "fix_back", "fix_ready", "fix_written"))
        pooled = [sem(f"pooled{j}") for j in range(GT)]
        out_ready, out_stored = sem("out_ready"), sem("out_stored")
        tick = {n: sem(f"tick_{n}") for n in ("sp", "act", "pe", "dve", "pool")}

        def hold(eng, name, s, value):
            eng.wait_ge(s, value)
            eng.sem_inc(tick[name], 1)

        N_EDGE_LOADS = 8
        N_WEIGHT_LOADS = len(weights) + len(rows) + len(cols)
        Z = {"L0": 0, "L1": 1, "prep": 2, "part0": 3, "post0": 4, "part1": 5, "post1": 6, "part2": 7, "post2": 8}
        TP = {"L1": 0, "L2": 1, "prep": 2, "post0": 3, "part1": 4, "post1": 5, "part2": 6, "post2": 7}
        XR = {"L0": 0, "L1": 1, "L2": 2, "post0": 3, "post1": 4}
        LN = {"L0": 0, "L1": 1, "L2": 2, "post1": 3, "post2": 4}

        def ln(stage, c):
            if stage == "out":
                return LN["post2"] * NG + 2 * c + 1
            return LN[stage] * NG + c * (2 if stage == "post2" else 1)

        block = ctx.enter_context(nc.Block())

        @block.sync
        def _(sp):
            flat = dst_flat.rearrange("(a e) -> a e", a=1)

            def stretch(shift):
                return dst_flat[shift:shift + EP].rearrange("(p t) -> p t", p=P)

            sp.dma_start(srcS[:, :], src_steps).then_inc(edges_in, 16)
            sp.dma_start(dstS[:, :], dst_steps).then_inc(edges_in, 16)
            sp.dma_start(wS[:, :], w_steps).then_inc(edges_in, 16)
            sp.dma_start(srcC[:, :], src_chunks).then_inc(edges_in, 16)
            sp.dma_start(dstC[:, :], stretch(0)).then_inc(edges_in, 16)
            sp.dma_start(dst_next[:, :], stretch(1)).then_inc(edges_in, 16)
            sp.dma_start(dst_far[:, :], stretch(FAR)).then_inc(edges_in, 16)
            sp.wait_ge(x_zero, 1)
            sp.dma_start(last_before[1:P, :], stretch(0)[0:P - 1, CH - 1:CH], allow_slow_non_contiguous=True).then_inc(edges_in, 16)
            sp.wait_ge(zeros_ready, 1)
            for t in range(NT):
                sp.dma_start(A_rows[t * P:(t + 1) * P, :], BT[:, 0, :]).then_inc(a_zeroed, 16)
            sp.dma_start(A_rows[NP:NP + 1, :].rearrange("o (p c) -> (o p) c", p=P), BT[:, 0, 0:NT]).then_inc(a_zeroed, 16)
            for l in range(LAYERS3):
                sp.dma_start(S[l][ZERO_ROW:ZERO_ROW + P, :], BT[:, 0, 0:D]).then_inc(zero_row_in, 16)
            full = N // P
            sp.dma_start(XA[:, 0:full, :], x[0:full * P, :].rearrange("(t p) d -> p t d", p=P)).then_inc(x_in, 16)
            sp.dma_start(XA[0:N - full * P, full, :], x[full * P:N, :]).then_inc(x_in, 16)
            sp.dma_start(eps1[:, :], eps.rearrange("(a b) -> a b", a=1).to_broadcast([P, 1])).then_inc(eps_in, 16)
            for tile, view in weights:
                sp.dma_start(tile[:, :, :], view).then_inc(weights_in, 16)
            for tile, v in rows.values():
                sp.dma_start(tile[:, :], v.rearrange("(a n) -> a n", a=1).to_broadcast([P, D])).then_inc(weights_in, 16)
            for tile, v in cols.values():
                sp.dma_start(tile[:, :], v.rearrange("(h p) -> p h", p=P), allow_slow_non_contiguous=True).then_inc(weights_in, 16)

            for q in range(STREAMS):
                sp.wait_ge(scattered[q], 16 * STEPS)
            sp.wait_ge(zero_row_in, 16 * LAYERS3)
            for layer in range(3):
                with sp.Fori(0, NG) as c:
                    with sp.Fori(0, NG) as k:
                        m = layer * NT + NG * c + k
                        for j in range(GT):
                            hold(sp, "sp", a_used, m * GT + j + 1)
                            sp.dma_start(a_ring[:, j, :], A_rows[bass.ds((k * GT + j) * P, P), bass.ds(c * GC, GC)]).then_inc(a_in[j], 16)

            def store_rows(l):
                for c in range(NG):
                    if l:
                        sp.wait_ge(x_ready, NG * XR[f"post{l - 1}"] + c + 1)
                    else:
                        sp.wait_ge(h_ready, c + 1)
                    sp.dma_start(H[l][c * GC:(c + 1) * GC, :].rearrange("(t p) d -> p t d", p=P),
                                 XA[:, c * GT:(c + 1) * GT, :]).then_inc(h_stored, 16)

            for l in range(LAYERS3):
                store_rows(l)
                running = S[l][0:EP, :].rearrange("(p t) d -> p (t d)", p=P)
                with sp.Fori(0, ROUNDS) as i:
                    for h in range(2):
                        hold(sp, "sp", max_done, RING + l * CH + RING * i + HALF * (h + 1))
                        sp.dma_start(running[:, bass.ds((RING * i + HALF * h) * D, HALF * D)],
                                     s_ring[:, HALF * h:HALF * (h + 1), :].rearrange("p t d -> p (t d)")).then_inc(max_stored[h], 16)
            for c in range(NG):
                sp.wait_ge(out_ready, c + 1)
                for j in range(GT):
                    t = c * GT + j
                    n = min(P, N - t * P)
                    sp.dma_start(out[t * P:t * P + n, :], XA[0:n, t, :]).then_inc(out_stored, 16)
            sp.wait_ge(out_stored, 16 * NT)

        @block.gpsimd
        def _(pool):
            pool.memset(BT[:, 0, :], 0.0).then_inc(zeros_ready, 1)
            pool.memset(last_before[:, :], -1)
            pool.memset(XA[:, NT - 1, :], 0.0).then_inc(x_zero, 1)
            pool.memset(ones[:, :], 1.0)
            pool.memset(eps_col[:, :], EPS)
            pool.memset(s_ring[:, :, :], 0.0)
            pool.memset(RT[:, :, :], -BIG).then_inc(pool_const, 1)
            pool.wait_ge(pool_const, 1)
            pool.affine_select(out=ident[:, :], in_=ones[:, :], compare_op=ALU.is_equal, fill=0.0, base=0,
                               pattern=[[-1, P]], channel_multiplier=1)
            pool.affine_select(out=before[:, :], in_=ones[:, :], compare_op=ALU.is_gt, fill=0.0, base=0,
                               pattern=[[-1, P]], channel_multiplier=1)
            pool.affine_select(out=upto[:, :], in_=ones[:, :], compare_op=ALU.is_ge, fill=0.0, base=0,
                               pattern=[[1, P]], channel_multiplier=-1)
            pool.affine_select(out=row0[:, :], in_=ones[:, :], compare_op=ALU.is_equal, fill=0.0, base=0,
                               pattern=[[0, P]], channel_multiplier=1)
            pool.iota(iota_i[:, :], pattern=[[1, P]], base=0, channel_multiplier=0).then_inc(pool_const, 1)
            pool.wait_ge(small_ready, 1)
            pool.iota(srcS[:, :].rearrange("p (s q) -> p s q", q=STREAMS), pattern=[[0, STEPS], [P, STREAMS]],
                      base=JUNK, channel_multiplier=1)
            pool.iota(fix_row[:, :], pattern=[[0, 1]], base=-1, channel_multiplier=CH).then_inc(pool_const, 1)

            pool.wait_ge(flag_ready, 1)
            serial = pool.value_load(flag[0:1, 0:1], min_val=0, max_val=1)
            pool.wait_ge(a_zeroed, 16 * (NT + 1))

            def scatter(q, h):
                pool.indirect_dma_start(out=A, out_offset=bass.IndirectOffsetOnAxis(ap=idx_out[:, h, q:q + 1], axis=0),
                                        in_=w_out[:, h, q:q + 1], in_offset=None,
                                        compute_op=ALU.add).then_inc(scattered[q], 16)

            def scatter_all(serially):
                for s in range(2):
                    pool.wait_ge(scatter_ready, s + 1)
                    for q in range(STREAMS):
                        before = (q - 1) % STREAMS if serially else q
                        done = s + 1 if serially and q else s
                        if done:
                            pool.wait_ge(scattered[before], 16 * done)
                        scatter(q, s)
                with pool.Fori(1, STEPS // 2) as i:
                    for h in range(2):
                        s = 2 * i + h
                        hold(pool, "pool", scatter_ready, s + 1)
                        for q in range(STREAMS):
                            if serially:
                                hold(pool, "pool", scattered[(q - 1) % STREAMS], 16 * (s + 1 if q else s))
                            else:
                                hold(pool, "pool", scattered[q], 16 * s)
                            scatter(q, h)

            with pool.If(serial):
                scatter_all(True)
            with pool.Else():
                scatter_all(False)

            for l in range(LAYERS3):
                pool.wait_ge(h_stored, 16 * NG * (l + 1))

                with pool.Fori(0, ROUNDS) as i:
                    for u in range(RING):
                        if u % HALF == 0:
                            hold(pool, "pool", idx_ready, l * 2 * ROUNDS + 2 * i + u // HALF + 1)
                        hold(pool, "pool", max_done, l * CH + RING * i + u + 1)
                        pool.indirect_dma_start(out=g_ring[:, u, :], out_offset=None, in_=H[l],
                                                in_offset=bass.IndirectOffsetOnAxis(ap=src_idx[:, u:u + 1], axis=0)
                                                ).then_inc(gathered[u], 16)

                for h in range(2):
                    pool.wait_ge(max_stored[h], 16 * ROUNDS * (l + 1))
                pool.indirect_dma_start(out=fix_old[:, :], out_offset=None, in_=S[l],
                                        in_offset=bass.IndirectOffsetOnAxis(ap=fix_row[:, 0:1], axis=0)).then_inc(fix_read, 16)
                pool.wait_ge(fix_ready, l + 1)
                pool.indirect_dma_start(out=S[l], out_offset=bass.IndirectOffsetOnAxis(ap=fix_row[:, 0:1], axis=0),
                                        in_=fix_new[:, :], in_offset=None).then_inc(fix_written, 16)
                pool.wait_ge(fix_written, 16 * (l + 1))
                if l == 0:
                    pool.wait_ge(zero_row_in, 16 * LAYERS3)
                for t in range(NT):
                    if l or t >= GT:
                        pool.wait_ge(tp_ready, TP[f"post{l}"] * NT + t - GT + 1)
                    pool.indirect_dma_start(out=p_ring[:, t % GT, :], out_offset=None, in_=S[l],
                                            in_offset=bass.IndirectOffsetOnAxis(ap=end_row[:, t:t + 1], axis=0)
                                            ).then_inc(pooled[t % GT], 16)

        @block.vector
        def _(v):
            chain = [0]

            def link(ins):
                chain[0] += 1
                ins.then_inc(dve, 1)
                v.wait_ge(dve, chain[0])

            v.sem_inc(rows_read, 2)
            v.sem_inc(z_free, 1)
            v.sem_inc(max_done, RING)
            v.sem_inc(back_free, 1)

            v.wait_ge(edges_in, 16 * N_EDGE_LOADS)
            v.tensor_copy(junk[:, :], srcS[:, :])
            link(v.tensor_copy(eq[:, :], dstS[:, :]))
            v.tensor_scalar(node_lo[:, :].bitcast(I32), dstS[:, :], P - 1, None, ALU.bitwise_and)
            v.tensor_scalar(node_hi[:, :].bitcast(I32), dstS[:, :], 7, None, ALU.logical_shift_right)
            link(v.scalar_tensor_tensor(out=key[:, :], in0=eq[:, :], scalar=float(NP), in1=junk[:, :], op0=ALU.mult, op1=ALU.add))
            v.tensor_copy(node_lo[:, :], node_lo[:, :].bitcast(I32))
            v.tensor_copy(node_hi[:, :], node_hi[:, :].bitcast(I32)).then_inc(small_ready, 1)
            v.wait_ge(pool_const, 3)
            v.tensor_copy(iota_f[:, :], iota_i[:, :])
            link(v.tensor_copy(junk[:, :], srcS[:, :]))
            link(v.tensor_tensor(junk[:, :], junk[:, :], key[:, :], ALU.subtract))
            v.tensor_tensor(eq[:, :], dstC[:, :], dst_next[:, :], ALU.is_gt)
            link(v.tensor_tensor(seg[:, :], dstC[:, :], dst_far[:, :], ALU.is_ge))
            link(v.tensor_tensor(eq[:, :], eq[:, :], seg[:, :], ALU.max))
            v.tensor_reduce(col[:, 0:1], eq[:, :], AX.X, ALU.max).then_inc(small_ready, 1)
            v.wait_ge(pe_small, 1)
            link(v.tensor_reduce(flagf[:, :], bank[7][0:1, 0:P], AX.X, ALU.max))
            v.tensor_copy(flag[:, :], flagf[:, :]).then_inc(flag_ready, 1)

            def merge(i, h, first=False):
                s = 2 * i + h
                if first:
                    v.wait_ge(hist_done, s + 1)
                else:
                    hold(v, "dve", hist_done, s + 1)
                at = STREAMS * s
                for u in range(STREAMS):
                    v.tensor_scalar(hot_lo[:, h, u, :], iota_f[:, :], node_lo[:, bass.ds(at + u, 1)], None, ALU.is_equal)
                v.tensor_tensor(hot_hi[:, h, :, :], node_hi[:, bass.ds(at, STREAMS)].unsqueeze(2).to_broadcast([P, STREAMS, NT]),
                                iota_f[:, 0:NT].unsqueeze(1).to_broadcast([P, STREAMS, NT]), ALU.is_equal).then_inc(hot_ready, 1)
                hold(v, "dve", rows_ready, s + 3)
                hold(v, "dve", w_rows_ready, s + 1)
                if not first:
                    for q in range(STREAMS):
                        hold(v, "dve", scattered[q], 16 * (s - 1))
                for u in range(STREAMS):
                    v.scalar_tensor_tensor(out=unused[:, 2 * u, :], in0=bank[2 * h][:, u * P:(u + 1) * P], scalar=key[:, bass.ds(at + u, 1)],
                                           in1=w_rows[:, h, u, :], op0=ALU.is_equal, op1=ALU.mult,
                                           accum_out=w_out[:, h, u:u + 1])
                    last = v.scalar_tensor_tensor(out=unused[:, 2 * u + 1, :], in0=bank[2 * h][:, u * P:(u + 1) * P],
                                                  scalar=key[:, bass.ds(at + u, 1)], in1=before[:, :],
                                                  op0=ALU.is_equal, op1=ALU.mult, accum_out=repeats[:, h, u:u + 1])
                last.then_inc(rows_read, 1)
                hold(v, "dve", rows_read, s + 3)
                v.scalar_tensor_tensor(out=moved[:, h, :], in0=repeats[:, h, :], scalar=1.0, in1=junk[:, bass.ds(at, STREAMS)],
                                       op0=ALU.min, op1=ALU.mult).then_inc(merged, 1)
                hold(v, "dve", merged, s + 1)
                v.tensor_tensor(idx_out[:, h, :], moved[:, h, :], key[:, bass.ds(at, STREAMS)], ALU.add).then_inc(scatter_ready, 1)

            merge(0, 0, True)
            merge(0, 1, True)
            with v.Fori(1, STEPS // 2) as i:
                merge(i, 0)
                merge(i, 1)

            link(v.tensor_copy(eq[:, :], dstC[:, :]))
            v.memset(seg[:, 0:1], 0.0)
            v.tensor_tensor(seg[:, 1:CH], eq[:, 1:CH], eq[:, 0:CH - 1], ALU.is_equal)
            v.tensor_copy(col[:, 1:2], last_before[:, :])
            link(v.tensor_copy(col[:, 2:3], fix_row[:, :]))
            v.tensor_tensor(carry_mask[:, :], eq[:, 0:1], col[:, 1:2], ALU.is_equal)
            v.tensor_tensor(whole_mask[:, :], eq[:, CH - 1:CH], col[:, 1:2], ALU.is_equal)
            link(v.tensor_scalar(node_lo[:, :], eq[:, :], eq[:, 0:1], None, ALU.is_equal))
            for m in (seg, carry_mask, whole_mask):
                last = v.tensor_scalar(m[:, :], m[:, :], 2.0, -1.0, ALU.mult, ALU.add)
            v.tensor_reduce(col[:, 3:4], node_lo[:, :], AX.X, ALU.add)
            v.wait_ge(hist_done, 2 + STEPS)
            link(v.tensor_copy(cnt[:, :], bank[4][:, 0:NT]))
            for m in (seg, carry_mask):
                v.tensor_scalar(m[:, :], m[:, :], BIG, None, ALU.mult)
            v.tensor_scalar(whole_mask[:, :], whole_mask[:, :], BIG, None, ALU.mult)
            v.tensor_tensor(fix_row[:, :], col[:, 2:3], col[:, 3:4], ALU.add).then_inc(small_ready, 1)
            v.wait_ge(pe_small, 2)
            v.tensor_copy(whole_row[:, :], bank[7][:, 0:P])
            link(v.tensor_copy(ends[:, :], bank[6][:, NT:2 * NT]))
            link(v.tensor_tensor_scan(incl[:, :], ones[:, 0:NT], ends[:, :], 0.0, ALU.mult, ALU.add))
            link(v.tensor_tensor(incl[:, :], incl[:, :], ends[:, :], ALU.subtract))
            link(v.tensor_tensor(incl[:, :], incl[:, :], bank[6][:, 0:NT], ALU.add))
            link(v.tensor_scalar(incl[:, :], incl[:, :], -1.0, None, ALU.add))
            v.tensor_scalar(ends[:, :], incl[:, :], -1.0, float(ZERO_ROW), ALU.mult, ALU.add)
            link(v.tensor_scalar(cnt[:, :], cnt[:, :], 0.0, None, ALU.is_equal))
            link(v.tensor_tensor(ends[:, :], ends[:, :], cnt[:, :], ALU.mult))
            link(v.tensor_tensor(end_row[:, :], ends[:, :], incl[:, :], ALU.add))
            v.wait_ge(eps_in, 16)
            v.tensor_scalar(eps1[:, :], eps1[:, :], 1.0, None, ALU.add).then_inc(small_ready, 1)

            class trip:
                def __init__(self, i, start, per):
                    self.value, self.n, self.per = start + i * per, 0, per

                def link(self, ins):
                    self.n += 1
                    ins.then_inc(dve, 1)
                    hold(v, "dve", dve, self.value + self.n)

            def evacuate(c, layer):
                hold(v, "dve", a_used, GT + NT * (NG * layer + c + 1))
                for f in (range(FH) if layer == 2 else (1,)):
                    for o in range(2):
                        at = c * GC + o * PIECE
                        dst, y = BT[:, f, bass.ds(at, PIECE)], bank[2 * f + o][:, 0:PIECE]
                        if layer == 2:
                            v.scalar_tensor_tensor(out=dst, in0=xT[:, f, bass.ds(at, PIECE)], scalar=eps1[:, 0:1], in1=y,
                                                   op0=ALU.mult, op1=ALU.add).then_inc(y_out, 1)
                        else:
                            v.tensor_copy(dst, y).then_inc(y_out, 1)

            def deviations(ch, n):
                for j in range(GT):
                    last = v.bn_stats(stats[:, j, :], tmp[:, j, :])
                ch.link(last)
                for j in range(GT):
                    last = v.bn_aggr(mv[:, j, :], stats[:, j, :])
                last.then_inc(var_ready, 1)
                hold(v, "dve", sd_ready, n + 1)
                ch.link(v.reciprocal(rstd[:, :], sd[:, :]))

            def normalise(ch, n, dst):
                deviations(ch, n)
                for j in range(GT):
                    last = v.tensor_scalar(dst(j), tmp[:, j, :], mv[:, j, 0:1], rstd[:, j:j + 1], ALU.subtract, ALU.mult)
                return last

            def take(ch, c, r, other):
                for j in range(GT):
                    hold(v, "dve", z_ready, NT * r + GT * c + j + 1)
                    v.tensor_tensor(tmp[:, j, :], bank[4 + j % 2][:, 0:D], other(j), ALU.add).then_inc(z_free, 1)
                hold(v, "dve", z_free, NT * r + GT * c + GT + 1)

            def tiles(X, c):
                return X[:, bass.ds(c * GT, GT), :]

            def tiles0(c, start):
                ch = trip(c, start, 3)
                take(ch, c, Z["L0"], lambda j: XA[:, bass.ds(c * GT + j, 1), :].rearrange("p t d -> p (t d)"))
                ch.link(v.tensor_tensor(tmp[:, :, :], tmp[:, :, :], row_group("b0"), ALU.add))
                normalise(ch, ln("L0", c), lambda j: XB[:, bass.ds(c * GT + j, 1), :].rearrange("p t d -> p (t d)")
                          ).then_inc(x_ready, 1)
                hold(v, "dve", x_ready, XR["L0"] * NG + c + 1)

            def tiles1(c, start):
                ch = trip(c, start, 3)
                take(ch, c, Z["L1"], lambda j: rows["b1L"][0][:, :])
                ch.link(v.scalar_tensor_tensor(out=tmpf, in0=tmpf, scalar=0.0, in1=tiles(XB, c).rearrange("p t d -> p (t d)"),
                                               op0=ALU.max, op1=ALU.add))
                normalise(ch, ln("L1", c), lambda j: XA[:, bass.ds(c * GT + j, 1), :].rearrange("p t d -> p (t d)")
                          ).then_inc(x_ready, 1)
                hold(v, "dve", x_ready, XR["L1"] * NG + c + 1)

            v.wait_ge(x_in, 32)
            v.wait_ge(weights_in, 16 * N_WEIGHT_LOADS)
            for layer, body in ((0, tiles0), (1, tiles1)):
                evacuate(0, layer)
                start = chain[0]
                with v.Fori(1, NG) as c:
                    evacuate(c, layer)
                    body(c - 1, start)
                body(NG - 1, start)
                chain[0] = start + 3 * NG

            with v.Fori(0, NG) as c:
                evacuate(c, 2)

            def batch_norm(n, g, be):
                v.wait_ge(t_free, 2 + 4 * NG * (n + 1))
                for f in range(FH):
                    for k in range(7):
                        lo, hi = 512 * k, min(512 * k + 512, N)
                        last = v.bn_stats(bn_stat[:, f, k, :], xT[:, f, lo:hi])
                link(last)
                for f in range(FH):
                    last = v.bn_aggr(bn_mv[:, f, :], bn_stat[:, f, :, :].rearrange("p k s -> p (k s)"))
                last.then_inc(bn_var, 1)
                v.wait_ge(bn_sd_ready, n + 1)
                link(v.reciprocal(bn_scale[:, :], bn_sd[:, :]))
                link(v.tensor_tensor(bn_scale[:, :], bn_scale[:, :], cols[g][0][:, :], ALU.mult))
                link(v.tensor_tensor(bn_ms[:, :], bn_mv[:, :, 0], bn_scale[:, :], ALU.mult))
                v.tensor_tensor(bn_shift[:, :], cols[be][0][:, :], bn_ms[:, :], ALU.subtract).then_inc(bn_ready, 1)

            batch_norm(0, "g1", "be1")
            batch_norm(1, "g2", "be2")
            def tiles2(c, start):
                ch = trip(c, start, 2)
                for j in range(GT):
                    hold(v, "dve", back_ready, GT * c + j + 1)
                    v.tensor_tensor(tmp[:, j, :], bank[j % 2][:, 0:D],
                                    XA[:, bass.ds(c * GT + j, 1), :].rearrange("p t d -> p (t d)"), ALU.add).then_inc(back_free, 1)
                hold(v, "dve", back_free, GT * c + GT + 1)
                normalise(ch, ln("L2", c), lambda j: XB[:, bass.ds(c * GT + j, 1), :].rearrange("p t d -> p (t d)")
                          ).then_inc(x_ready, 1)
                hold(v, "dve", x_ready, XR["L2"] * NG + c + 1)

            def prepare(c):
                take(None, c, Z["prep"], lambda j: rows["bp"][0][:, :])
                v.tensor_scalar(tiles(XA, c).rearrange("p t d -> p (t d)"), tmpf, 0.0, None, ALU.max).then_inc(h_ready, 1)
                hold(v, "dve", h_ready, c + 1)

            start = chain[0]
            tiles2(0, start)
            with v.Fori(1, NG) as c:
                tiles2(c, start)
                prepare(c - 1)
            prepare(NG - 1)
            chain[0] = start + 2 * NG

            def running_max(l, i, first=False):
                for u in range(RING):
                    if u % HALF == 0 and not first:
                        hold(v, "dve", max_stored[u // HALF], 16 * (l * ROUNDS + i))
                    hold(v, "dve", gathered[u], 16 * (l * ROUNDS + i + 1))
                    hold(v, "dve", max_done, RING + l * CH + RING * i + u)
                    v.scalar_tensor_tensor(out=s_ring[:, u, :], in0=s_ring[:, (u - 1) % RING, :],
                                           scalar=seg[:, bass.ds(RING * i + u, 1)], in1=g_ring[:, u, :],
                                           op0=ALU.min, op1=ALU.max).then_inc(max_done, 1)

            for l in range(LAYERS3):
                if l == 0:
                    running_max(l, 0, True)
                with v.Fori(1 if l == 0 else 0, ROUNDS) as i:
                    running_max(l, i)
                v.wait_ge(fix_T, l + 1)
                for f in range(FH):
                    last = v.tensor_tensor_scan(RT[:, f, 1:P + 1], whole_row[:, :], bank[0][:, f * P:(f + 1) * P], -BIG,
                                                ALU.min, ALU.max)
                last.then_inc(fix_scan, 1)
                v.wait_ge(fix_back, l + 1)
                v.wait_ge(fix_read, 16 * (l + 1))
                v.scalar_tensor_tensor(out=fix_new[:, :], in0=bank[1][:, 0:D], scalar=carry_mask[:, 0:1], in1=fix_old[:, :],
                                       op0=ALU.min, op1=ALU.max).then_inc(fix_ready, 1)
                if l == 0:
                    for c in range(NG):
                        last = v.tensor_tensor(XB[:, c * GT:(c + 1) * GT, :], XB[:, c * GT:(c + 1) * GT, :], row_group("lb3"), ALU.add)
                    link(last)

                start = chain[0]
                per = (0, 4, 7)[l]
                with v.Fori(0, NG) as c:
                    ch = trip(c, start, per)
                    take(ch, c, Z[f"post{l}"], lambda j: PG[:, bass.ds(c * GT + j, 1), :].rearrange("p t d -> p (t d)"))
                    xg = tiles(XA, c).rearrange("p t d -> p (t d)")
                    if l == 0:
                        v.tensor_scalar(xg, tmpf, 0.0, None, ALU.max).then_inc(x_ready, 1)
                    else:
                        g, b = rows[f"lg{l + 1}"][0], rows[f"lb{l + 1}"][0]
                        ch.link(v.scalar_tensor_tensor(out=tmpf, in0=tmpf, scalar=0.0, in1=xg, op0=ALU.max, op1=ALU.add))
                        deviations(ch, ln(f"post{l}", c))
                        for j in range(GT):
                            last = v.scalar_tensor_tensor(out=tmp[:, j, :], in0=tmp[:, j, :], scalar=mv[:, j, 0:1], in1=g[:, :],
                                                          op0=ALU.subtract, op1=ALU.mult)
                        ch.link(last)
                    if l == 1:
                        for j in range(GT):
                            last = v.scalar_tensor_tensor(out=XA[:, bass.ds(c * GT + j, 1), :].rearrange("p t d -> p (t d)"),
                                                          in0=tmp[:, j, :], scalar=rstd[:, j:j + 1], in1=b[:, :],
                                                          op0=ALU.mult, op1=ALU.add)
                        last.then_inc(x_ready, 1)
                    if l == 2:
                        for j in range(GT):
                            last = v.scalar_tensor_tensor(out=tmp[:, j, :], in0=tmp[:, j, :], scalar=rstd[:, j:j + 1],
                                                          in1=XB[:, bass.ds(c * GT + j, 1), :].rearrange("p t d -> p (t d)"),
                                                          op0=ALU.mult, op1=ALU.add)
                        ch.link(last)
                        normalise(ch, ln("out", c), lambda j: XA[:, bass.ds(c * GT + j, 1), :].rearrange("p t d -> p (t d)")
                                  ).then_inc(out_ready, 1)
                    if l < 2:
                        hold(v, "dve", x_ready, XR[f"post{l}"] * NG + c + 1)
                    else:
                        hold(v, "dve", out_ready, c + 1)
                    assert ch.n == per, (l, ch.n, per)
                chain[0] = start + per * NG

        @block.scalar
        def _(act):
            act.sem_inc(tp_free, 1)
            act.sem_inc(t_free, 2)
            def copy_cols(i, h):
                s = 2 * i + h
                hold(act, "act", rows_ready, s + 1)
                act.activation(key_cols[:, h, :], key[:, bass.ds(STREAMS * s, STREAMS)], ACT.Copy)
                act.activation(w_cols[:, h, :], wS[:, bass.ds(STREAMS * s, STREAMS)], ACT.Copy).then_inc(cols_ready, 1)

            def copy_rows(i, h):
                s = 2 * i + h
                hold(act, "act", rows_read, s + 1)
                hold(act, "act", rows_ready, s + 3)
                act.activation(w_rows[:, h, :, :].rearrange("p q n -> p (q n)"), bank[2 * h + 1][:, :], ACT.Copy).then_inc(w_rows_ready, 1)

            act.wait_ge(small_ready, 1)
            for h in range(2):
                copy_cols(0, h)
            with act.Fori(0, STEPS // 2 - 1) as i:
                for h in range(2):
                    copy_rows(i, h)
                    copy_cols(i + 1, h)
            for h in range(2):
                copy_rows(STEPS // 2 - 1, h)

            def evacuate(c, layer):
                hold(act, "act", a_used, GT + NT * (NG * layer + c + 1))
                for o in range(2):
                    act.activation(BT[:, 0, bass.ds(c * GC + o * PIECE, PIECE)], bank[o][:, 0:PIECE], ACT.Copy).then_inc(y_out, 1)

            def deviation(n):
                hold(act, "act", var_ready, n + 1)
                act.activation(sd[:, :], mv[:, :, 1], ACT.Sqrt, bias=eps_col[:, 0:1]).then_inc(sd_ready, 1)

            def turned(c, r, dst):
                for j in range(GT):
                    hold(act, "act", tp_ready, NT * r + GT * c + j + 1)
                    act.activation(dst(j), bank[6 + j % 2][:, 0:D].rearrange("p (h n) -> p h n", h=FH), ACT.Copy).then_inc(tp_free, 1)

            def turn_x(c, r):
                turned(c, r, lambda j: xT[:, :, bass.ds(c * GC + j * P, P)])

            evacuate(0, 0)
            with act.Fori(1, NG) as c:
                evacuate(c, 0)
                deviation(ln("L0", c - 1))
            deviation(ln("L0", NG - 1))
            turn_x(0, TP["L1"])
            evacuate(0, 1)
            with act.Fori(1, NG) as c:
                turn_x(c, TP["L1"])
                evacuate(c, 1)
                deviation(ln("L1", c - 1))
            deviation(ln("L1", NG - 1))

            def take_t(c, n, b, dst):
                for f in range(FH):
                    for o in range(2):
                        hold(act, "act", t_ready, 4 * (NG * n + c) + 2 * f + o + 1)
                        ins = act.activation(dst[:, f, bass.ds(c * GC + o * PIECE, PIECE)], bank[4 + o][:, 0:PIECE], ACT.Identity,
                                             bias=cols[b][0][:, f:f + 1])
                        ins.then_inc(t_free, 1)

            def bn_deviation(n):
                act.wait_ge(bn_var, n + 1)
                act.activation(bn_sd[:, :], bn_mv[:, :, 1], ACT.Sqrt, bias=eps_col[:, 0:1]).then_inc(bn_sd_ready, 1)
                act.wait_ge(bn_ready, n + 1)

            def rectify(c):
                for f in range(FH):
                    last = act.activation(BT[:, f, bass.ds(c * GC, GC)], xT[:, f, bass.ds(c * GC, GC)], ACT.Relu,
                                          scale=bn_scale[:, f:f + 1], bias=bn_shift[:, f:f + 1])
                last.then_inc(r_ready, 1)

            turn_x(0, TP["L2"])
            with act.Fori(1, NG) as c:
                turn_x(c, TP["L2"])
                take_t(c - 1, 0, "b1", xT)
            take_t(NG - 1, 0, "b1", xT)
            bn_deviation(0)
            rectify(0)
            with act.Fori(1, NG) as c:
                rectify(c)
                take_t(c - 1, 1, "b2", xT)
            take_t(NG - 1, 1, "b2", xT)
            bn_deviation(1)
            with act.Fori(0, NG) as c:
                rectify(c)
            deviation(ln("L2", 0))
            with act.Fori(1, NG) as c:
                deviation(ln("L2", c))
                turn_x(c - 1, TP["prep"])
            turn_x(NG - 1, TP["prep"])


            def stage(l, i, h, first=False):
                if not first:
                    for u in range(HALF * h, HALF * (h + 1)):
                        hold(act, "act", gathered[u], 16 * (l * ROUNDS + i))
                act.activation(src_idx[:, HALF * h:HALF * (h + 1)], srcC[:, bass.ds(RING * i + HALF * h, HALF)],
                               ACT.Copy).then_inc(idx_ready, 1)

            for l in range(LAYERS3):
                for h in range(2):
                    stage(l, 0, h, l == 0)
                if l:
                    with act.Fori(0, NG) as c:
                        turn_x(c, TP[f"part{l}"])
                def keep(j, t):
                    hold(act, "act", z_ready, NT * Z[f"part{l}"] + t + 1)
                    act.activation(PG[:, bass.ds(t, 1), :].rearrange("p t d -> p (t d)"), bank[4 + j % 2][:, 0:D], ACT.Copy).then_inc(z_free, 1)

                with act.Fori(0, NG) as c:
                    for j in range(GT):
                        for h in range(2):
                            stage(l, c * GT + j + 1, h)
                        keep(j, c * GT + j)
                with act.Fori(NT + 1, ROUNDS) as i:
                    for h in range(2):
                        stage(l, i, h)
                with act.Fori(0, NG) as c:
                    turned(c, TP[f"post{l}"], lambda j: pT[:, j, :, :])
                    if l:
                        deviation(ln(f"post{l}", c))
                    if l == 2:
                        deviation(ln("out", c))

        @block.tensor
        def _(pe):
            pe.sem_inc(hist_done, 2)
            pe.sem_inc(rows_ready, 2)
            pe.sem_inc(a_used, GT)

            pe.wait_ge(pool_const, 2)
            pe.wait_ge(small_ready, 2)
            pe.transpose(bank[7][0:1, 0:P], col[:, 0:1], ident[:, :]).then_inc(pe_small, 1)

            def edge_step(i, h, start=False, stop=False):
                s = 2 * i + h
                hold(pe, "pe", rows_read, s + 1)
                hold(pe, "pe", cols_ready, s + 1)
                for u in range(STREAMS):
                    pe.transpose(bank[2 * h][:, u * P:(u + 1) * P], key_cols[:, h, u:u + 1].to_broadcast([P, P]), ident[:, :])
                    last = pe.transpose(bank[2 * h + 1][:, u * P:(u + 1) * P], w_cols[:, h, u:u + 1].to_broadcast([P, P]), ident[:, :])
                last.then_inc(rows_ready, 1)
                hold(pe, "pe", hot_ready, s + 1)
                for u in range(STREAMS):
                    last = pe.matmul(bank[4][:, 0:NT], hot_lo[:, h, u, :], hot_hi[:, h, u, :],
                                     start=start and u == 0, stop=stop and u == STREAMS - 1)
                last.then_inc(hist_done, 1)

            edge_step(0, 0, start=True)
            edge_step(0, 1)
            with pe.Fori(1, STEPS // 2 - 1) as i:
                edge_step(i, 0)
                edge_step(i, 1)
            edge_step(STEPS // 2 - 1, 0)
            edge_step(STEPS // 2 - 1, 1, stop=True)

            pe.wait_ge(small_ready, 3)
            pe.matmul(bank[6][:, 0:NT], upto[:, :], cnt[:, :], start=True, stop=True)
            pe.matmul(bank[6][:, NT:2 * NT], ones[:, :], cnt[:, :], start=True, stop=True)
            pe.transpose(bank[7][:, 0:P], whole_mask[:, 0:1].to_broadcast([P, P]), ident[:, :]).then_inc(pe_small, 1)

            def turn(src, c, r):
                for j in range(GT):
                    g = NT * r + GT * c + j
                    pe.wait_ge(tp_free, g if j else g + 1)
                    for f in range(FH):
                        last = pe.transpose(bank[6 + j % 2][:, f * P:(f + 1) * P], src(j, f), ident[:, :])
                    last.then_inc(tp_ready, 1)

            def tile_of(X, c):
                return lambda j, f: X[:, c * GT + j, f * P:(f + 1) * P]

            def aggregate(X, c, layer):
                pe.wait_ge(y_out, 4 * (NG * layer + c) + y_start)

                def rows_of(k, start, stop):
                    m = layer * NT + NG * c + k
                    if layer and c == 0:
                        pe.wait_ge(x_ready, NG * (layer - 1) + k + 1)
                    for j in range(GT):
                        pe.wait_ge(a_in[j], 16 * (m + 1))
                        for f in range(FH):
                            for o in range(2):
                                last = pe.matmul(bank[2 * f + o][:, 0:PIECE], X[:, GT * k + j, f * P:(f + 1) * P],
                                                 a_ring[:, j, o * PIECE:(o + 1) * PIECE],
                                                 start=start and j == 0, stop=stop and j == GT - 1)
                        last.then_inc(a_used, 1)

                for k in range(NG):
                    rows_of(k, k == 0, k == NG - 1)

            y_start = 1
            pe.sem_inc(y_out, 1)

            def product(c, r, terms, j):
                g = NT * r + GT * c + j
                pe.wait_ge(z_free, g if j else g + 1)
                for n, (lhs, rhs) in enumerate(terms):
                    last = pe.matmul(bank[4 + j % 2][:, 0:D], lhs, rhs, start=n == 0, stop=n == len(terms) - 1)
                last.then_inc(z_ready, 1)

            def nodes(B, c, j, f):
                return B[:, f, bass.ds(c * GC + j * P, P)]

            def dense0(c):
                pe.wait_ge(y_out, 4 * (NG * 0 + c) + 4 + y_start)
                for j in range(GT):
                    product(c, Z["L0"], [(nodes(BT, c, j, f), W0s[:, f, :]) for f in range(FH)], j)

            def dense1(c):
                pe.wait_ge(y_out, 4 * (NG * 1 + c) + 4 + y_start)
                pe.wait_ge(tp_free, 1 + NT * TP["L1"] + GT * c + GT)
                for j in range(GT):
                    product(c, Z["L1"], [(nodes(B, c, j, f), W1Ls[:, FH * n + f, :]) for n, B in enumerate((xT, BT)) for f in range(FH)], j)

            def block_product(c, n, w):
                for f in range(FH):
                    for o in range(2):
                        g = 4 * (NG * n + c) + 2 * f + o
                        pe.wait_ge(t_free, g + 1)
                        for k in range(FH):
                            last = pe.matmul(bank[4 + o][:, 0:PIECE], w[:, k, f * P:(f + 1) * P],
                                             BT[:, k, bass.ds(c * GC + o * PIECE, PIECE)], start=k == 0, stop=k == FH - 1)
                        last.then_inc(t_ready, 1)

            pe.wait_ge(x_in, 32)
            pe.wait_ge(weights_in, 16 * N_WEIGHT_LOADS)
            pe.wait_ge(small_ready, 4)
            aggregate(XA, 0, 0)
            for c in range(1, NG):
                aggregate(XA, c, 0)
                dense0(c - 1)
            dense0(NG - 1)

            pe.wait_ge(x_ready, 1)
            turn(tile_of(XB, 0), 0, TP["L1"])
            aggregate(XB, 0, 1)
            for c in range(1, NG):
                turn(tile_of(XB, c), c, TP["L1"])
                aggregate(XB, c, 1)
                dense1(c - 1)
            dense1(NG - 1)

            def dense2(c):
                pe.wait_ge(y_out, 4 * (NG * 2 + c) + 4 + y_start)
                block_product(c, 0, W1s)

            pe.wait_ge(x_ready, NG + 1)
            pe.wait_ge(z_free, 1 + 2 * NT)
            turn(tile_of(XA, 0), 0, TP["L2"])
            pe.wait_ge(tp_free, 1 + NT * TP["L2"] + GT)
            aggregate(XA, 0, 2)
            for c in range(1, NG):
                turn(tile_of(XA, c), c, TP["L2"])
                pe.wait_ge(tp_free, 1 + NT * TP["L2"] + GT * c + GT)
                aggregate(XA, c, 2)
                dense2(c - 1)
            dense2(NG - 1)
            for c in range(NG):
                pe.wait_ge(r_ready, c + 1)
                block_product(c, 1, W2s)
            pe.wait_ge(t_free, 2 + 8 * NG)
            for c in range(NG + 1):
                if c < NG:
                    pe.wait_ge(r_ready, NG + c + 1)
                    for j in range(GT):
                        g = GT * c + j
                        pe.wait_ge(back_free, g if j else g + 1)
                        for f in range(FH):
                            last = pe.transpose(bank[j % 2][:, f * P:(f + 1) * P], nodes(BT, c, j, f), ident[:, :])
                        last.then_inc(back_ready, 1)
                if c:
                    pe.wait_ge(x_ready, NG * XR["L2"] + c)
                    turn(tile_of(XB, c - 1), c - 1, TP["prep"])
                    pe.wait_ge(tp_free, 1 + NT * TP["prep"] + GT * c)
                    for j in range(GT):
                        product(c - 1, Z["prep"], [(nodes(xT, c - 1, j, f), Wps[:, f, :]) for f in range(FH)], j)

            for l, Wm in enumerate((Wm1s, Wm2s, Wm3s)):
                for c in range(NG):
                    if l:
                        pe.wait_ge(x_ready, NG * XR[f"post{l - 1}"] + c + 1)
                        turn(tile_of(XA, c), c, TP[f"part{l}"])
                        pe.wait_ge(tp_free, 1 + NT * TP[f"part{l}"] + GT * c + GT)
                for c in range(NG):
                    for j in range(GT):
                        product(c, Z[f"part{l}"], [(nodes(xT, c, j, f), Wm[:, f, :]) for f in range(FH)]
                                + [(row0[:, :], rows[f"bm{l + 1}"][0][:, :])], j)
                pe.wait_ge(max_done, RING + CH * (l + 1))
                for f in range(FH):
                    last = pe.transpose(bank[0][:, f * P:(f + 1) * P], s_ring[:, RING - 1, f * P:(f + 1) * P], ident[:, :])
                last.then_inc(fix_T, 1)
                pe.wait_ge(fix_scan, l + 1)
                for f in range(FH):
                    last = pe.transpose(bank[1][:, f * P:(f + 1) * P], RT[:, f, 0:P], ident[:, :])
                last.then_inc(fix_back, 1)
                pe.wait_ge(z_free, 1 + NT * (Z[f"part{l}"] + 1))

                def turn_pooled(t):
                    c, j = divmod(t, GT)
                    g = NT * TP[f"post{l}"] + t
                    pe.wait_ge(pooled[j], 16 * (NG * l + c + 1))
                    pe.wait_ge(tp_free, g if j else g + 1)
                    for f in range(FH):
                        last = pe.transpose(bank[6 + j % 2][:, f * P:(f + 1) * P], p_ring[:, j, f * P:(f + 1) * P], ident[:, :])
                    last.then_inc(tp_ready, 1)

                turn_pooled(0)
                for t in range(NT):
                    if t + 1 < NT:
                        turn_pooled(t + 1)
                    c, j = divmod(t, GT)
                    pe.wait_ge(tp_free, NT * TP[f"post{l}"] + t + 2)
                    product(c, Z[f"post{l}"], [(pT[:, j, f, :], Wm[:, FH + f, :]) for f in range(FH)], j)


def kernel(**inputs):
    import concourse.bacc as _bacc
    from concourse.bass_utils import run_bass_kernel_spmd as _run

    def arr(name):
        return np.asarray(inputs[name])

    def padded(a, fill, n=EP):
        return np.concatenate([a, np.full(n - a.shape[0], fill, a.dtype)])

    def in_steps(a):
        return np.ascontiguousarray(a.reshape(STREAMS, STEPS, P).transpose(2, 1, 0).reshape(P, CH))

    src, w = padded(arr("src"), 0), padded(arr("edge_weight"), 0)
    dst = padded(arr("dst"), PAD_DST)
    given = {
        "src_steps": in_steps(src), "dst_steps": in_steps(dst), "w_steps": in_steps(w),
        "src_chunks": src.reshape(P, CH), "dst_flat": padded(dst, END_DST, EP + FAR),
        "x": arr("x"), "W0": arr("L0_gnn_weight"), "b0": arr("L0_gnn_bias"), "W1L": arr("L1_gnn_W"), "b1L": arr("L1_gnn_b"),
        "eps": arr("L2_gnn_eps"), "W1": arr("L2_gnn_W1"), "b1": arr("L2_gnn_b1"), "g1": arr("L2_gnn_g1"), "be1": arr("L2_gnn_be1"),
        "W2": arr("L2_gnn_W2"), "b2": arr("L2_gnn_b2"), "g2": arr("L2_gnn_g2"), "be2": arr("L2_gnn_be2"),
        "Wp": arr("L3_gnn_Wp1").T, "bp": arr("L3_gnn_bp1"), "Wm1": arr("L3_gnn_Wm1").T, "bm1": arr("L3_gnn_bm1"),
        "Wm2": arr("L3_gnn_Wm2").T, "bm2": arr("L3_gnn_bm2"), "Wm3": arr("L3_gnn_Wm3").T, "bm3": arr("L3_gnn_bm3"),
        "lg2": arr("L3_gnn_ln2_g"), "lb2": arr("L3_gnn_ln2_b"), "lg3": arr("L3_gnn_ln3_g"), "lb3": arr("L3_gnn_ln3_b"),
    }
    nc = _bacc.Bacc("TRN2", target_bir_lowering=False, num_devices=1)
    arrays, args = {}, []
    for name, a in given.items():
        a = np.ascontiguousarray(a)
        arrays[f"in_{name}"] = a
        args.append(nc.dram_tensor(f"in_{name}", a.shape, mybir.dt.from_np(a.dtype), kind="ExternalInput").ap())
    args.append(nc.dram_tensor("out_0", (N, D), F32, kind="ExternalOutput").ap())
    build(nc, *args)
    r = _run(nc, [arrays], core_ids=[0])
    return r.results[0]["out_0"]
```

```python
from contextlib import ExitStack

import numpy as np

import concourse.bass as bass
from concourse import mybir

P = 128
ALU = mybir.AluOpType
ACT = mybir.ActivationFunctionType
AX = mybir.AxisListType
F32 = mybir.dt.float32
BF16 = mybir.dt.bfloat16
I32 = mybir.dt.int32
F32R = mybir.dt.float32r

N, E, D = 3125, 50000, 256
FH = D // P
NT = -(-N // P)
NP = NT * P
GT = 5
NG = NT // GT
GC = GT * P
PIECE = GC // 2
STREAMS = 4
BLOCKS, RUN = 7, 14
STEPS = BLOCKS * RUN
CH = STREAMS * STEPS
EP = CH * P
FAR = (RUN - 2) * P
PAD_DST = N
END_DST = N + 1
JUNK = NP * NP
A_ROWS = NP + 1
ZERO_ROW = EP
BIG = float(np.finfo(np.float32).max)
EPS = 1e-5
RING = 8
HALF = RING // 2
ROUNDS = CH // RING
LAYERS3 = 3


def build(nc, src_steps, dst_steps, w_steps, src_chunks, dst_flat, x, W0, b0, W1L, b1L, eps, W1, b1, g1, be1,
          W2, b2, g2, be2, Wp, bp, Wm1, bm1, Wm2, bm2, Wm3, bm3, lg2, lb2, lg3, lb3, out):
    A = nc.dram_tensor("adjacency", (A_ROWS * NP, 1), F32, kind="Internal").ap()
    A_rows = A.rearrange("(r c) o -> r (c o)", c=NP)
    H = [nc.dram_tensor(f"pool_in_{l}", (NP, D), F32, kind="Internal").ap() for l in range(LAYERS3)]
    S = [nc.dram_tensor(f"running_max_{l}", (EP + P, D), F32, kind="Internal").ap() for l in range(LAYERS3)]

    with ExitStack() as ctx:
        place = {}

        def sb(name, shape, dt=F32):
            place[name] = -(-nc.sbuf_base // 32) * 32
            return ctx.enter_context(nc.sbuf_tensor(name, shape, dt))

        def sem(name):
            return ctx.enter_context(nc.semaphore(name))

        def one_pass(name, like, shape):
            return nc.alloc_sbuf_tensor_at(name, shape, F32R, offset=place[like])

        XA, XB = sb("XA", [P, NT, D]), sb("XB", [P, NT, D])
        xT, AT = sb("xT", [P, FH, NP]), sb("AT", [P, FH, NP])

        def by_node(buf):
            return buf[:, :, :].rearrange("p h n -> p (h n)").rearrange("p (t d) -> p t d", d=D)

        HT = XA[:, :, :].rearrange("p t d -> p (t d)").rearrange("p (h n) -> p h n", n=NP)
        XC = AT[:, :, :].rearrange("p h (t n) -> p t h n", n=P)
        XD, PG = by_node(AT), XA
        X_LO = [one_pass(f"x_lo{n}", buf, [P, NT, D]) for n, buf in enumerate(("xT", "XA", "XB"))]
        a_ring = sb("a_ring", [P, GT, GC])
        rings = sb("rings", [P, 2 * RING, D])
        g_ring, s_ring = rings[:, 0:RING, :], rings[:, RING:2 * RING, :]
        hi_ring = one_pass("hi_ring", "rings", [P, GT, GC])
        lo_ring = one_pass("lo_ring", "a_ring", [P, GT, GC])
        p_ring = a_ring[:, 0:2, :].rearrange("p a n -> p (a n)").rearrange("p (t d) -> p t d", d=D)
        pT = a_ring[:, 2:4, :].rearrange("p a n -> p (a n)").rearrange("p (t h n) -> p t h n", h=FH, n=P)
        tmp = sb("tmp", [P, GT, D])
        tmpf = tmp[:, :, :].rearrange("p t d -> p (t d)")

        srcS, dstS, wS = sb("srcS", [P, CH], I32), sb("dstS", [P, CH], I32), sb("wS", [P, CH])
        key, junk = sb("key", [P, CH]), sb("junk", [P, CH])
        node_lo, node_hi = sb("node_lo", [P, CH]), sb("node_hi", [P, CH])
        srcC, dstC = sb("srcC", [P, CH], I32), sb("dstC", [P, CH], I32)
        x_hi_ring = one_pass("x_hi_ring", "srcS", [P, GT, D])
        tmp_b = nc.alloc_sbuf_tensor_at("tmp_b", [P, GT, D], F32, offset=place["srcS"] + 4 * GT * D)
        assert 7 * CH >= 2 * GT * D
        dst_next, dst_far = sb("dst_next", [P, CH], I32), sb("dst_far", [P, CH], I32)
        seg = sb("seg", [P, CH])
        eq = sb("eq", [P, CH])
        last_before = sb("last_before", [P, 1], I32)
        carry_mask = sb("carry_mask", [P, 1])
        whole_mask = sb("whole_mask", [P, 1])
        whole_row = sb("whole_row", [P, P])
        col = sb("col", [P, 16])
        fix_row = sb("fix_row", [P, 1], I32)
        end_row = sb("end_row", [P, NT], I32)
        cnt, incl, ends = sb("cnt", [P, NT]), sb("incl", [P, NT]), sb("ends", [P, NT])
        reach, reach_all = sb("reach", [P, BLOCKS + 1]), sb("reach_all", [P, BLOCKS + 1])
        reach_i = sb("reach_i", [1, BLOCKS + 1], I32)

        ident, ones = sb("ident", [P, P]), sb("ones", [P, P])
        before = sb("before", [P, P])
        upto = sb("upto", [P, P])
        row0 = sb("row0", [P, P])
        iota_i = sb("iota_i", [P, P], I32)
        iota_f = sb("iota_f", [P, P])
        key_cols, w_cols = sb("key_cols", [P, 2, STREAMS]), sb("w_cols", [P, 2, STREAMS])
        w_rows = sb("w_rows", [P, 2, STREAMS, P])
        unused = sb("unused", [P, 2 * STREAMS, P], BF16)
        hot_lo = sb("hot_lo", [P, 2, STREAMS, P], BF16)
        hot_hi = sb("hot_hi", [P, 2, STREAMS, NT], BF16)
        w_out = sb("w_out", [P, 2, STREAMS])
        repeats = sb("repeats", [P, 2, STREAMS])
        moved = sb("moved", [P, 2, STREAMS])
        idx_out = sb("idx_out", [P, 2, STREAMS], I32)
        src_idx = sb("src_idx", [P, RING], I32)

        stats = sb("stats", [P, GT, 6])
        mv = sb("mv", [P, GT, 2])
        sd, rstd = sb("sd", [P, GT]), sb("rstd", [P, GT])
        bn_stat = sb("bn_stat", [P, FH, 2 * NG, 6])
        bn_mv = sb("bn_mv", [P, FH, 2])
        bn_sd, bn_scale, bn_shift, bn_ms = (sb(n, [P, FH]) for n in ("bn_sd", "bn_scale", "bn_shift", "bn_ms"))
        eps_col = sb("eps_col", [P, 1])
        eps1 = sb("eps1", [P, 1])
        out_scale, out_shift = sb("out_scale", [P, GT]), sb("out_shift", [P, GT])

        RT = sb("RT", [P, FH, P + 1])
        fix_old, fix_new = sb("fix_old", [P, D]), sb("fix_new", [P, D])

        def weight(name, w):
            return sb(name, [P, w.shape[0] // P, D]), w.rearrange("(h p) n -> p h n", p=P)

        W0s, W1Ls, W1s, W2s, Wps, Wm1s, Wm2s, Wm3s = weights = [
            weight(n, w) for n, w in (("W0s", W0), ("W1Ls", W1L), ("W1s", W1), ("W2s", W2), ("Wps", Wp),
                                      ("Wm1s", Wm1), ("Wm2s", Wm2), ("Wm3s", Wm3))]
        W0s, W1Ls, W1s, W2s, Wps, Wm1s, Wm2s, Wm3s = (w[0] for w in weights)
        rows = {}
        for name, v in (("b0", b0), ("b1L", b1L), ("bp", bp), ("bm1", bm1), ("bm2", bm2), ("bm3", bm3),
                        ("lg2", lg2), ("lb2", lb2), ("lg3", lg3), ("lb3", lb3)):
            rows[name] = (sb(f"row_{name}", [P, D]), v)
        cols = {}
        for name, v in (("b1", b1), ("g1", g1), ("be1", be1), ("b2", b2), ("g2", g2), ("be2", be2)):
            cols[name] = (sb(f"col_{name}", [P, FH]), v)

        bank = [ctx.enter_context(nc.psum_tensor(f"bank{i}", [P, 512], F32)) for i in range(8)]

        def row_group(name):
            return rows[name][0][:, :].unsqueeze(1).to_broadcast([P, GT, D])

        edges_in = sem("edges_in")
        x_in, x_zero = sem("x_in"), sem("x_zero")
        weights_in = sem("weights_in")
        eps_in = sem("eps_in")
        zeros_ready, tiles_zero = sem("zeros_ready"), sem("tiles_zero")
        a_zeroed = [sem(f"a_zeroed{c}") for c in range(NG)]
        zero_row_in = sem("zero_row_in")
        pool_const = sem("pool_const")
        dve = sem("dve")
        cols_ready, rows_ready, w_rows_ready, rows_read = (
            sem(n) for n in ("cols_ready", "rows_ready", "w_rows_ready", "rows_read"))
        hot_ready, hist_done = sem("hot_ready"), sem("hist_done")
        merged, scatter_ready = sem("merged"), sem("scatter_ready")
        scattered = [sem(f"scattered{q}") for q in range(STREAMS)]
        pe_small = sem("pe_small")
        small_ready = sem("small_ready")
        hi_ready, split_ready, lo_ready = sem("hi_ready"), sem("split_ready"), sem("lo_ready")
        reach_ready, flag_ready = sem("reach_ready"), sem("flag_ready")
        a_in = [sem(f"a_in{j}") for j in range(GT)]
        a_used = sem("a_used")
        y_out = sem("y_out")
        t_ready, t_free = sem("t_ready"), sem("t_free")
        z_ready, z_free = sem("z_ready"), sem("z_free")
        tp_ready, tp_free, tp_copied = sem("tp_ready"), sem("tp_free"), sem("tp_copied")
        back_ready, back_free = sem("back_ready"), sem("back_free")
        x_ready = sem("x_ready")
        var_ready, sd_ready = sem("var_ready"), sem("sd_ready")
        bn_var, bn_sd_ready, bn_ready = sem("bn_var"), sem("bn_sd_ready"), sem("bn_ready")
        r_ready = sem("r_ready")
        h_ready, h_stored = sem("h_ready"), sem("h_stored")
        idx_ready = sem("idx_ready")
        gathered = [sem(f"gathered{u}") for u in range(RING)]
        max_done = sem("max_done")
        max_stored = [sem("max_stored0"), sem("max_stored1")]
        fix_read, fix_T, fix_scan, fix_back, fix_ready, fix_written = (
            sem(n) for n in ("fix_read", "fix_T", "fix_scan", "fix_back", "fix_ready", "fix_written"))
        pooled = [sem(f"pooled{j}") for j in range(GT)]
        out_ready, out_stored = sem("out_ready"), sem("out_stored")
        out_scale_ready = sem("out_scale_ready")
        tick = {n: sem(f"tick_{n}") for n in ("sp", "act", "pe", "dve", "pool")}

        def hold(eng, name, s, value):
            eng.wait_ge(s, value)
            eng.sem_inc(tick[name], 1)

        N_EDGE_LOADS = 8
        EARLY, LATE = range(3), range(3, GT)
        AHEAD = GT
        N_WEIGHT_LOADS = len(weights) + len(rows) + len(cols)
        Z = {"L0": 0, "L1": 1, "prep": 2, "part0": 3, "post0": 4, "part1": 5, "post1": 6, "part2": 7, "post2": 8}
        TP = {"L1": 0, "L2": 1, "prep": 2, "post0": 3, "part1": 4, "post1": 5, "part2": 6, "post2": 7}
        def z_bank(stage, j):
            return bank[2 + j % 4] if stage.startswith("post") else bank[4 + j % 2]

        def z_out(stage, c, j):
            g = NT * Z[stage] + GT * c + j
            if stage.startswith("post"):
                return g + (1, -3, -3, -3, -2)[j]
            return g + (0 if j else 1)

        XR = {"L0": 0, "L1": 1, "L2": 2, "post0": 3, "post1": 4}
        LN = {"L0": 0, "L1": 1, "L2": 2, "post1": 3, "post2": 4}

        def ln(stage, c):
            if stage == "out":
                return LN["post2"] * NG + 2 * c + 1
            return LN[stage] * NG + c * (2 if stage == "post2" else 1)

        block = ctx.enter_context(nc.Block())

        @block.sync
        def _(sp):
            flat = dst_flat.rearrange("(a e) -> a e", a=1)

            def stretch(shift):
                return dst_flat[shift:shift + EP].rearrange("(p t) -> p t", p=P)

            sp.dma_start(srcS[:, :], src_steps).then_inc(edges_in, 16)
            sp.dma_start(dstS[:, :], dst_steps).then_inc(edges_in, 16)
            sp.dma_start(wS[:, :], w_steps).then_inc(edges_in, 16)
            sp.dma_start(srcC[:, :], src_chunks).then_inc(edges_in, 16)
            sp.dma_start(dstC[:, :], stretch(0)).then_inc(edges_in, 16)
            sp.dma_start(dst_next[:, :], stretch(1)).then_inc(edges_in, 16)
            sp.dma_start(dst_far[:, :], stretch(FAR)).then_inc(edges_in, 16)
            sp.wait_ge(x_zero, 1)
            sp.dma_start(last_before[1:P, :], stretch(0)[0:P - 1, CH - 1:CH], allow_slow_non_contiguous=True).then_inc(edges_in, 16)
            full = N // P
            sp.dma_start(XA[:, 0:full, :], x[0:full * P, :].rearrange("(t p) d -> p t d", p=P)).then_inc(x_in, 16)
            sp.dma_start(XA[0:N - full * P, full, :], x[full * P:N, :]).then_inc(x_in, 16)
            sp.dma_start(eps1[:, :], eps.rearrange("(a b) -> a b", a=1).to_broadcast([P, 1])).then_inc(eps_in, 16)
            sp.wait_ge(zeros_ready, 1)
            sp.dma_start(A_rows[NP:NP + 1, :].rearrange("o (p c) -> (o p) c", p=P), AT[:, 0, 0:NT]).then_inc(a_zeroed[0], 16)
            for t in range(NT):
                if t == AHEAD:
                    for c in range(AHEAD // GT):
                        sp.wait_ge(a_zeroed[c], 16 * (GT + (c == 0)))
                    sp.sem_inc(tiles_zero, AHEAD)
                if t > AHEAD:
                    sp.wait_ge(a_zeroed[(t - 1) // GT], 16 * ((t - 1) % GT + 1))
                    sp.sem_inc(tiles_zero, 1)
                sp.dma_start(A_rows[t * P:(t + 1) * P, :], AT[:, 0, :]).then_inc(a_zeroed[t // GT], 16)
            for l in range(LAYERS3):
                sp.dma_start(S[l][ZERO_ROW:ZERO_ROW + P, :], AT[:, 0, 0:D]).then_inc(zero_row_in, 16)
            sp.wait_ge(a_zeroed[NG - 1], 16 * GT)
            sp.sem_inc(tiles_zero, 1)
            for tile, view in weights:
                sp.dma_start(tile[:, :, :], view).then_inc(weights_in, 16)
            for tile, v in rows.values():
                sp.dma_start(tile[:, :], v.rearrange("(a n) -> a n", a=1).to_broadcast([P, D])).then_inc(weights_in, 16)
            for tile, v in cols.values():
                sp.dma_start(tile[:, :], v.rearrange("(h p) -> p h", p=P), allow_slow_non_contiguous=True).then_inc(weights_in, 16)

            for q in range(STREAMS):
                sp.wait_ge(scattered[q], 16 * STEPS)
            sp.wait_ge(zero_row_in, 16 * LAYERS3)
            for layer in range(3):
                with sp.Fori(0, NG) as c:
                    with sp.Fori(0, NG) as k:
                        m = layer * NT + NG * c + k
                        for j in range(GT):
                            hold(sp, "sp", a_used, m * GT + j + 1)
                            sp.dma_start(a_ring[:, j, :], A_rows[bass.ds((k * GT + j) * P, P), bass.ds(c * GC, GC)]).then_inc(a_in[j], 16)

            def store_rows(l):
                for c in range(NG):
                    if l:
                        sp.wait_ge(x_ready, NG * XR[f"post{l - 1}"] + c + 1)
                    else:
                        sp.wait_ge(h_ready, c + 1)
                    to = H[l][c * GC:(c + 1) * GC, :]
                    if l:
                        sp.dma_start(to.rearrange("(t p) d -> p t d", p=P), XD[:, c * GT:(c + 1) * GT, :]).then_inc(h_stored, 16)
                    else:
                        for f in range(FH):
                            sp.dma_start(to[:, f * P:(f + 1) * P].rearrange("(t p) n -> p t n", p=P),
                                         XC[:, c * GT:(c + 1) * GT, f, :]).then_inc(h_stored, 16)

            for l in range(LAYERS3):
                store_rows(l)
                running = S[l][0:EP, :].rearrange("(p t) d -> p (t d)", p=P)
                with sp.Fori(0, ROUNDS) as i:
                    for h in range(2):
                        hold(sp, "sp", max_done, RING + l * CH + RING * i + HALF * (h + 1))
                        sp.dma_start(running[:, bass.ds((RING * i + HALF * h) * D, HALF * D)],
                                     s_ring[:, HALF * h:HALF * (h + 1), :].rearrange("p t d -> p (t d)")).then_inc(max_stored[h], 16)
            for c in range(NG):
                sp.wait_ge(out_ready, c + 2)
                for j in range(GT):
                    t = c * GT + j
                    n = min(P, N - t * P)
                    sp.dma_start(out[t * P:t * P + n, :], XD[0:n, t, :]).then_inc(out_stored, 16)
            sp.wait_ge(out_stored, 16 * NT)

        @block.gpsimd
        def _(pool):
            pool.memset(AT[:, 0, :], 0.0).then_inc(zeros_ready, 1)
            pool.memset(last_before[:, :], -1)
            pool.memset(XA[:, NT - 1, :], 0.0).then_inc(x_zero, 1)
            pool.memset(ones[:, :], 1.0)
            pool.memset(eps_col[:, :], EPS)
            pool.memset(RT[:, :, :], -BIG).then_inc(pool_const, 1)
            pool.wait_ge(pool_const, 1)
            pool.affine_select(out=ident[:, :], in_=ones[:, :], compare_op=ALU.is_equal, fill=0.0, base=0,
                               pattern=[[-1, P]], channel_multiplier=1)
            pool.affine_select(out=before[:, :], in_=ones[:, :], compare_op=ALU.is_gt, fill=0.0, base=0,
                               pattern=[[-1, P]], channel_multiplier=1)
            pool.affine_select(out=upto[:, :], in_=ones[:, :], compare_op=ALU.is_ge, fill=0.0, base=0,
                               pattern=[[1, P]], channel_multiplier=-1)
            pool.affine_select(out=row0[:, :], in_=ones[:, :], compare_op=ALU.is_equal, fill=0.0, base=0,
                               pattern=[[0, P]], channel_multiplier=1)
            pool.iota(iota_i[:, :], pattern=[[1, P]], base=0, channel_multiplier=0).then_inc(pool_const, 1)
            pool.wait_ge(small_ready, 1)
            pool.iota(srcS[:, :].rearrange("p (s q) -> p s q", q=STREAMS), pattern=[[0, STEPS], [P, STREAMS]],
                      base=JUNK, channel_multiplier=1)
            pool.iota(fix_row[:, :], pattern=[[0, 1]], base=-1, channel_multiplier=CH).then_inc(pool_const, 1)

            pool.wait_ge(small_ready, 2)
            pool.partition_all_reduce(reach_all[:, :], reach[:, :], P, bass.bass_isa.ReduceOp.max).then_inc(reach_ready, 1)

            pool.wait_ge(flag_ready, 1)
            serial = pool.value_load(reach_i[0:1, BLOCKS:BLOCKS + 1], min_val=0, max_val=1)

            def scatter(q, h):
                pool.indirect_dma_start(out=A, out_offset=bass.IndirectOffsetOnAxis(ap=idx_out[:, h, q:q + 1], axis=0),
                                        in_=w_out[:, h, q:q + 1], in_offset=None,
                                        compute_op=ALU.add).then_inc(scattered[q], 16)

            def scatter_serially():
                pool.wait_ge(tiles_zero, NT)
                for s in range(2):
                    pool.wait_ge(scatter_ready, s + 1)
                    for q in range(STREAMS):
                        if s or q:
                            pool.wait_ge(scattered[(q - 1) % STREAMS], 16 * (s + 1 if q else s))
                        scatter(q, s)
                with pool.Fori(1, STEPS // 2) as i:
                    for h in range(2):
                        s = 2 * i + h
                        hold(pool, "pool", scatter_ready, s + 1)
                        for q in range(STREAMS):
                            hold(pool, "pool", scattered[(q - 1) % STREAMS], 16 * (s + 1 if q else s))
                            scatter(q, h)

            def scatter_pair(i, first=False):
                for h in range(2):
                    s = 2 * i + h
                    hold(pool, "pool", scatter_ready, s + 1)
                    for q in [*range(1, STREAMS), 0]:
                        if not first or h:
                            hold(pool, "pool", scattered[q], 16 * s)
                        scatter(q, h)

            def zeroed(b):
                need = pool.value_load(reach_i[0:1, bass.ds(b, 1)], min_val=1, max_val=NT)
                hold(pool, "pool", tiles_zero, need)

            with pool.If(serial):
                scatter_serially()
            with pool.Else():
                zeroed(0)
                scatter_pair(0, True)
                with pool.Fori(1, RUN // 2) as i:
                    scatter_pair(i)
                with pool.Fori(1, BLOCKS) as b:
                    zeroed(b)
                    with pool.Fori(0, RUN // 2) as i:
                        scatter_pair(b * (RUN // 2) + i)

            for l in range(LAYERS3):
                pool.wait_ge(h_stored, 16 * NG * (l + FH))

                with pool.Fori(0, ROUNDS) as i:
                    for u in range(RING):
                        if u % HALF == 0:
                            hold(pool, "pool", idx_ready, l * 2 * ROUNDS + 2 * i + u // HALF + 1)
                        hold(pool, "pool", max_done, l * CH + RING * i + u + 1)
                        pool.indirect_dma_start(out=g_ring[:, u, :], out_offset=None, in_=H[l],
                                                in_offset=bass.IndirectOffsetOnAxis(ap=src_idx[:, u:u + 1], axis=0)
                                                ).then_inc(gathered[u], 16)

                for h in range(2):
                    pool.wait_ge(max_stored[h], 16 * ROUNDS * (l + 1))
                pool.indirect_dma_start(out=fix_old[:, :], out_offset=None, in_=S[l],
                                        in_offset=bass.IndirectOffsetOnAxis(ap=fix_row[:, 0:1], axis=0)).then_inc(fix_read, 16)
                pool.wait_ge(fix_ready, l + 1)
                pool.indirect_dma_start(out=S[l], out_offset=bass.IndirectOffsetOnAxis(ap=fix_row[:, 0:1], axis=0),
                                        in_=fix_new[:, :], in_offset=None).then_inc(fix_written, 16)
                pool.wait_ge(fix_written, 16 * (l + 1))
                if l == 0:
                    pool.wait_ge(zero_row_in, 16 * LAYERS3)
                for t in range(NT):
                    if l or t >= GT:
                        pool.wait_ge(tp_ready, TP[f"post{l}"] * NT + t - GT + 1)
                    pool.indirect_dma_start(out=p_ring[:, t % GT, :], out_offset=None, in_=S[l],
                                            in_offset=bass.IndirectOffsetOnAxis(ap=end_row[:, t:t + 1], axis=0)
                                            ).then_inc(pooled[t % GT], 16)

        @block.vector
        def _(v):
            chain = [0]

            def link(ins):
                chain[0] += 1
                ins.then_inc(dve, 1)
                v.wait_ge(dve, chain[0])

            v.sem_inc(rows_read, 2)
            v.sem_inc(z_free, 1)
            v.sem_inc(max_done, RING)
            v.sem_inc(back_free, 1)

            v.wait_ge(edges_in, 16 * N_EDGE_LOADS)
            v.tensor_copy(junk[:, :], srcS[:, :])
            link(v.tensor_copy(eq[:, :], dstS[:, :]))
            v.tensor_scalar(node_lo[:, :].bitcast(I32), dstS[:, :], P - 1, None, ALU.bitwise_and)
            v.tensor_scalar(node_hi[:, :].bitcast(I32), dstS[:, :], 7, None, ALU.logical_shift_right)
            link(v.scalar_tensor_tensor(out=key[:, :], in0=eq[:, :], scalar=float(NP), in1=junk[:, :], op0=ALU.mult, op1=ALU.add))
            v.tensor_copy(node_lo[:, :], node_lo[:, :].bitcast(I32))
            v.tensor_copy(node_hi[:, :], node_hi[:, :].bitcast(I32)).then_inc(small_ready, 1)
            v.wait_ge(pool_const, 3)
            v.tensor_copy(iota_f[:, :], iota_i[:, :])
            link(v.tensor_copy(junk[:, :], srcS[:, :]))
            link(v.tensor_tensor(junk[:, :], junk[:, :], key[:, :], ALU.subtract))
            v.tensor_tensor(eq[:, :], dstC[:, :], dst_next[:, :], ALU.is_gt)
            link(v.tensor_tensor(seg[:, :], dstC[:, :], dst_far[:, :], ALU.is_ge))
            link(v.tensor_tensor(eq[:, :], eq[:, :], seg[:, :], ALU.max))
            v.tensor_reduce(reach[:, 0:BLOCKS], node_hi[:, :].rearrange("p (b e) -> p b e", b=BLOCKS), AX.X, ALU.max)
            v.tensor_reduce(reach[:, BLOCKS:BLOCKS + 1], eq[:, :], AX.X, ALU.max).then_inc(small_ready, 1)
            v.wait_ge(reach_ready, 1)
            link(v.tensor_scalar(reach[0:1, 0:BLOCKS], reach_all[0:1, 0:BLOCKS], 1.0, 1.0, ALU.mult, ALU.add))
            v.tensor_copy(reach_i[:, 0:BLOCKS], reach[0:1, 0:BLOCKS])
            v.tensor_copy(reach_i[:, BLOCKS:BLOCKS + 1], reach_all[0:1, BLOCKS:BLOCKS + 1]).then_inc(flag_ready, 1)

            def merge(i, h, first=False):
                s = 2 * i + h
                if first:
                    v.wait_ge(hist_done, s + 1)
                else:
                    hold(v, "dve", hist_done, s + 1)
                at = STREAMS * s
                for u in range(STREAMS):
                    v.tensor_scalar(hot_lo[:, h, u, :], iota_f[:, :], node_lo[:, bass.ds(at + u, 1)], None, ALU.is_equal)
                v.tensor_tensor(hot_hi[:, h, :, :], node_hi[:, bass.ds(at, STREAMS)].unsqueeze(2).to_broadcast([P, STREAMS, NT]),
                                iota_f[:, 0:NT].unsqueeze(1).to_broadcast([P, STREAMS, NT]), ALU.is_equal).then_inc(hot_ready, 1)
                hold(v, "dve", rows_ready, s + 3)
                hold(v, "dve", w_rows_ready, s + 1)
                if not first:
                    for q in range(STREAMS):
                        hold(v, "dve", scattered[q], 16 * (s - 1))
                for u in range(STREAMS):
                    v.scalar_tensor_tensor(out=unused[:, 2 * u, :], in0=bank[2 * h][:, u * P:(u + 1) * P], scalar=key[:, bass.ds(at + u, 1)],
                                           in1=w_rows[:, h, u, :], op0=ALU.is_equal, op1=ALU.mult,
                                           accum_out=w_out[:, h, u:u + 1])
                    last = v.scalar_tensor_tensor(out=unused[:, 2 * u + 1, :], in0=bank[2 * h][:, u * P:(u + 1) * P],
                                                  scalar=key[:, bass.ds(at + u, 1)], in1=before[:, :],
                                                  op0=ALU.is_equal, op1=ALU.mult, accum_out=repeats[:, h, u:u + 1])
                last.then_inc(rows_read, 1)
                hold(v, "dve", rows_read, s + 3)
                v.scalar_tensor_tensor(out=moved[:, h, :], in0=repeats[:, h, :], scalar=1.0, in1=junk[:, bass.ds(at, STREAMS)],
                                       op0=ALU.min, op1=ALU.mult).then_inc(merged, 1)
                hold(v, "dve", merged, s + 1)
                v.tensor_tensor(idx_out[:, h, :], moved[:, h, :], key[:, bass.ds(at, STREAMS)], ALU.add).then_inc(scatter_ready, 1)

            merge(0, 0, True)
            merge(0, 1, True)
            def low_part(ch, c, layer):
                lo = X_LO[layer][:, bass.ds(c * GT, GT), :]
                if layer == 2:
                    x_rows = XC[:, bass.ds(c * GT, GT), :, :]
                    lo = lo.rearrange("p t (h n) -> p t h n", h=FH)
                else:
                    x_rows = (XA, XB)[layer][:, bass.ds(c * GT, GT), :]
                ch.link(v.tensor_copy(lo, x_rows))
                v.tensor_tensor(lo, x_rows, lo.bitcast(F32), ALU.subtract).then_inc(lo_ready, 1)

            class straight:
                def link(self, ins):
                    link(ins)

            v.wait_ge(x_in, 32)
            for c in range(NG):
                low_part(straight(), c, 0)
            with v.Fori(1, STEPS // 2) as i:
                merge(i, 0)
                merge(i, 1)

            link(v.tensor_copy(eq[:, :], dstC[:, :]))
            v.memset(seg[:, 0:1], 0.0)
            v.tensor_tensor(seg[:, 1:CH], eq[:, 1:CH], eq[:, 0:CH - 1], ALU.is_equal)
            v.tensor_copy(col[:, 1:2], last_before[:, :])
            link(v.tensor_copy(col[:, 2:3], fix_row[:, :]))
            v.tensor_tensor(carry_mask[:, :], eq[:, 0:1], col[:, 1:2], ALU.is_equal)
            v.tensor_tensor(whole_mask[:, :], eq[:, CH - 1:CH], col[:, 1:2], ALU.is_equal)
            link(v.tensor_scalar(node_lo[:, :], eq[:, :], eq[:, 0:1], None, ALU.is_equal))
            for m in (seg, carry_mask, whole_mask):
                last = v.tensor_scalar(m[:, :], m[:, :], 2.0, -1.0, ALU.mult, ALU.add)
            v.tensor_reduce(col[:, 3:4], node_lo[:, :], AX.X, ALU.add)
            v.wait_ge(hist_done, 2 + STEPS)
            link(v.tensor_copy(cnt[:, :], bank[4][:, 0:NT]))
            for m in (seg, carry_mask):
                v.tensor_scalar(m[:, :], m[:, :], BIG, None, ALU.mult)
            v.tensor_scalar(whole_mask[:, :], whole_mask[:, :], BIG, None, ALU.mult)
            v.tensor_tensor(fix_row[:, :], col[:, 2:3], col[:, 3:4], ALU.add).then_inc(small_ready, 1)
            v.wait_ge(pe_small, 1)
            v.tensor_copy(whole_row[:, :], bank[7][:, 0:P])
            link(v.tensor_copy(ends[:, :], bank[6][:, NT:2 * NT]))
            link(v.tensor_tensor_scan(incl[:, :], ones[:, 0:NT], ends[:, :], 0.0, ALU.mult, ALU.add))
            link(v.tensor_tensor(incl[:, :], incl[:, :], ends[:, :], ALU.subtract))
            link(v.tensor_tensor(incl[:, :], incl[:, :], bank[6][:, 0:NT], ALU.add))
            link(v.tensor_scalar(incl[:, :], incl[:, :], -1.0, None, ALU.add))
            v.tensor_scalar(ends[:, :], incl[:, :], -1.0, float(ZERO_ROW), ALU.mult, ALU.add)
            link(v.tensor_scalar(cnt[:, :], cnt[:, :], 0.0, None, ALU.is_equal))
            link(v.tensor_tensor(ends[:, :], ends[:, :], cnt[:, :], ALU.mult))
            link(v.tensor_tensor(end_row[:, :], ends[:, :], incl[:, :], ALU.add))
            v.wait_ge(eps_in, 16)
            v.tensor_scalar(eps1[:, :], eps1[:, :], 1.0, None, ALU.add).then_inc(small_ready, 1)

            class trip:
                def __init__(self, i, start, per):
                    self.value, self.n, self.per = start + i * per, 0, per

                def link(self, ins):
                    self.n += 1
                    ins.then_inc(dve, 1)
                    hold(v, "dve", dve, self.value + self.n)

            def evacuate(c, layer):
                hold(v, "dve", a_used, GT + NT * (NG * layer + c + 1))
                for f in (range(FH) if layer == 2 else (1,)):
                    for o in range(2):
                        at = c * GC + o * PIECE
                        y = bank[2 * f + o][:, 0:PIECE]
                        if layer == 2:
                            v.scalar_tensor_tensor(out=HT[:, f, bass.ds(at, PIECE)], in0=xT[:, f, bass.ds(at, PIECE)],
                                                   scalar=eps1[:, 0:1], in1=y, op0=ALU.mult, op1=ALU.add).then_inc(y_out, 1)
                        else:
                            v.tensor_copy(AT[:, f, bass.ds(at, PIECE)], y).then_inc(y_out, 1)

            def split(layer, c, k, js=range(GT)):
                for j in js:
                    hold(v, "dve", hi_ready, (layer * NT + NG * c + k) * GT + j + 1)
                    v.tensor_tensor(lo_ring[:, j, :], a_ring[:, j, :], hi_ring[:, j, :].bitcast(F32), ALU.subtract).then_inc(split_ready, 1)

            def statistics(ch, src):
                for j in range(GT):
                    last = v.bn_stats(stats[:, j, :], src(j))
                ch.link(last)

            def reciprocals(ch, n):
                for j in range(GT):
                    last = v.bn_aggr(mv[:, j, :], stats[:, j, :])
                last.then_inc(var_ready, 1)
                hold(v, "dve", sd_ready, n + 1)
                ch.link(v.reciprocal(rstd[:, :], sd[:, :]))

            def deviations(ch, n, src):
                statistics(ch, src)
                reciprocals(ch, n)

            def scale_rows(src, dst):
                for j in range(GT):
                    last = v.tensor_scalar(dst(j), src(j), mv[:, j, 0:1], rstd[:, j:j + 1], ALU.subtract, ALU.mult)
                return last

            def take(c, stage, other, dst):
                for j in range(GT):
                    hold(v, "dve", z_ready, NT * Z[stage] + GT * c + j + 1)
                    v.tensor_tensor(dst(j), z_bank(stage, j)[:, 0:D], other(j), ALU.add).then_inc(z_free, 1)
                hold(v, "dve", z_free, NT * Z[stage] + GT * c + GT + 1)

            def tmp_tile(j):
                return tmp[:, j, :]

            def tile(X, c):
                return lambda j: X[:, bass.ds(c * GT + j, 1), :].rearrange("p t d -> p (t d)")

            def tiles(X, c):
                return X[:, bass.ds(c * GT, GT), :]

            def tile_c(c):
                return lambda j: XC[:, bass.ds(c * GT + j, 1), :, :].rearrange("p t h n -> p (t h) n")

            def take_layer(c, layer, y=tmp):
                dst = lambda j: y[:, j, :]
                if layer == 0:
                    take(c, "L0", tile(XA, c), dst)
                else:
                    take(c, "L1", lambda j: rows["b1L"][0][:, :], dst)

            def sum_layer(ch, c, layer, y=tmp):
                flat_y = y[:, :, :].rearrange("p t d -> p (t d)")
                if layer == 0:
                    ch.link(v.tensor_tensor(y[:, :, :], y[:, :, :], row_group("b0"), ALU.add))
                else:
                    ch.link(v.scalar_tensor_tensor(out=flat_y, in0=flat_y, scalar=0.0, in1=tiles(XB, c).rearrange("p t d -> p (t d)"),
                                                   op0=ALU.max, op1=ALU.add))
                statistics(ch, lambda j: y[:, j, :])

            def norm_layer(c, layer, y=tmp):
                if layer == 0:
                    scale_rows(lambda j: y[:, j, :], tile(XB, c)).then_inc(x_ready, 1)
                else:
                    scale_rows(lambda j: y[:, j, :].rearrange("p (h n) -> p h n", h=FH), tile_c(c)).then_inc(x_ready, 1)
                hold(v, "dve", x_ready, NG * layer + c + 1)

            v.wait_ge(weights_in, 16 * N_WEIGHT_LOADS)
            for layer in range(3):
                split(layer, 0, 0, EARLY)
                if layer:
                    done = layer - 1
                    evacuate(NG - 1, done)
                    take_layer(NG - 2, done)
                    take_layer(NG - 1, done, tmp_b)
                    low_part(straight(), 0, layer)
                split(layer, 0, 0, LATE)
                if layer:
                    low_part(straight(), 1, layer)
                split(layer, 0, 1)
                if layer:
                    sum_layer(straight(), NG - 2, done)
                    reciprocals(straight(), ln(f"L{done}", NG - 2))
                    norm_layer(NG - 2, done)
                    low_part(straight(), 2, layer)
                split(layer, 0, 2)
                if layer:
                    sum_layer(straight(), NG - 1, done, tmp_b)
                    reciprocals(straight(), ln(f"L{done}", NG - 1))
                    norm_layer(NG - 1, done, tmp_b)
                    low_part(straight(), 3, layer)
                split(layer, 0, 3)
                if layer:
                    low_part(straight(), 4, layer)
                split(layer, 0, 4)
                split(layer, 1, 0, EARLY)
                evacuate(0, layer)
                split(layer, 1, 0, LATE)
                for k in range(1, NG):
                    split(layer, 1, k)
                start = chain[0]
                with v.Fori(2, NG) as c:
                    ch = trip(c - 2, start, 3)
                    split(layer, c, 0, EARLY)
                    evacuate(c - 1, layer)
                    if layer < 2:
                        take_layer(c - 2, layer)
                    split(layer, c, 0, LATE)
                    split(layer, c, 1)
                    if layer < 2:
                        sum_layer(ch, c - 2, layer)
                    split(layer, c, 2)
                    if layer < 2:
                        reciprocals(ch, ln(f"L{layer}", c - 2))
                    split(layer, c, 3)
                    if layer < 2:
                        norm_layer(c - 2, layer)
                    split(layer, c, 4)
                if layer < 2:
                    chain[0] = start + 3 * (NG - 2)
            evacuate(NG - 1, 2)
            link(v.memset(s_ring[:, RING - 1, :], 0.0))

            def batch_norm(n, g, be):
                for c in range(NG):
                    for f in range(FH):
                        for o in range(2):
                            v.wait_ge(t_free, 2 + 4 * (NG * n + c) + 2 * f + o + 1)
                            lo = c * GC + o * PIECE
                            last = v.bn_stats(bn_stat[:, f, 2 * c + o, :], xT[:, f, lo:min(lo + PIECE, N)])
                link(last)
                for f in range(FH):
                    last = v.bn_aggr(bn_mv[:, f, :], bn_stat[:, f, :, :].rearrange("p k s -> p (k s)"))
                last.then_inc(bn_var, 1)
                v.wait_ge(bn_sd_ready, n + 1)
                link(v.reciprocal(bn_scale[:, :], bn_sd[:, :]))
                link(v.tensor_tensor(bn_scale[:, :], bn_scale[:, :], cols[g][0][:, :], ALU.mult))
                link(v.tensor_tensor(bn_ms[:, :], bn_mv[:, :, 0], bn_scale[:, :], ALU.mult))
                v.tensor_tensor(bn_shift[:, :], cols[be][0][:, :], bn_ms[:, :], ALU.subtract).then_inc(bn_ready, 1)

            batch_norm(0, "g1", "be1")
            batch_norm(1, "g2", "be2")
            def tiles2(c, start):
                ch = trip(c, start, 2)
                for j in range(GT):
                    hold(v, "dve", back_ready, GT * c + j + 1)
                    v.tensor_tensor(XB[:, bass.ds(c * GT + j, 1), :].rearrange("p t (h n) -> p (t h) n", h=FH),
                                    bank[j % 4][:, 0:D].rearrange("p (h n) -> p h n", h=FH), tile_c(c)(j), ALU.add).then_inc(back_free, 1)
                hold(v, "dve", back_free, GT * c + GT + 1)
                deviations(ch, ln("L2", c), tile(XB, c))
                scale_rows(tile(XB, c), tile(XB, c)).then_inc(x_ready, 1)
                hold(v, "dve", x_ready, XR["L2"] * NG + c + 1)

            start = chain[0]
            with v.Fori(0, NG) as c:
                tiles2(c, start)
            chain[0] = start + 2 * NG

            def running_max(l, i, first=False):
                for u in range(RING):
                    if u % HALF == 0 and not first:
                        hold(v, "dve", max_stored[u // HALF], 16 * (l * ROUNDS + i))
                    hold(v, "dve", gathered[u], 16 * (l * ROUNDS + i + 1))
                    hold(v, "dve", max_done, RING + l * CH + RING * i + u)
                    v.scalar_tensor_tensor(out=s_ring[:, u, :], in0=s_ring[:, (u - 1) % RING, :],
                                           scalar=seg[:, bass.ds(RING * i + u, 1)], in1=g_ring[:, u, :],
                                           op0=ALU.min, op1=ALU.max).then_inc(max_done, 1)

            for l in range(LAYERS3):
                if l == 0:
                    running_max(l, 0, True)
                with v.Fori(1 if l == 0 else 0, ROUNDS) as i:
                    running_max(l, i)
                v.wait_ge(fix_T, l + 1)
                for f in range(FH):
                    last = v.tensor_tensor_scan(RT[:, f, 1:P + 1], whole_row[:, :], bank[0][:, f * P:(f + 1) * P], -BIG,
                                                ALU.min, ALU.max)
                last.then_inc(fix_scan, 1)
                v.wait_ge(fix_back, l + 1)
                v.wait_ge(fix_read, 16 * (l + 1))
                v.scalar_tensor_tensor(out=fix_new[:, :], in0=bank[1][:, 0:D], scalar=carry_mask[:, 0:1], in1=fix_old[:, :],
                                       op0=ALU.min, op1=ALU.max).then_inc(fix_ready, 1)
                if l == 0:
                    for c in range(NG):
                        last = v.tensor_tensor(XB[:, c * GT:(c + 1) * GT, :], XB[:, c * GT:(c + 1) * GT, :], row_group("lb3"), ALU.add)
                    link(last)

                start = chain[0]
                per = (0, 4, 7)[l]

                def take_post(c):
                    take(c, f"post{l}", tile(PG, c), tile(PG, c))

                def finish(c):
                    ch = trip(c, start, per)
                    y, ys = tile(PG, c), tiles(PG, c).rearrange("p t d -> p (t d)")
                    xs = tiles(XD, c).rearrange("p t d -> p (t d)")
                    if l == 0:
                        v.tensor_scalar(xs, ys, 0.0, None, ALU.max).then_inc(x_ready, 1)
                        return
                    g, b = rows[f"lg{l + 1}"][0], rows[f"lb{l + 1}"][0]
                    ch.link(v.scalar_tensor_tensor(out=ys, in0=ys, scalar=0.0, in1=xs, op0=ALU.max, op1=ALU.add))
                    deviations(ch, ln(f"post{l}", c), y)
                    for j in range(GT):
                        last = v.scalar_tensor_tensor(out=y(j), in0=y(j), scalar=mv[:, j, 0:1], in1=g[:, :],
                                                      op0=ALU.subtract, op1=ALU.mult)
                    ch.link(last)
                    for j in range(GT):
                        last = v.scalar_tensor_tensor(out=tile(XD, c)(j) if l == 1 else y(j), in0=y(j), scalar=rstd[:, j:j + 1],
                                                      in1=b[:, :] if l == 1 else tile(XB, c)(j), op0=ALU.mult, op1=ALU.add)
                    if l == 1:
                        last.then_inc(x_ready, 1)
                        hold(v, "dve", x_ready, XR["post1"] * NG + c + 1)
                    else:
                        ch.link(last)
                        deviations(ch, ln("out", c), y)
                        hold(v, "dve", out_ready, c + 1)
                        v.tensor_copy(out_scale[:, :], rstd[:, :])
                        v.scalar_tensor_tensor(out=out_shift[:, :], in0=mv[:, :, 0], scalar=-1.0, in1=rstd[:, :],
                                               op0=ALU.mult, op1=ALU.mult).then_inc(out_scale_ready, 1)
                        hold(v, "dve", out_scale_ready, c + 1)
                    assert ch.n == per, (l, ch.n, per)

                take_post(0)
                with v.Fori(1, NG) as c:
                    take_post(c)
                    finish(c - 1)
                finish(NG - 1)
                chain[0] = start + per * NG

        @block.scalar
        def _(act):
            act.sem_inc(tp_free, 1)
            act.sem_inc(out_ready, 1)
            act.sem_inc(t_free, 2)
            def copy_cols(i, h):
                s = 2 * i + h
                hold(act, "act", rows_ready, s + 1)
                act.activation(key_cols[:, h, :], key[:, bass.ds(STREAMS * s, STREAMS)], ACT.Copy)
                act.activation(w_cols[:, h, :], wS[:, bass.ds(STREAMS * s, STREAMS)], ACT.Copy).then_inc(cols_ready, 1)

            def copy_rows(i, h):
                s = 2 * i + h
                hold(act, "act", rows_read, s + 1)
                hold(act, "act", rows_ready, s + 3)
                act.activation(w_rows[:, h, :, :].rearrange("p q n -> p (q n)"), bank[2 * h + 1][:, :], ACT.Copy).then_inc(w_rows_ready, 1)

            act.wait_ge(small_ready, 1)
            for h in range(2):
                copy_cols(0, h)
            with act.Fori(0, STEPS // 2 - 1) as i:
                for h in range(2):
                    copy_rows(i, h)
                    copy_cols(i + 1, h)
            for h in range(2):
                copy_rows(STEPS // 2 - 1, h)

            def evacuate(c, layer):
                hold(act, "act", a_used, GT + NT * (NG * layer + c + 1))
                for o in range(2):
                    act.activation(AT[:, 0, bass.ds(c * GC + o * PIECE, PIECE)], bank[o][:, 0:PIECE], ACT.Copy).then_inc(y_out, 1)

            def deviation(n):
                hold(act, "act", var_ready, n + 1)
                act.activation(sd[:, :], mv[:, :, 1], ACT.Sqrt, bias=eps_col[:, 0:1]).then_inc(sd_ready, 1)

            def turned_one(c, j, r, dst):
                hold(act, "act", tp_ready, NT * r + GT * c + j + 1)
                act.activation(dst, bank[6 + j % 2][:, 0:D].rearrange("p (h n) -> p h n", h=FH), ACT.Copy).then_inc(tp_free, 1)

            def turned(c, r, dst):
                for j in range(GT):
                    turned_one(c, j, r, dst(j))

            def turn_x(c, r):
                turned(c, r, lambda j: xT[:, :, bass.ds(c * GC + j * P, P)])

            def high_parts(layer, c, k, js=range(GT)):
                if layer:
                    act.wait_ge(x_ready, NG * (layer - 1) + k + 1)
                for j in js:
                    hold(act, "act", a_in[j], 16 * (layer * NT + NG * c + k + 1))
                    act.activation(hi_ring[:, j, :], a_ring[:, j, :], ACT.Copy)
                    t = k * GT + j
                    if layer == 2:
                        x_tile, dst = XC[:, t, :, :], x_hi_ring[:, j, :].rearrange("p (h n) -> p h n", h=FH)
                    else:
                        x_tile, dst = (XA, XB)[layer][:, t, :], x_hi_ring[:, j, :]
                    act.activation(dst, x_tile, ACT.Copy).then_inc(hi_ready, 1)

            def take_t(c, n, b, dst):
                for f in range(FH):
                    for o in range(2):
                        hold(act, "act", t_ready, 4 * (NG * n + c) + 2 * f + o + 1)
                        ins = act.activation(dst[:, f, bass.ds(c * GC + o * PIECE, PIECE)], bank[4 + o][:, 0:PIECE], ACT.Identity,
                                             bias=cols[b][0][:, f:f + 1])
                        ins.then_inc(t_free, 1)

            def bn_deviation(n):
                act.wait_ge(bn_var, n + 1)
                act.activation(bn_sd[:, :], bn_mv[:, :, 1], ACT.Sqrt, bias=eps_col[:, 0:1]).then_inc(bn_sd_ready, 1)
                act.wait_ge(bn_ready, n + 1)

            def rectify(c):
                for f in range(FH):
                    last = act.activation(HT[:, f, bass.ds(c * GC, GC)], xT[:, f, bass.ds(c * GC, GC)], ACT.Relu,
                                          scale=bn_scale[:, f:f + 1], bias=bn_shift[:, f:f + 1])
                last.then_inc(r_ready, 1)

            for layer in range(3):
                high_parts(layer, 0, 0, EARLY)
                if layer:
                    evacuate(NG - 1, layer - 1)
                    turn_x(0, TP[f"L{layer}"])
                high_parts(layer, 0, 0, LATE)
                high_parts(layer, 0, 1)
                if layer:
                    deviation(ln(f"L{layer - 1}", NG - 2))
                high_parts(layer, 0, 2)
                if layer:
                    deviation(ln(f"L{layer - 1}", NG - 1))
                high_parts(layer, 0, 3)
                high_parts(layer, 0, 4)

                def group(c, complete):
                    high_parts(layer, c, 0, EARLY)
                    if layer < 2:
                        evacuate(c - 1, layer)
                    high_parts(layer, c, 0, LATE)
                    if layer == 2 and complete:
                        take_t(c - 2, 0, "b1", xT)
                    if layer:
                        turn_x(c, TP[f"L{layer}"])
                    high_parts(layer, c, 1)
                    high_parts(layer, c, 2)
                    if layer < 2 and complete:
                        deviation(ln(f"L{layer}", c - 2))
                    high_parts(layer, c, 3)
                    high_parts(layer, c, 4)

                group(1, False)
                with act.Fori(2, NG) as c:
                    group(c, True)
            take_t(NG - 2, 0, "b1", xT)
            take_t(NG - 1, 0, "b1", xT)
            bn_deviation(0)
            rectify(0)
            with act.Fori(1, NG) as c:
                rectify(c)
                take_t(c - 1, 1, "b2", xT)
            take_t(NG - 1, 1, "b2", xT)
            bn_deviation(1)
            with act.Fori(0, NG) as c:
                rectify(c)

            def prepare(c):
                turn_x(c, TP["prep"])
                for j in range(GT):
                    hold(act, "act", z_ready, NT * Z["prep"] + GT * c + j + 1)
                    last = act.activation(XC[:, bass.ds(c * GT + j, 1), :, :].rearrange("p t h n -> p (t h) n"),
                                          z_bank("prep", j)[:, 0:D].rearrange("p (h n) -> p h n", h=FH), ACT.Relu)
                    last.then_inc(z_free, 1)
                hold(act, "act", z_free, NT * Z["prep"] + GT * c + GT + 1)
                act.sem_inc(h_ready, 1)

            deviation(ln("L2", 0))
            with act.Fori(1, NG) as c:
                deviation(ln("L2", c))
                prepare(c - 1)
            prepare(NG - 1)


            def stage(l, i, h, first=False):
                if not first:
                    for u in range(HALF * h, HALF * (h + 1)):
                        hold(act, "act", gathered[u], 16 * (l * ROUNDS + i))
                act.activation(src_idx[:, HALF * h:HALF * (h + 1)], srcC[:, bass.ds(RING * i + HALF * h, HALF)],
                               ACT.Copy).then_inc(idx_ready, 1)

            for l in range(LAYERS3):
                for h in range(2):
                    stage(l, 0, h, l == 0)
                with act.Fori(0, NG) as c:
                    for j in range(GT):
                        t = c * GT + j
                        for h in range(2):
                            stage(l, t + 1, h)
                        if l:
                            turned_one(c, j, TP[f"part{l}"], xT[:, :, bass.ds(c * GC + j * P, P)])
                        hold(act, "act", z_ready, NT * Z[f"part{l}"] + t + 1)
                        act.activation(PG[:, bass.ds(t, 1), :].rearrange("p t d -> p (t d)"), bank[4 + j % 2][:, 0:D], ACT.Copy).then_inc(z_free, 1)
                with act.Fori(NT + 1, ROUNDS) as i:
                    for h in range(2):
                        stage(l, i, h)

                def turn_pooled(c, js):
                    for j in js:
                        turned_one(c, j, TP[f"post{l}"], pT[:, j, :, :])

                def finish(c, after=None):
                    def turn_next(js):
                        if after is not None:
                            turn_pooled(after, js)

                    turn_next((0, 1))
                    if l:
                        deviation(ln(f"post{l}", c))
                    turn_next((2, 3))
                    if l == 2:
                        deviation(ln("out", c))
                    turn_next((4,))
                    if l == 2:
                        hold(act, "act", out_scale_ready, c + 1)
                        for j in range(GT):
                            t = bass.ds(c * GT + j, 1)
                            last = act.activation(XD[:, t, :].rearrange("p t d -> p (t d)"), PG[:, t, :].rearrange("p t d -> p (t d)"),
                                                  ACT.Identity, scale=out_scale[:, j:j + 1], bias=out_shift[:, j:j + 1])
                        last.then_inc(out_ready, 1)

                turn_pooled(0, range(GT))
                turn_pooled(1, range(GT))
                with act.Fori(0, NG - 2) as c:
                    finish(c, c + 2)
                finish(NG - 2)
                finish(NG - 1)

        @block.tensor
        def _(pe):
            pe.sem_inc(hist_done, 2)
            pe.sem_inc(rows_ready, 2)
            pe.sem_inc(a_used, GT)

            pe.wait_ge(pool_const, 2)
            def edge_step(i, h, start=False, stop=False):
                s = 2 * i + h
                hold(pe, "pe", rows_read, s + 1)
                hold(pe, "pe", cols_ready, s + 1)
                for u in range(STREAMS):
                    pe.transpose(bank[2 * h][:, u * P:(u + 1) * P], key_cols[:, h, u:u + 1].to_broadcast([P, P]), ident[:, :])
                    last = pe.transpose(bank[2 * h + 1][:, u * P:(u + 1) * P], w_cols[:, h, u:u + 1].to_broadcast([P, P]), ident[:, :])
                last.then_inc(rows_ready, 1)
                hold(pe, "pe", hot_ready, s + 1)
                for u in range(STREAMS):
                    last = pe.matmul(bank[4][:, 0:NT], hot_lo[:, h, u, :], hot_hi[:, h, u, :],
                                     start=start and u == 0, stop=stop and u == STREAMS - 1)
                last.then_inc(hist_done, 1)

            edge_step(0, 0, start=True)
            edge_step(0, 1)
            with pe.Fori(1, STEPS // 2 - 1) as i:
                edge_step(i, 0)
                edge_step(i, 1)
            edge_step(STEPS // 2 - 1, 0)
            edge_step(STEPS // 2 - 1, 1, stop=True)

            pe.wait_ge(small_ready, 3)
            pe.matmul(bank[6][:, 0:NT], upto[:, :], cnt[:, :], start=True, stop=True)
            pe.matmul(bank[6][:, NT:2 * NT], ones[:, :], cnt[:, :], start=True, stop=True)
            pe.transpose(bank[7][:, 0:P], whole_mask[:, 0:1].to_broadcast([P, P]), ident[:, :]).then_inc(pe_small, 1)

            def turn_one(src, c, j, r):
                g = NT * r + GT * c + j
                pe.wait_ge(tp_free, g if j else g + 1)
                for f in range(FH):
                    last = pe.transpose(bank[6 + j % 2][:, f * P:(f + 1) * P], src(j, f), ident[:, :])
                last.then_inc(tp_ready, 1)

            def turn(src, c, r):
                for j in range(GT):
                    turn_one(src, c, j, r)

            def tile_of(X, c):
                return lambda j, f: X[:, c * GT + j, f * P:(f + 1) * P]

            def tile_h(c):
                return lambda j, f: XC[:, c * GT + j, f, :]

            def aggregate(c, layer):
                pe.wait_ge(y_out, 4 * (NG * layer + c) + y_start)
                for k in range(NG):
                    m = layer * NT + NG * c + k
                    if c == 0:
                        pe.wait_ge(lo_ready, NG * layer + k + 1)
                    for j in range(GT):
                        pe.wait_ge(split_ready, m * GT + j + 1)
                        first, final = k == 0 and j == 0, k == NG - 1 and j == GT - 1
                        a_hi = [hi_ring[:, j, o * PIECE:(o + 1) * PIECE] for o in range(2)]
                        a_lo = [lo_ring[:, j, o * PIECE:(o + 1) * PIECE] for o in range(2)]
                        for f in range(FH):
                            x_hi = x_hi_ring[:, j, f * P:(f + 1) * P]
                            x_lo = X_LO[layer][:, k * GT + j, f * P:(f + 1) * P]
                            for o in range(2):
                                pe.matmul(bank[2 * f + o][:, 0:PIECE], x_hi, a_hi[o], start=first, stop=False)
                            for o in range(2):
                                pe.matmul(bank[2 * f + o][:, 0:PIECE], x_hi, a_lo[o], start=False, stop=False)
                            for o in range(2):
                                last = pe.matmul(bank[2 * f + o][:, 0:PIECE], x_lo, a_hi[o], start=False, stop=final)
                        last.then_inc(a_used, 1)

            y_start = 1
            pe.sem_inc(y_out, 1)

            def product(c, stage, terms, j):
                pe.wait_ge(z_free, z_out(stage, c, j))
                for n, (lhs, rhs) in enumerate(terms):
                    last = pe.matmul(z_bank(stage, j)[:, 0:D], lhs, rhs, start=n == 0, stop=n == len(terms) - 1)
                last.then_inc(z_ready, 1)

            def nodes(B, c, j, f):
                return B[:, f, bass.ds(c * GC + j * P, P)]

            def dense0(c):
                pe.wait_ge(y_out, 4 * (NG * 0 + c) + 4 + y_start)
                for j in range(GT):
                    product(c, "L0", [(nodes(AT, c, j, f), W0s[:, f, :]) for f in range(FH)], j)

            def dense1(c):
                pe.wait_ge(y_out, 4 * (NG * 1 + c) + 4 + y_start)
                pe.wait_ge(tp_free, 1 + NT * TP["L1"] + GT * c + GT)
                for j in range(GT):
                    product(c, "L1", [(nodes(B, c, j, f), W1Ls[:, FH * n + f, :]) for n, B in enumerate((xT, AT)) for f in range(FH)], j)

            def block_product(c, n, w):
                for f in range(FH):
                    for o in range(2):
                        g = 4 * (NG * n + c) + 2 * f + o
                        pe.wait_ge(t_free, g + 1)
                        for k in range(FH):
                            last = pe.matmul(bank[4 + o][:, 0:PIECE], w[:, k, f * P:(f + 1) * P],
                                             HT[:, k, bass.ds(c * GC + o * PIECE, PIECE)], start=k == 0, stop=k == FH - 1)
                        last.then_inc(t_ready, 1)

            pe.wait_ge(x_in, 32)
            pe.wait_ge(weights_in, 16 * N_WEIGHT_LOADS)
            pe.wait_ge(small_ready, 4)
            aggregate(0, 0)
            for c in range(1, NG):
                aggregate(c, 0)
                dense0(c - 1)
            dense0(NG - 1)

            pe.wait_ge(x_ready, 1)
            turn(tile_of(XB, 0), 0, TP["L1"])
            aggregate(0, 1)
            for c in range(1, NG):
                turn(tile_of(XB, c), c, TP["L1"])
                aggregate(c, 1)
                dense1(c - 1)
            dense1(NG - 1)

            def dense2(c):
                pe.wait_ge(y_out, 4 * (NG * 2 + c) + 4 + y_start)
                block_product(c, 0, W1s)

            pe.wait_ge(x_ready, NG + 1)
            pe.wait_ge(z_free, 1 + 2 * NT)
            turn(tile_h(0), 0, TP["L2"])
            pe.wait_ge(tp_free, 1 + NT * TP["L2"] + GT)
            aggregate(0, 2)
            for c in range(1, NG):
                turn(tile_h(c), c, TP["L2"])
                pe.wait_ge(tp_free, 1 + NT * TP["L2"] + GT * c + GT)
                aggregate(c, 2)
                dense2(c - 1)
            dense2(NG - 1)
            for c in range(NG):
                pe.wait_ge(r_ready, c + 1)
                block_product(c, 1, W2s)
            pe.wait_ge(t_free, 2 + 8 * NG)
            for c in range(NG + 1):
                if c < NG:
                    pe.wait_ge(r_ready, NG + c + 1)
                    for j in range(GT):
                        g = GT * c + j
                        pe.wait_ge(back_free, max(1, g + (1, -3, -3, -3, -2)[j]))
                        for f in range(FH):
                            last = pe.transpose(bank[j % 4][:, f * P:(f + 1) * P], nodes(HT, c, j, f), ident[:, :])
                        last.then_inc(back_ready, 1)
                if c:
                    pe.wait_ge(x_ready, NG * XR["L2"] + c)
                    turn(tile_of(XB, c - 1), c - 1, TP["prep"])
                    pe.wait_ge(tp_free, 1 + NT * TP["prep"] + GT * c)
                    for j in range(GT):
                        product(c - 1, "prep", [(nodes(xT, c - 1, j, f), Wps[:, f, :]) for f in range(FH)]
                                + [(row0[:, :], rows["bp"][0][:, :])], j)

            for l, Wm in enumerate((Wm1s, Wm2s, Wm3s)):
                for c in range(NG):
                    if l:
                        pe.wait_ge(x_ready, NG * XR[f"post{l - 1}"] + c + 1)
                    for j in range(GT):
                        if l:
                            turn_one(tile_of(XD, c), c, j, TP[f"part{l}"])
                            pe.wait_ge(tp_free, 1 + NT * TP[f"part{l}"] + GT * c + j + 1)
                        product(c, f"part{l}", [(nodes(xT, c, j, f), Wm[:, f, :]) for f in range(FH)]
                                + [(row0[:, :], rows[f"bm{l + 1}"][0][:, :])], j)
                pe.wait_ge(max_done, RING + CH * (l + 1))
                for f in range(FH):
                    last = pe.transpose(bank[0][:, f * P:(f + 1) * P], s_ring[:, RING - 1, f * P:(f + 1) * P], ident[:, :])
                last.then_inc(fix_T, 1)
                pe.wait_ge(fix_scan, l + 1)
                for f in range(FH):
                    last = pe.transpose(bank[1][:, f * P:(f + 1) * P], RT[:, f, 0:P], ident[:, :])
                last.then_inc(fix_back, 1)
                pe.wait_ge(z_free, 1 + NT * (Z[f"part{l}"] + 1))

                def turn_pooled(t):
                    c, j = divmod(t, GT)
                    g = NT * TP[f"post{l}"] + t
                    pe.wait_ge(pooled[j], 16 * (NG * l + c + 1))
                    pe.wait_ge(tp_free, g if j else g + 1)
                    for f in range(FH):
                        last = pe.transpose(bank[6 + j % 2][:, f * P:(f + 1) * P], p_ring[:, j, f * P:(f + 1) * P], ident[:, :])
                    last.then_inc(tp_ready, 1)

                turn_pooled(0)
                for t in range(NT):
                    if t + 1 < NT:
                        turn_pooled(t + 1)
                    c, j = divmod(t, GT)
                    pe.wait_ge(tp_free, NT * TP[f"post{l}"] + t + 2)
                    product(c, f"post{l}", [(pT[:, j, f, :], Wm[:, FH + f, :]) for f in range(FH)], j)


def kernel(**inputs):
    import concourse.bacc as _bacc
    from concourse.bass_utils import run_bass_kernel_spmd as _run

    def arr(name):
        return np.asarray(inputs[name])

    def padded(a, fill, n=EP):
        return np.concatenate([a, np.full(n - a.shape[0], fill, a.dtype)])

    def in_steps(a):
        return np.ascontiguousarray(a.reshape(BLOCKS, STREAMS, RUN, P).transpose(3, 0, 2, 1).reshape(P, CH))

    src, w = padded(arr("src"), 0), padded(arr("edge_weight"), 0)
    dst = padded(arr("dst"), PAD_DST)
    given = {
        "src_steps": in_steps(src), "dst_steps": in_steps(dst), "w_steps": in_steps(w),
        "src_chunks": src.reshape(P, CH), "dst_flat": padded(dst, END_DST, EP + FAR),
        "x": arr("x"), "W0": arr("L0_gnn_weight"), "b0": arr("L0_gnn_bias"), "W1L": arr("L1_gnn_W"), "b1L": arr("L1_gnn_b"),
        "eps": arr("L2_gnn_eps"), "W1": arr("L2_gnn_W1"), "b1": arr("L2_gnn_b1"), "g1": arr("L2_gnn_g1"), "be1": arr("L2_gnn_be1"),
        "W2": arr("L2_gnn_W2"), "b2": arr("L2_gnn_b2"), "g2": arr("L2_gnn_g2"), "be2": arr("L2_gnn_be2"),
        "Wp": arr("L3_gnn_Wp1").T, "bp": arr("L3_gnn_bp1"), "Wm1": arr("L3_gnn_Wm1").T, "bm1": arr("L3_gnn_bm1"),
        "Wm2": arr("L3_gnn_Wm2").T, "bm2": arr("L3_gnn_bm2"), "Wm3": arr("L3_gnn_Wm3").T, "bm3": arr("L3_gnn_bm3"),
        "lg2": arr("L3_gnn_ln2_g"), "lb2": arr("L3_gnn_ln2_b"), "lg3": arr("L3_gnn_ln3_g"), "lb3": arr("L3_gnn_ln3_b"),
    }
    nc = _bacc.Bacc("TRN2", target_bir_lowering=False, num_devices=1)
    arrays, args = {}, []
    for name, a in given.items():
        a = np.ascontiguousarray(a)
        arrays[f"in_{name}"] = a
        args.append(nc.dram_tensor(f"in_{name}", a.shape, mybir.dt.from_np(a.dtype), kind="ExternalInput").ap())
    args.append(nc.dram_tensor("out_0", (N, D), F32, kind="ExternalOutput").ap())
    build(nc, *args)
    r = _run(nc, [arrays], core_ids=[0])
    return r.results[0]["out_0"]
```

```python
from contextlib import ExitStack

import numpy as np

import concourse.bass as bass
from concourse import mybir

P = 128
ALU = mybir.AluOpType
ACT = mybir.ActivationFunctionType
AX = mybir.AxisListType
F32 = mybir.dt.float32
BF16 = mybir.dt.bfloat16
I32 = mybir.dt.int32
F32R = mybir.dt.float32r

N, E, D = 3125, 50000, 256
FH = D // P
NT = -(-N // P)
NP = NT * P
GT = 5
NG = NT // GT
GC = GT * P
PIECE = GC // 2
WIDE = 4
STREAMS = 2 * WIDE
BLOCKS, RUN = 7, 7
TURNS = BLOCKS * RUN
STEPS = 2 * TURNS
CH = STREAMS * TURNS
EP = CH * P
FAR = (RUN - 2) * P
PAD_DST = N
END_DST = N + 1
JUNK = NP * NP
A_ROWS = NP + 1
ZERO_ROW = EP
BIG = float(np.finfo(np.float32).max)
EPS = 1e-5
RING = 8
HALF = RING // 2
ROUNDS = CH // RING
LAYERS3 = 3


def build(nc, src_steps, dst_steps, w_steps, src_chunks, dst_flat, x, W0, b0, W1L, b1L, eps, W1, b1, g1, be1,
          W2, b2, g2, be2, Wp, bp, Wm1, bm1, Wm2, bm2, Wm3, bm3, lg2, lb2, lg3, lb3, out):
    A = nc.dram_tensor("adjacency", (A_ROWS * NP, 1), F32, kind="Internal").ap()
    A_rows = A.rearrange("(r c) o -> r (c o)", c=NP)
    H = [nc.dram_tensor(f"pool_in_{l}", (NP, D), F32, kind="Internal").ap() for l in range(LAYERS3)]
    S = [nc.dram_tensor(f"running_max_{l}", (EP + P, D), F32, kind="Internal").ap() for l in range(LAYERS3)]

    with ExitStack() as ctx:
        place = {}

        def sb(name, shape, dt=F32):
            place[name] = -(-nc.sbuf_base // 32) * 32
            return ctx.enter_context(nc.sbuf_tensor(name, shape, dt))

        def sem(name):
            return ctx.enter_context(nc.semaphore(name))

        def one_pass(name, like, shape):
            return nc.alloc_sbuf_tensor_at(name, shape, F32R, offset=place[like])

        XA, XB = sb("XA", [P, NT, D]), sb("XB", [P, NT, D])
        xT, AT = sb("xT", [P, FH, NP]), sb("AT", [P, FH, NP])

        def by_node(buf):
            return buf[:, :, :].rearrange("p h n -> p (h n)").rearrange("p (t d) -> p t d", d=D)

        HT = XA[:, :, :].rearrange("p t d -> p (t d)").rearrange("p (h n) -> p h n", n=NP)
        XC = AT[:, :, :].rearrange("p h (t n) -> p t h n", n=P)
        XD, PG = by_node(AT), XA
        X_LO = [one_pass(f"x_lo{n}", buf, [P, NT, D]) for n, buf in enumerate(("xT", "XA", "XB"))]
        a_ring = sb("a_ring", [P, GT, GC])
        rings = sb("rings", [P, 2 * RING, D])
        g_ring, s_ring = rings[:, 0:RING, :], rings[:, RING:2 * RING, :]
        hi_ring = one_pass("hi_ring", "rings", [P, GT, GC])
        lo_ring = one_pass("lo_ring", "a_ring", [P, GT, GC])
        p_ring = a_ring[:, 0:2, :].rearrange("p a n -> p (a n)").rearrange("p (t d) -> p t d", d=D)
        pT = a_ring[:, 2:4, :].rearrange("p a n -> p (a n)").rearrange("p (t h n) -> p t h n", h=FH, n=P)
        tmp = sb("tmp", [P, GT, D])
        tmpf = tmp[:, :, :].rearrange("p t d -> p (t d)")

        srcS, dstS, wS = sb("srcS", [P, CH], I32), sb("dstS", [P, CH], I32), sb("wS", [P, CH])
        key, junk = sb("key", [P, CH]), sb("junk", [P, CH])
        node_lo, node_hi = sb("node_lo", [P, CH]), sb("node_hi", [P, CH])
        srcC, dstC = sb("srcC", [P, CH], I32), sb("dstC", [P, CH], I32)
        x_hi_ring = one_pass("x_hi_ring", "srcS", [P, GT, D])
        tmp_b = nc.alloc_sbuf_tensor_at("tmp_b", [P, GT, D], F32, offset=place["srcS"] + 4 * GT * D)
        assert 7 * CH >= 2 * GT * D
        dst_next, dst_far = sb("dst_next", [P, CH], I32), sb("dst_far", [P, CH], I32)
        seg = sb("seg", [P, CH])
        eq = sb("eq", [P, CH])
        last_before = sb("last_before", [P, 1], I32)
        carry_mask = sb("carry_mask", [P, 1])
        whole_mask = sb("whole_mask", [P, 1])
        whole_row = sb("whole_row", [P, P])
        col = sb("col", [P, 16])
        fix_row = sb("fix_row", [P, 1], I32)
        end_row = sb("end_row", [P, NT], I32)
        cnt, incl, ends = sb("cnt", [P, NT]), sb("incl", [P, NT]), sb("ends", [P, NT])
        reach, reach_all = sb("reach", [P, BLOCKS + 1]), sb("reach_all", [P, BLOCKS + 1])
        reach_i = sb("reach_i", [1, BLOCKS + 1], I32)

        ident, ones = sb("ident", [P, P]), sb("ones", [P, P])
        before = sb("before", [P, P])
        upto = sb("upto", [P, P])
        row0 = sb("row0", [P, P])
        iota_i = sb("iota_i", [P, P], I32)
        iota_f = sb("iota_f", [P, P])
        key_cols, w_cols = sb("key_cols", [P, 2, WIDE]), sb("w_cols", [P, 2, WIDE])
        w_rows = sb("w_rows", [P, 2, WIDE, P])
        unused = sb("unused", [P, 2 * WIDE, P], BF16)
        hot_lo = sb("hot_lo", [P, 2, WIDE, P], BF16)
        hot_hi = sb("hot_hi", [P, 2, WIDE, NT], BF16)
        w_sum, w_out = sb("w_sum", [P, 2, WIDE]), sb("w_out", [P, 2, WIDE])
        repeats = sb("repeats", [P, 2, WIDE])
        moved = sb("moved", [P, 2, WIDE])
        idx_out = sb("idx_out", [P, 2, WIDE], I32)
        src_idx = sb("src_idx", [P, RING], I32)

        stats = sb("stats", [P, GT, 6])
        mv = sb("mv", [P, GT, 2])
        sd, rstd = sb("sd", [P, GT]), sb("rstd", [P, GT])
        bn_stat = sb("bn_stat", [P, FH, 2 * NG, 6])
        bn_mv = sb("bn_mv", [P, FH, 2])
        bn_sd, bn_scale, bn_shift, bn_ms = (sb(n, [P, FH]) for n in ("bn_sd", "bn_scale", "bn_shift", "bn_ms"))
        eps_col = sb("eps_col", [P, 1])
        eps1 = sb("eps1", [P, 1])
        row_sum, less_mean, sq_sum = (sb(n, [P, 2, GT]) for n in ("row_sum", "less_mean", "sq_sum"))
        sd_out = sb("sd_out", [P, GT])
        squares = a_ring[:, 4, :].bitcast(BF16).rearrange("p (t d) -> p t d", d=D)
        out_scale, out_shift = sb("out_scale", [P, GT]), sb("out_shift", [P, GT])

        RT = sb("RT", [P, FH, P + 1])
        fix_old, fix_new = sb("fix_old", [P, D]), sb("fix_new", [P, D])

        def weight(name, w):
            return sb(name, [P, w.shape[0] // P, D]), w.rearrange("(h p) n -> p h n", p=P)

        W0s, W1Ls, W1s, W2s, Wps, Wm1s, Wm2s, Wm3s = weights = [
            weight(n, w) for n, w in (("W0s", W0), ("W1Ls", W1L), ("W1s", W1), ("W2s", W2), ("Wps", Wp),
                                      ("Wm1s", Wm1), ("Wm2s", Wm2), ("Wm3s", Wm3))]
        W0s, W1Ls, W1s, W2s, Wps, Wm1s, Wm2s, Wm3s = (w[0] for w in weights)
        rows = {}
        for name, v in (("b0", b0), ("b1L", b1L), ("bp", bp), ("bm1", bm1), ("bm2", bm2), ("bm3", bm3),
                        ("lg2", lg2), ("lb2", lb2), ("lg3", lg3), ("lb3", lb3)):
            rows[name] = (sb(f"row_{name}", [P, D]), v)
        cols = {}
        for name, v in (("b1", b1), ("g1", g1), ("be1", be1), ("b2", b2), ("g2", g2), ("be2", be2)):
            cols[name] = (sb(f"col_{name}", [P, FH]), v)

        bank = [ctx.enter_context(nc.psum_tensor(f"bank{i}", [P, 512], F32)) for i in range(8)]

        def row_group(name):
            return rows[name][0][:, :].unsqueeze(1).to_broadcast([P, GT, D])

        edges_in = sem("edges_in")
        x_in, x_zero = sem("x_in"), sem("x_zero")
        weights_in = sem("weights_in")
        eps_in = sem("eps_in")
        zeros_ready, tiles_zero = sem("zeros_ready"), sem("tiles_zero")
        a_zeroed = [sem(f"a_zeroed{c}") for c in range(NG)]
        zero_row_in = sem("zero_row_in")
        pool_const = sem("pool_const")
        dve = sem("dve")
        cols_ready, rows_ready, w_rows_ready, rows_read = (
            sem(n) for n in ("cols_ready", "rows_ready", "w_rows_ready", "rows_read"))
        hot_ready, hist_done = sem("hot_ready"), sem("hist_done")
        merged, scatter_ready = sem("merged"), sem("scatter_ready")
        scattered = [sem(f"scattered{q}") for q in range(STREAMS)]
        sums_ready = sem("sums_ready")
        small_ready = sem("small_ready")
        hi_ready, split_ready, lo_ready = sem("hi_ready"), sem("split_ready"), sem("lo_ready")
        reach_ready, flag_ready = sem("reach_ready"), sem("flag_ready")
        a_in = [sem(f"a_in{j}") for j in range(GT)]
        a_used = sem("a_used")
        y_out = sem("y_out")
        t_ready, t_free = sem("t_ready"), sem("t_free")
        z_ready, z_free = sem("z_ready"), sem("z_free")
        tp_ready, tp_free = sem("tp_ready"), sem("tp_free")
        back_ready, back_free = sem("back_ready"), sem("back_free")
        x_ready = sem("x_ready")
        var_ready, sd_ready = sem("var_ready"), sem("sd_ready")
        bn_var, bn_sd_ready, bn_ready = sem("bn_var"), sem("bn_sd_ready"), sem("bn_ready")
        r_ready = sem("r_ready")
        h_ready, h_stored = sem("h_ready"), sem("h_stored")
        idx_ready = sem("idx_ready")
        gathered = [sem(f"gathered{u}") for u in range(RING)]
        max_done = sem("max_done")
        max_stored = [sem("max_stored0"), sem("max_stored1")]
        fix_read, fix_T, fix_scan, fix_back, fix_ready, fix_written = (
            sem(n) for n in ("fix_read", "fix_T", "fix_scan", "fix_back", "fix_ready", "fix_written"))
        pooled = [sem(f"pooled{j}") for j in range(GT)]
        out_ready, out_stored = sem("out_ready"), sem("out_stored")
        mean_ready, squared = sem("mean_ready"), sem("squared")
        out_scale_ready = sem("out_scale_ready")
        tick = {n: sem(f"tick_{n}") for n in ("sp", "act", "pe", "dve", "pool")}

        def hold(eng, name, s, value):
            eng.wait_ge(s, value)
            eng.sem_inc(tick[name], 1)

        N_EDGE_LOADS = 8
        EARLY, LATE = range(2), range(2, GT)
        AHEAD = GT
        N_WEIGHT_LOADS = len(weights) + len(rows) + len(cols)
        Z = {"L0": 0, "L1": 1, "prep": 2, "part0": 3, "post0": 4, "part1": 5, "post1": 6, "part2": 7, "post2": 8}
        TP = {"L1": 0, "L2": 1, "prep": 2, "post0": 3, "part1": 4, "post1": 5, "part2": 6, "post2": 7}
        def z_bank(stage, j):
            return bank[2 + j % 4] if stage.startswith("post") else bank[4 + j % 2]

        def t_bank(n, f, o):
            return bank[4 + 2 * f * n + o]

        def z_out(stage, c, j):
            g = NT * Z[stage] + GT * c + j
            if stage.startswith("post"):
                return g + (1, -3, -3, -3, -2)[j]
            return g + (0 if j else 1)

        XR = {"L0": 0, "L1": 1, "L2": 2, "post0": 3, "post1": 4}
        LN = {"L0": 0, "L1": 1, "L2": 2, "post1": 3, "post2": 4}

        def ln(stage, c):
            if stage == "out":
                return LN["post2"] * NG + 2 * c + 1
            return LN[stage] * NG + c * (2 if stage == "post2" else 1)

        def means(l, c, which):
            return c if l == 1 else NG + 2 * c + which

        block = ctx.enter_context(nc.Block())

        @block.sync
        def _(sp):
            def stretch(shift):
                return dst_flat[shift:shift + EP].rearrange("(p t) -> p t", p=P)

            sp.dma_start(srcS[:, :], src_steps).then_inc(edges_in, 16)
            sp.dma_start(dstS[:, :], dst_steps).then_inc(edges_in, 16)
            sp.dma_start(wS[:, :], w_steps).then_inc(edges_in, 16)
            sp.dma_start(srcC[:, :], src_chunks).then_inc(edges_in, 16)
            sp.dma_start(dstC[:, :], stretch(0)).then_inc(edges_in, 16)
            sp.dma_start(dst_next[:, :], stretch(1)).then_inc(edges_in, 16)
            sp.dma_start(dst_far[:, :], stretch(FAR)).then_inc(edges_in, 16)
            sp.wait_ge(x_zero, 1)
            sp.dma_start(last_before[1:P, :], stretch(0)[0:P - 1, CH - 1:CH], allow_slow_non_contiguous=True).then_inc(edges_in, 16)
            sp.dma_start(eps1[:, :], eps.rearrange("(a b) -> a b", a=1).to_broadcast([P, 1])).then_inc(eps_in, 16)
            sp.wait_ge(zeros_ready, 1)
            sp.dma_start(A_rows[NP:NP + 1, :].rearrange("o (p c) -> (o p) c", p=P), AT[:, 0, 0:NT]).then_inc(a_zeroed[0], 16)
            for t in range(NT):
                if t == AHEAD:
                    full = N // P
                    sp.dma_start(XA[:, 0:full, :], x[0:full * P, :].rearrange("(t p) d -> p t d", p=P)).then_inc(x_in, 16)
                    sp.dma_start(XA[0:N - full * P, full, :], x[full * P:N, :]).then_inc(x_in, 16)
                    for c in range(AHEAD // GT):
                        sp.wait_ge(a_zeroed[c], 16 * (GT + (c == 0)))
                    sp.sem_inc(tiles_zero, AHEAD)
                if t > AHEAD:
                    sp.wait_ge(a_zeroed[(t - 1) // GT], 16 * ((t - 1) % GT + 1))
                    sp.sem_inc(tiles_zero, 1)
                sp.dma_start(A_rows[t * P:(t + 1) * P, :], AT[:, 0, :]).then_inc(a_zeroed[t // GT], 16)
            for l in range(LAYERS3):
                sp.dma_start(S[l][ZERO_ROW:ZERO_ROW + P, :], AT[:, 0, 0:D]).then_inc(zero_row_in, 16)
            sp.wait_ge(a_zeroed[NG - 1], 16 * GT)
            sp.sem_inc(tiles_zero, 1)
            for tile, view in weights:
                sp.dma_start(tile[:, :, :], view).then_inc(weights_in, 16)
            for tile, v in rows.values():
                sp.dma_start(tile[:, :], v.rearrange("(a n) -> a n", a=1).to_broadcast([P, D])).then_inc(weights_in, 16)
            for tile, v in cols.values():
                sp.dma_start(tile[:, :], v.rearrange("(h p) -> p h", p=P), allow_slow_non_contiguous=True).then_inc(weights_in, 16)

            for q in range(STREAMS):
                sp.wait_ge(scattered[q], 16 * TURNS)
            sp.wait_ge(zero_row_in, 16 * LAYERS3)
            for layer in range(3):
                with sp.Fori(0, NG) as c:
                    with sp.Fori(0, NG) as k:
                        m = layer * NT + NG * c + k
                        for j in range(GT):
                            hold(sp, "sp", a_used, m * GT + j + 1)
                            sp.dma_start(a_ring[:, j, :], A_rows[bass.ds((k * GT + j) * P, P), bass.ds(c * GC, GC)]).then_inc(a_in[j], 16)

            def store_rows(l):
                for c in range(NG):
                    if l:
                        sp.wait_ge(x_ready, NG * XR[f"post{l - 1}"] + c + 1)
                    else:
                        sp.wait_ge(h_ready, c + 1)
                    to = H[l][c * GC:(c + 1) * GC, :]
                    if l:
                        sp.dma_start(to.rearrange("(t p) d -> p t d", p=P), XD[:, c * GT:(c + 1) * GT, :]).then_inc(h_stored, 16)
                    else:
                        for f in range(FH):
                            sp.dma_start(to[:, f * P:(f + 1) * P].rearrange("(t p) n -> p t n", p=P),
                                         XC[:, c * GT:(c + 1) * GT, f, :]).then_inc(h_stored, 16)

            for l in range(LAYERS3):
                store_rows(l)
                running = S[l][0:EP, :].rearrange("(p t) d -> p (t d)", p=P)
                with sp.Fori(0, ROUNDS) as i:
                    for h in range(2):
                        hold(sp, "sp", max_done, RING + l * CH + RING * i + HALF * (h + 1))
                        sp.dma_start(running[:, bass.ds((RING * i + HALF * h) * D, HALF * D)],
                                     s_ring[:, HALF * h:HALF * (h + 1), :].rearrange("p t d -> p (t d)")).then_inc(max_stored[h], 16)
            for c in range(NG):
                sp.wait_ge(out_ready, c + 2)
                for j in range(GT):
                    t = c * GT + j
                    n = min(P, N - t * P)
                    sp.dma_start(out[t * P:t * P + n, :], XD[0:n, t, :]).then_inc(out_stored, 16)
            sp.wait_ge(out_stored, 16 * NT)

        @block.gpsimd
        def _(pool):
            pool.memset(AT[:, 0, :], 0.0).then_inc(zeros_ready, 1)
            pool.memset(last_before[:, :], -1)
            pool.memset(XA[:, NT - 1, :], 0.0).then_inc(x_zero, 1)
            pool.memset(ones[:, :], 1.0)
            pool.memset(eps_col[:, :], EPS)
            pool.memset(RT[:, :, :], -BIG).then_inc(pool_const, 1)
            pool.wait_ge(pool_const, 1)
            pool.affine_select(out=ident[:, :], in_=ones[:, :], compare_op=ALU.is_equal, fill=0.0, base=0,
                               pattern=[[-1, P]], channel_multiplier=1)
            pool.affine_select(out=before[:, :], in_=ones[:, :], compare_op=ALU.is_gt, fill=0.0, base=0,
                               pattern=[[-1, P]], channel_multiplier=1)
            pool.affine_select(out=upto[:, :], in_=ones[:, :], compare_op=ALU.is_ge, fill=0.0, base=0,
                               pattern=[[1, P]], channel_multiplier=-1)
            pool.affine_select(out=row0[:, :], in_=ones[:, :], compare_op=ALU.is_equal, fill=0.0, base=0,
                               pattern=[[0, P]], channel_multiplier=1)
            pool.iota(iota_i[:, :], pattern=[[1, P]], base=0, channel_multiplier=0).then_inc(pool_const, 1)
            pool.wait_ge(small_ready, 1)
            pool.iota(srcS[:, :].rearrange("p (s q) -> p s q", q=STREAMS), pattern=[[0, TURNS], [P, STREAMS]],
                      base=JUNK, channel_multiplier=1)
            pool.iota(fix_row[:, :], pattern=[[0, 1]], base=-1, channel_multiplier=CH).then_inc(pool_const, 1)

            pool.wait_ge(small_ready, 2)
            pool.partition_all_reduce(reach_all[:, :], reach[:, :], P, bass.bass_isa.ReduceOp.max).then_inc(reach_ready, 1)

            pool.wait_ge(flag_ready, 1)
            serial = pool.value_load(reach_i[0:1, BLOCKS:BLOCKS + 1], min_val=0, max_val=1)

            def scatter(q):
                h, u = divmod(q, WIDE)
                pool.indirect_dma_start(out=A, out_offset=bass.IndirectOffsetOnAxis(ap=idx_out[:, h, u:u + 1], axis=0),
                                        in_=w_out[:, h, u:u + 1], in_offset=None,
                                        compute_op=ALU.add).then_inc(scattered[q], 16)

            def scatter_serially():
                pool.wait_ge(tiles_zero, NT)
                for q in range(STREAMS):
                    pool.wait_ge(scatter_ready, q // WIDE + 1)
                    if q:
                        pool.wait_ge(scattered[q - 1], 16)
                    scatter(q)
                with pool.Fori(1, TURNS) as i:
                    for q in range(STREAMS):
                        if q % WIDE == 0:
                            hold(pool, "pool", scatter_ready, 2 * i + q // WIDE + 1)
                        hold(pool, "pool", scattered[(q - 1) % STREAMS], 16 * (i + 1 if q else i))
                        scatter(q)

            def scatter_turn(i, first=False):
                for h, order in enumerate(((1, 2, 3, 0), (7, 4, 5, 6))):
                    hold(pool, "pool", scatter_ready, 2 * i + h + 1)
                    for q in order:
                        if not first:
                            hold(pool, "pool", scattered[q], 16 * i)
                            if q == 0:
                                hold(pool, "pool", scattered[STREAMS - 1], 16 * i)
                        scatter(q)

            def zeroed(b):
                need = pool.value_load(reach_i[0:1, bass.ds(b, 1)], min_val=1, max_val=NT)
                hold(pool, "pool", tiles_zero, need)

            with pool.If(serial):
                scatter_serially()
            with pool.Else():
                zeroed(0)
                scatter_turn(0, True)
                with pool.Fori(1, RUN) as i:
                    scatter_turn(i)
                with pool.Fori(1, BLOCKS) as b:
                    zeroed(b)
                    with pool.Fori(0, RUN) as i:
                        scatter_turn(b * RUN + i)

            for l in range(LAYERS3):
                pool.wait_ge(h_stored, 16 * NG * (l + FH))

                with pool.Fori(0, ROUNDS) as i:
                    for u in range(RING):
                        if u % HALF == 0:
                            hold(pool, "pool", idx_ready, l * 2 * ROUNDS + 2 * i + u // HALF + 1)
                        hold(pool, "pool", max_done, l * CH + RING * i + u + 1)
                        pool.indirect_dma_start(out=g_ring[:, u, :], out_offset=None, in_=H[l],
                                                in_offset=bass.IndirectOffsetOnAxis(ap=src_idx[:, u:u + 1], axis=0)
                                                ).then_inc(gathered[u], 16)

                for h in range(2):
                    pool.wait_ge(max_stored[h], 16 * ROUNDS * (l + 1))
                pool.indirect_dma_start(out=fix_old[:, :], out_offset=None, in_=S[l],
                                        in_offset=bass.IndirectOffsetOnAxis(ap=fix_row[:, 0:1], axis=0)).then_inc(fix_read, 16)
                pool.wait_ge(fix_ready, l + 1)
                pool.indirect_dma_start(out=S[l], out_offset=bass.IndirectOffsetOnAxis(ap=fix_row[:, 0:1], axis=0),
                                        in_=fix_new[:, :], in_offset=None).then_inc(fix_written, 16)
                pool.wait_ge(fix_written, 16 * (l + 1))
                if l == 0:
                    pool.wait_ge(zero_row_in, 16 * LAYERS3)
                for t in range(NT):
                    if l or t >= GT:
                        pool.wait_ge(tp_ready, TP[f"post{l}"] * NT + t - GT + 1)
                    pool.indirect_dma_start(out=p_ring[:, t % GT, :], out_offset=None, in_=S[l],
                                            in_offset=bass.IndirectOffsetOnAxis(ap=end_row[:, t:t + 1], axis=0)
                                            ).then_inc(pooled[t % GT], 16)

        @block.vector
        def _(v):
            chain = [0]

            def link(ins):
                chain[0] += 1
                ins.then_inc(dve, 1)
                v.wait_ge(dve, chain[0])

            v.sem_inc(rows_read, 2)
            v.sem_inc(z_free, 1)
            v.sem_inc(max_done, RING)
            v.sem_inc(back_free, 1)

            v.wait_ge(edges_in, 16 * N_EDGE_LOADS)
            v.tensor_copy(junk[:, :], srcS[:, :])
            link(v.tensor_copy(eq[:, :], dstS[:, :]))
            v.tensor_scalar(node_lo[:, :].bitcast(I32), dstS[:, :], P - 1, None, ALU.bitwise_and)
            v.tensor_scalar(node_hi[:, :].bitcast(I32), dstS[:, :], 7, None, ALU.logical_shift_right)
            link(v.scalar_tensor_tensor(out=key[:, :], in0=eq[:, :], scalar=float(NP), in1=junk[:, :], op0=ALU.mult, op1=ALU.add))
            v.tensor_copy(node_lo[:, :], node_lo[:, :].bitcast(I32))
            v.tensor_copy(node_hi[:, :], node_hi[:, :].bitcast(I32)).then_inc(small_ready, 1)
            v.wait_ge(pool_const, 3)
            v.tensor_copy(iota_f[:, :], iota_i[:, :])
            link(v.tensor_copy(junk[:, :], srcS[:, :]))
            link(v.tensor_tensor(junk[:, :], junk[:, :], key[:, :], ALU.subtract))
            v.tensor_tensor(eq[:, :], dstC[:, :], dst_next[:, :], ALU.is_gt)
            link(v.tensor_tensor(seg[:, :], dstC[:, :], dst_far[:, :], ALU.is_ge))
            link(v.tensor_tensor(eq[:, :], eq[:, :], seg[:, :], ALU.max))
            v.tensor_reduce(reach[:, 0:BLOCKS], node_hi[:, :].rearrange("p (b e) -> p b e", b=BLOCKS), AX.X, ALU.max)
            v.tensor_reduce(reach[:, BLOCKS:BLOCKS + 1], eq[:, :], AX.X, ALU.max).then_inc(small_ready, 1)
            v.wait_ge(reach_ready, 1)
            link(v.tensor_scalar(reach[0:1, 0:BLOCKS], reach_all[0:1, 0:BLOCKS], 1.0, 1.0, ALU.mult, ALU.add))
            v.tensor_copy(reach_i[:, 0:BLOCKS], reach[0:1, 0:BLOCKS])
            v.tensor_copy(reach_i[:, BLOCKS:BLOCKS + 1], reach_all[0:1, BLOCKS:BLOCKS + 1]).then_inc(flag_ready, 1)

            def merge(i, h, first=False):
                s = 2 * i + h
                at = WIDE * s
                v.tensor_tensor(hot_lo[:, h, :, :], node_lo[:, bass.ds(at, WIDE)].unsqueeze(2).to_broadcast([P, WIDE, P]),
                                iota_f[:, :].unsqueeze(1).to_broadcast([P, WIDE, P]), ALU.is_equal)
                v.tensor_tensor(hot_hi[:, h, :, :], node_hi[:, bass.ds(at, WIDE)].unsqueeze(2).to_broadcast([P, WIDE, NT]),
                                iota_f[:, 0:NT].unsqueeze(1).to_broadcast([P, WIDE, NT]), ALU.is_equal).then_inc(hot_ready, 1)
                hold(v, "dve", w_rows_ready, s + 1)
                for u in range(WIDE):
                    v.scalar_tensor_tensor(out=unused[:, 2 * u, :], in0=bank[2 * h][:, u * P:(u + 1) * P], scalar=key[:, bass.ds(at + u, 1)],
                                           in1=w_rows[:, h, u, :], op0=ALU.is_equal, op1=ALU.mult,
                                           accum_out=w_sum[:, h, u:u + 1])
                    last = v.scalar_tensor_tensor(out=unused[:, 2 * u + 1, :], in0=bank[2 * h][:, u * P:(u + 1) * P],
                                                  scalar=key[:, bass.ds(at + u, 1)], in1=before[:, :],
                                                  op0=ALU.is_equal, op1=ALU.mult, accum_out=repeats[:, h, u:u + 1])
                last.then_inc(rows_read, 1)
                hold(v, "dve", rows_read, s + 3)
                v.scalar_tensor_tensor(out=moved[:, h, :], in0=repeats[:, h, :], scalar=1.0, in1=junk[:, bass.ds(at, WIDE)],
                                       op0=ALU.min, op1=ALU.mult).then_inc(merged, 1)
                hold(v, "dve", merged, s + 1)
                if not first:
                    for u in range(WIDE):
                        hold(v, "dve", scattered[WIDE * h + u], 16 * i)
                v.tensor_copy(w_out[:, h, :], w_sum[:, h, :])
                v.tensor_tensor(idx_out[:, h, :], moved[:, h, :], key[:, bass.ds(at, WIDE)], ALU.add).then_inc(scatter_ready, 1)

            merge(0, 0, True)
            merge(0, 1, True)
            same = dst_far[:, :].bitcast(F32)
            link(v.tensor_copy(eq[:, :], dstC[:, :]))
            v.memset(seg[:, 0:1], 0.0)
            v.tensor_tensor(seg[:, 1:CH], eq[:, 1:CH], eq[:, 0:CH - 1], ALU.is_equal)
            v.tensor_copy(col[:, 1:2], last_before[:, :])
            link(v.tensor_copy(col[:, 2:3], fix_row[:, :]))
            v.tensor_tensor(carry_mask[:, :], eq[:, 0:1], col[:, 1:2], ALU.is_equal)
            v.tensor_tensor(whole_mask[:, :], eq[:, CH - 1:CH], col[:, 1:2], ALU.is_equal)
            link(v.tensor_scalar(same, eq[:, :], eq[:, 0:1], None, ALU.is_equal))
            for m in (seg, carry_mask, whole_mask):
                last = v.tensor_scalar(m[:, :], m[:, :], 2.0, -1.0, ALU.mult, ALU.add)
            link(v.tensor_reduce(col[:, 3:4], same, AX.X, ALU.add))
            for m in (seg, carry_mask):
                v.tensor_scalar(m[:, :], m[:, :], BIG, None, ALU.mult)
            v.tensor_scalar(whole_mask[:, :], whole_mask[:, :], BIG, None, ALU.mult)
            with v.Fori(1, STEPS // 2) as i:
                merge(i, 0)
                merge(i, 1)

            v.wait_ge(hist_done, STEPS)
            link(v.tensor_copy(cnt[:, :], bank[4][:, 0:NT]))
            v.tensor_tensor(fix_row[:, :], col[:, 2:3], col[:, 3:4], ALU.add).then_inc(small_ready, 1)
            v.wait_ge(sums_ready, 1)
            v.tensor_copy(whole_row[:, :], bank[7][:, 0:P])
            link(v.tensor_copy(ends[:, :], bank[6][:, NT:2 * NT]))
            link(v.tensor_tensor_scan(incl[:, :], ones[:, 0:NT], ends[:, :], 0.0, ALU.mult, ALU.add))
            link(v.tensor_tensor(incl[:, :], incl[:, :], ends[:, :], ALU.subtract))
            link(v.tensor_tensor(incl[:, :], incl[:, :], bank[6][:, 0:NT], ALU.add))
            link(v.tensor_scalar(incl[:, :], incl[:, :], -1.0, None, ALU.add))
            v.tensor_scalar(ends[:, :], incl[:, :], -1.0, float(ZERO_ROW), ALU.mult, ALU.add)
            link(v.tensor_scalar(cnt[:, :], cnt[:, :], 0.0, None, ALU.is_equal))
            link(v.tensor_tensor(ends[:, :], ends[:, :], cnt[:, :], ALU.mult))
            link(v.tensor_tensor(end_row[:, :], ends[:, :], incl[:, :], ALU.add))
            v.wait_ge(eps_in, 16)
            v.tensor_scalar(eps1[:, :], eps1[:, :], 1.0, None, ALU.add).then_inc(small_ready, 1)

            class trip:
                def __init__(self, i, start, per):
                    self.value, self.n, self.per = start + i * per, 0, per

                def link(self, ins):
                    self.n += 1
                    ins.then_inc(dve, 1)
                    hold(v, "dve", dve, self.value + self.n)

            def evacuate(c, layer):
                hold(v, "dve", a_used, GT + NT * (NG * layer + c + 1))
                for f in (range(FH) if layer == 2 else (1,)):
                    for o in range(2):
                        at = c * GC + o * PIECE
                        y = bank[2 * f + o][:, 0:PIECE]
                        if layer == 2:
                            v.scalar_tensor_tensor(out=HT[:, f, bass.ds(at, PIECE)], in0=xT[:, f, bass.ds(at, PIECE)],
                                                   scalar=eps1[:, 0:1], in1=y, op0=ALU.mult, op1=ALU.add).then_inc(y_out, 1)
                        else:
                            v.tensor_copy(AT[:, f, bass.ds(at, PIECE)], y).then_inc(y_out, 1)

            def split(layer, c, k, js=range(GT)):
                for j in js:
                    hold(v, "dve", hi_ready, (layer * NT + NG * c + k) * GT + j + 1)
                    v.tensor_tensor(lo_ring[:, j, :], a_ring[:, j, :], hi_ring[:, j, :].bitcast(F32), ALU.subtract).then_inc(split_ready, 1)

            def low_part(ch, c, layer):
                lo = X_LO[layer][:, bass.ds(c * GT, GT), :]
                if layer == 2:
                    x_rows = XC[:, bass.ds(c * GT, GT), :, :]
                    lo = lo.rearrange("p t (h n) -> p t h n", h=FH)
                else:
                    x_rows = (XA, XB)[layer][:, bass.ds(c * GT, GT), :]
                ch.link(v.tensor_copy(lo, x_rows))
                v.tensor_tensor(lo, x_rows, lo.bitcast(F32), ALU.subtract).then_inc(lo_ready, 1)

            class straight:
                def link(self, ins):
                    link(ins)

            def statistics(ch, src):
                for j in range(GT):
                    last = v.bn_stats(stats[:, j, :], src(j))
                ch.link(last)

            def reciprocals(ch, n):
                for j in range(GT):
                    last = v.bn_aggr(mv[:, j, :], stats[:, j, :])
                last.then_inc(var_ready, 1)
                hold(v, "dve", sd_ready, n + 1)
                ch.link(v.reciprocal(rstd[:, :], sd[:, :]))

            def deviations(ch, n, src):
                statistics(ch, src)
                reciprocals(ch, n)

            def scale_rows(src, dst):
                for j in range(GT):
                    last = v.tensor_scalar(dst(j), src(j), mv[:, j, 0:1], rstd[:, j:j + 1], ALU.subtract, ALU.mult)
                return last

            def take(c, stage, other, dst):
                for j in range(GT):
                    hold(v, "dve", z_ready, NT * Z[stage] + GT * c + j + 1)
                    v.tensor_tensor(dst(j), z_bank(stage, j)[:, 0:D], other(j), ALU.add).then_inc(z_free, 1)
                hold(v, "dve", z_free, NT * Z[stage] + GT * c + GT + 1)

            def tile(X, c):
                return lambda j: X[:, bass.ds(c * GT + j, 1), :].rearrange("p t d -> p (t d)")

            def tiles(X, c):
                return X[:, bass.ds(c * GT, GT), :]

            def tile_c(c):
                return lambda j: XC[:, bass.ds(c * GT + j, 1), :, :].rearrange("p t h n -> p (t h) n")

            def take_layer(c, layer, y=tmp):
                dst = lambda j: y[:, j, :]
                if layer == 0:
                    take(c, "L0", tile(XA, c), dst)
                else:
                    take(c, "L1", lambda j: rows["b1L"][0][:, :], dst)

            def sum_layer(ch, c, layer, y=tmp):
                flat_y = y[:, :, :].rearrange("p t d -> p (t d)")
                if layer == 0:
                    ch.link(v.tensor_tensor(y[:, :, :], y[:, :, :], row_group("b0"), ALU.add))
                else:
                    ch.link(v.scalar_tensor_tensor(out=flat_y, in0=flat_y, scalar=0.0, in1=tiles(XB, c).rearrange("p t d -> p (t d)"),
                                                   op0=ALU.max, op1=ALU.add))
                statistics(ch, lambda j: y[:, j, :])

            def norm_layer(c, layer, y=tmp):
                if layer == 0:
                    scale_rows(lambda j: y[:, j, :], tile(XB, c)).then_inc(x_ready, 1)
                else:
                    scale_rows(lambda j: y[:, j, :].rearrange("p (h n) -> p h n", h=FH), tile_c(c)).then_inc(x_ready, 1)
                hold(v, "dve", x_ready, NG * layer + c + 1)

            v.wait_ge(weights_in, 16 * N_WEIGHT_LOADS)
            v.wait_ge(x_in, 32)
            for layer in range(3):
                split(layer, 0, 0, EARLY)
                if layer:
                    done = layer - 1
                    evacuate(NG - 1, done)
                    take_layer(NG - 2, done)
                    take_layer(NG - 1, done, tmp_b)
                low_part(straight(), 0, layer)
                split(layer, 0, 0, LATE)
                low_part(straight(), 1, layer)
                split(layer, 0, 1)
                if layer:
                    sum_layer(straight(), NG - 2, done)
                    reciprocals(straight(), ln(f"L{done}", NG - 2))
                    norm_layer(NG - 2, done)
                low_part(straight(), 2, layer)
                split(layer, 0, 2)
                if layer:
                    sum_layer(straight(), NG - 1, done, tmp_b)
                    reciprocals(straight(), ln(f"L{done}", NG - 1))
                    norm_layer(NG - 1, done, tmp_b)
                low_part(straight(), 3, layer)
                split(layer, 0, 3)
                low_part(straight(), 4, layer)
                split(layer, 0, 4)
                split(layer, 1, 0, EARLY)
                evacuate(0, layer)
                split(layer, 1, 0, LATE)
                for k in range(1, NG):
                    split(layer, 1, k)
                start = chain[0]
                with v.Fori(2, NG) as c:
                    ch = trip(c - 2, start, 3)
                    split(layer, c, 0, EARLY)
                    evacuate(c - 1, layer)
                    if layer < 2:
                        take_layer(c - 2, layer)
                    split(layer, c, 0, LATE)
                    split(layer, c, 1)
                    if layer < 2:
                        sum_layer(ch, c - 2, layer)
                    split(layer, c, 2)
                    if layer < 2:
                        reciprocals(ch, ln(f"L{layer}", c - 2))
                    split(layer, c, 3)
                    if layer < 2:
                        norm_layer(c - 2, layer)
                    split(layer, c, 4)
                if layer < 2:
                    chain[0] = start + 3 * (NG - 2)
            evacuate(NG - 1, 2)
            link(v.memset(s_ring[:, RING - 1, :], 0.0))

            def batch_norm(n, g, be):
                for c in range(NG):
                    for f in range(FH):
                        for o in range(2):
                            v.wait_ge(t_free, 2 + 4 * (NG * n + c) + 2 * f + o + 1)
                            lo = c * GC + o * PIECE
                            last = v.bn_stats(bn_stat[:, f, 2 * c + o, :], xT[:, f, lo:min(lo + PIECE, N)])
                link(last)
                for f in range(FH):
                    last = v.bn_aggr(bn_mv[:, f, :], bn_stat[:, f, :, :].rearrange("p k s -> p (k s)"))
                last.then_inc(bn_var, 1)
                v.wait_ge(bn_sd_ready, n + 1)
                link(v.reciprocal(bn_scale[:, :], bn_sd[:, :]))
                link(v.tensor_tensor(bn_scale[:, :], bn_scale[:, :], cols[g][0][:, :], ALU.mult))
                link(v.tensor_tensor(bn_ms[:, :], bn_mv[:, :, 0], bn_scale[:, :], ALU.mult))
                v.tensor_tensor(bn_shift[:, :], cols[be][0][:, :], bn_ms[:, :], ALU.subtract).then_inc(bn_ready, 1)

            batch_norm(0, "g1", "be1")
            batch_norm(1, "g2", "be2")
            def tiles2(c, start):
                ch = trip(c, start, 2)
                for j in range(GT):
                    hold(v, "dve", back_ready, GT * c + j + 1)
                    v.tensor_tensor(XB[:, bass.ds(c * GT + j, 1), :].rearrange("p t (h n) -> p (t h) n", h=FH),
                                    bank[j % 4][:, 0:D].rearrange("p (h n) -> p h n", h=FH), tile_c(c)(j), ALU.add).then_inc(back_free, 1)
                hold(v, "dve", back_free, GT * c + GT + 1)
                deviations(ch, ln("L2", c), tile(XB, c))
                scale_rows(tile(XB, c), tile(XB, c)).then_inc(x_ready, 1)
                hold(v, "dve", x_ready, XR["L2"] * NG + c + 1)

            start = chain[0]
            with v.Fori(0, NG) as c:
                tiles2(c, start)
            chain[0] = start + 2 * NG

            def running_max(l, i, first=False):
                for u in range(RING):
                    if u % HALF == 0 and not first:
                        hold(v, "dve", max_stored[u // HALF], 16 * (l * ROUNDS + i))
                    hold(v, "dve", gathered[u], 16 * (l * ROUNDS + i + 1))
                    hold(v, "dve", max_done, RING + l * CH + RING * i + u)
                    v.scalar_tensor_tensor(out=s_ring[:, u, :], in0=s_ring[:, (u - 1) % RING, :],
                                           scalar=seg[:, bass.ds(RING * i + u, 1)], in1=g_ring[:, u, :],
                                           op0=ALU.min, op1=ALU.max).then_inc(max_done, 1)

            for l in range(LAYERS3):
                if l == 0:
                    for c in range(NG):
                        running_max(l, c, c == 0)
                        v.tensor_tensor(XB[:, c * GT:(c + 1) * GT, :], XB[:, c * GT:(c + 1) * GT, :], row_group("lb3"), ALU.add)
                with v.Fori(0 if l else NG, ROUNDS) as i:
                    running_max(l, i)
                v.wait_ge(fix_T, l + 1)
                for f in range(FH):
                    last = v.tensor_tensor_scan(RT[:, f, 1:P + 1], whole_row[:, :], bank[0][:, f * P:(f + 1) * P], -BIG,
                                                ALU.min, ALU.max)
                last.then_inc(fix_scan, 1)
                v.wait_ge(fix_back, l + 1)
                v.wait_ge(fix_read, 16 * (l + 1))
                v.scalar_tensor_tensor(out=fix_new[:, :], in0=bank[1][:, 0:D], scalar=carry_mask[:, 0:1], in1=fix_old[:, :],
                                       op0=ALU.min, op1=ALU.max).then_inc(fix_ready, 1)
                def take_post(c):
                    take(c, f"post{l}", tile(PG, c), tile(PG, c))

                if l == 0:
                    with v.Fori(0, NG) as c:
                        take_post(c)
                        v.tensor_scalar(tiles(XD, c).rearrange("p t d -> p (t d)"), tiles(PG, c).rearrange("p t d -> p (t d)"),
                                        0.0, None, ALU.max).then_inc(x_ready, 1)
                    continue

                def begin(ch, c):
                    for j in range(GT):
                        last = v.scalar_tensor_tensor(out=tile(PG, c)(j), in0=tile(PG, c)(j), scalar=0.0, in1=tile(XD, c)(j),
                                                      op0=ALU.max, op1=ALU.add, accum_out=row_sum[:, 0, j:j + 1])
                    ch.link(last)
                    v.tensor_scalar(less_mean[:, 0, :], row_sum[:, 0, :], -1.0 / D, None, ALU.mult).then_inc(mean_ready, 1)
                    hold(v, "dve", mean_ready, means(l, c, 0) + 1)

                def middle(ch, c):
                    g, b = rows[f"lg{l + 1}"][0], rows[f"lb{l + 1}"][0]
                    for j in range(GT):
                        last = v.scalar_tensor_tensor(out=tmp[:, j, :], in0=tile(PG, c)(j), scalar=less_mean[:, 0, j:j + 1],
                                                      in1=g[:, :], op0=ALU.add, op1=ALU.mult)
                    ch.link(last)
                    hold(v, "dve", sd_ready, ln(f"post{l}", c) + 1)
                    ch.link(v.reciprocal(rstd[:, :], sd[:, :]))
                    if l == 1:
                        for j in range(GT):
                            last = v.scalar_tensor_tensor(out=tile(XD, c)(j), in0=tmp[:, j, :], scalar=rstd[:, j:j + 1],
                                                          in1=b[:, :], op0=ALU.mult, op1=ALU.add)
                        last.then_inc(x_ready, 1)
                        hold(v, "dve", x_ready, XR["post1"] * NG + c + 1)
                    else:
                        for j in range(GT):
                            last = v.scalar_tensor_tensor(out=tile(PG, c)(j), in0=tmp[:, j, :], scalar=rstd[:, j:j + 1],
                                                          in1=tile(XB, c)(j), op0=ALU.mult, op1=ALU.add,
                                                          accum_out=row_sum[:, 1, j:j + 1])
                        ch.link(last)
                        v.tensor_scalar(less_mean[:, 1, :], row_sum[:, 1, :], -1.0 / D, None, ALU.mult).then_inc(mean_ready, 1)
                        hold(v, "dve", mean_ready, means(l, c, 1) + 1)

                def end(ch, c):
                    if l == 2:
                        hold(v, "dve", sd_ready, ln("out", c) + 1)
                        hold(v, "dve", out_ready, c + 1)
                        ch.link(v.reciprocal(out_scale[:, :], sd_out[:, :]))
                        v.tensor_tensor(out_shift[:, :], less_mean[:, 1, :], out_scale[:, :], ALU.mult).then_inc(out_scale_ready, 1)
                        hold(v, "dve", out_scale_ready, c + 1)

                take_post(0)
                begin(straight(), 0)
                start, per = chain[0], (0, 3, 5)[l]
                with v.Fori(0, NG - 1) as c:
                    ch = trip(c, start, per)
                    take_post(c + 1)
                    middle(ch, c)
                    begin(ch, c + 1)
                    end(ch, c)
                    assert ch.n == per, (l, ch.n, per)
                chain[0] = start + per * (NG - 1)
                middle(straight(), NG - 1)
                end(straight(), NG - 1)

        @block.scalar
        def _(act):
            act.sem_inc(tp_free, 1)
            act.sem_inc(out_ready, 1)
            act.sem_inc(t_free, 2)
            def copy_cols(i, h):
                s = 2 * i + h
                hold(act, "act", rows_ready, s + 1)
                act.activation(key_cols[:, h, :], key[:, bass.ds(WIDE * s, WIDE)], ACT.Copy)
                act.activation(w_cols[:, h, :], wS[:, bass.ds(WIDE * s, WIDE)], ACT.Copy).then_inc(cols_ready, 1)

            def copy_rows(i, h):
                s = 2 * i + h
                hold(act, "act", rows_read, s + 1)
                hold(act, "act", rows_ready, s + 3)
                act.activation(w_rows[:, h, :, :].rearrange("p q n -> p (q n)"), bank[2 * h + 1][:, :], ACT.Copy).then_inc(w_rows_ready, 1)

            act.wait_ge(small_ready, 1)
            for h in range(2):
                copy_cols(0, h)
            with act.Fori(0, STEPS // 2 - 1) as i:
                for h in range(2):
                    copy_rows(i, h)
                    copy_cols(i + 1, h)
            for h in range(2):
                copy_rows(STEPS // 2 - 1, h)

            def evacuate(c, layer):
                hold(act, "act", a_used, GT + NT * (NG * layer + c + 1))
                for o in range(2):
                    act.activation(AT[:, 0, bass.ds(c * GC + o * PIECE, PIECE)], bank[o][:, 0:PIECE], ACT.Copy).then_inc(y_out, 1)

            def deviation(n):
                hold(act, "act", var_ready, n + 1)
                act.activation(sd[:, :], mv[:, :, 1], ACT.Sqrt, bias=eps_col[:, 0:1]).then_inc(sd_ready, 1)

            def turned_one(c, j, r, dst):
                hold(act, "act", tp_ready, NT * r + GT * c + j + 1)
                act.activation(dst, bank[6 + j % 2][:, 0:D].rearrange("p (h n) -> p h n", h=FH), ACT.Copy).then_inc(tp_free, 1)

            def turned(c, r, dst):
                for j in range(GT):
                    turned_one(c, j, r, dst(j))

            def turn_x(c, r):
                turned(c, r, lambda j: xT[:, :, bass.ds(c * GC + j * P, P)])

            def high_parts(layer, c, k, js=range(GT)):
                if layer:
                    act.wait_ge(x_ready, NG * (layer - 1) + k + 1)
                for j in js:
                    hold(act, "act", a_in[j], 16 * (layer * NT + NG * c + k + 1))
                    act.activation(hi_ring[:, j, :], a_ring[:, j, :], ACT.Copy)
                    t = k * GT + j
                    if layer == 2:
                        x_tile, dst = XC[:, t, :, :], x_hi_ring[:, j, :].rearrange("p (h n) -> p h n", h=FH)
                    else:
                        x_tile, dst = (XA, XB)[layer][:, t, :], x_hi_ring[:, j, :]
                    act.activation(dst, x_tile, ACT.Copy).then_inc(hi_ready, 1)

            def take_t(c, n, b, dst):
                for f in range(FH):
                    for o in range(2):
                        hold(act, "act", t_ready, 4 * (NG * n + c) + 2 * f + o + 1)
                        ins = act.activation(dst[:, f, bass.ds(c * GC + o * PIECE, PIECE)], t_bank(n, f, o)[:, 0:PIECE], ACT.Identity,
                                             bias=cols[b][0][:, f:f + 1])
                        ins.then_inc(t_free, 1)

            def bn_deviation(n):
                act.wait_ge(bn_var, n + 1)
                act.activation(bn_sd[:, :], bn_mv[:, :, 1], ACT.Sqrt, bias=eps_col[:, 0:1]).then_inc(bn_sd_ready, 1)
                act.wait_ge(bn_ready, n + 1)

            def rectify(c):
                for f in range(FH):
                    last = act.activation(HT[:, f, bass.ds(c * GC, GC)], xT[:, f, bass.ds(c * GC, GC)], ACT.Relu,
                                          scale=bn_scale[:, f:f + 1], bias=bn_shift[:, f:f + 1])
                last.then_inc(r_ready, 1)

            for layer in range(3):
                high_parts(layer, 0, 0, EARLY)
                if layer:
                    evacuate(NG - 1, layer - 1)
                    turn_x(0, TP[f"L{layer}"])
                high_parts(layer, 0, 0, LATE)
                high_parts(layer, 0, 1)
                if layer:
                    deviation(ln(f"L{layer - 1}", NG - 2))
                high_parts(layer, 0, 2)
                if layer:
                    deviation(ln(f"L{layer - 1}", NG - 1))
                high_parts(layer, 0, 3)
                high_parts(layer, 0, 4)

                def group(c, complete):
                    high_parts(layer, c, 0, EARLY)
                    if layer < 2:
                        evacuate(c - 1, layer)
                    high_parts(layer, c, 0, LATE)
                    if layer == 2 and complete:
                        take_t(c - 2, 0, "b1", xT)
                    if layer:
                        turn_x(c, TP[f"L{layer}"])
                    high_parts(layer, c, 1)
                    high_parts(layer, c, 2)
                    if layer < 2 and complete:
                        deviation(ln(f"L{layer}", c - 2))
                    high_parts(layer, c, 3)
                    high_parts(layer, c, 4)

                group(1, False)
                with act.Fori(2, NG) as c:
                    group(c, True)
            take_t(NG - 2, 0, "b1", xT)
            take_t(NG - 1, 0, "b1", xT)
            bn_deviation(0)
            rectify(0)
            with act.Fori(1, NG) as c:
                rectify(c)
                take_t(c - 1, 1, "b2", xT)
            take_t(NG - 1, 1, "b2", xT)
            bn_deviation(1)
            with act.Fori(0, NG) as c:
                rectify(c)

            def prepare(c):
                for j in range(GT):
                    hold(act, "act", z_ready, NT * Z["prep"] + GT * c + j + 1)
                    last = act.activation(XC[:, bass.ds(c * GT + j, 1), :, :].rearrange("p t h n -> p (t h) n"),
                                          z_bank("prep", j)[:, 0:D].rearrange("p (h n) -> p h n", h=FH), ACT.Relu)
                    last.then_inc(z_free, 1)
                hold(act, "act", z_free, NT * Z["prep"] + GT * c + GT + 1)
                act.sem_inc(h_ready, 1)

            deviation(ln("L2", 0))
            with act.Fori(1, NG) as c:
                turn_x(c - 1, TP["prep"])
                deviation(ln("L2", c))
                prepare(c - 1)
            turn_x(NG - 1, TP["prep"])
            prepare(NG - 1)


            def stage(l, i, h, first=False):
                if not first:
                    for u in range(HALF * h, HALF * (h + 1)):
                        hold(act, "act", gathered[u], 16 * (l * ROUNDS + i))
                act.activation(src_idx[:, HALF * h:HALF * (h + 1)], srcC[:, bass.ds(RING * i + HALF * h, HALF)],
                               ACT.Copy).then_inc(idx_ready, 1)

            for l in range(LAYERS3):
                for h in range(2):
                    stage(l, 0, h, l == 0)
                with act.Fori(0, NG) as c:
                    for j in range(GT):
                        t = c * GT + j
                        for h in range(2):
                            stage(l, t + 1, h)
                        if l:
                            turned_one(c, j, TP[f"part{l}"], xT[:, :, bass.ds(c * GC + j * P, P)])
                        hold(act, "act", z_ready, NT * Z[f"part{l}"] + t + 1)
                        act.activation(PG[:, bass.ds(t, 1), :].rearrange("p t d -> p (t d)"), bank[4 + j % 2][:, 0:D], ACT.Copy).then_inc(z_free, 1)
                with act.Fori(NT + 1, ROUNDS) as i:
                    for h in range(2):
                        stage(l, i, h)

                def turn_pooled(c, js):
                    for j in js:
                        turned_one(c, j, TP[f"post{l}"], pT[:, j, :, :])

                def deviations(c, which, dst):
                    hold(act, "act", mean_ready, means(l, c, which) + 1)
                    for j in range(GT):
                        last = act.activation(squares[:, j, :], PG[:, bass.ds(c * GT + j, 1), :].rearrange("p t d -> p (t d)"),
                                              ACT.Square, bias=less_mean[:, which, j:j + 1], accum_out=sq_sum[:, which, j:j + 1])
                    last.then_inc(squared, 1)
                    hold(act, "act", squared, means(l, c, which) + 1)
                    act.activation(dst[:, :], sq_sum[:, which, :], ACT.Sqrt, bias=eps_col[:, 0:1], scale=1.0 / D).then_inc(sd_ready, 1)

                def finish(c, after=None):
                    def turn_next(js):
                        if after is not None:
                            turn_pooled(after, js)

                    turn_next((0, 1))
                    if l:
                        deviations(c, 0, sd)
                    turn_next((2, 3))
                    if l == 2:
                        deviations(c, 1, sd_out)
                    turn_next((4,))
                    if l == 2:
                        hold(act, "act", out_scale_ready, c + 1)
                        for j in range(GT):
                            t = bass.ds(c * GT + j, 1)
                            last = act.activation(XD[:, t, :].rearrange("p t d -> p (t d)"), PG[:, t, :].rearrange("p t d -> p (t d)"),
                                                  ACT.Identity, scale=out_scale[:, j:j + 1], bias=out_shift[:, j:j + 1])
                        last.then_inc(out_ready, 1)

                turn_pooled(0, range(GT))
                turn_pooled(1, range(GT))
                with act.Fori(0, NG - 2) as c:
                    finish(c, c + 2)
                finish(NG - 2)
                finish(NG - 1)

        @block.tensor
        def _(pe):
            pe.sem_inc(rows_ready, 2)
            pe.sem_inc(a_used, GT)

            pe.wait_ge(pool_const, 2)
            def edge_step(i, h, start=False, stop=False):
                s = 2 * i + h
                hold(pe, "pe", rows_read, s + 1)
                hold(pe, "pe", cols_ready, s + 1)
                for u in range(WIDE):
                    pe.transpose(bank[2 * h][:, u * P:(u + 1) * P], key_cols[:, h, u:u + 1].to_broadcast([P, P]), ident[:, :])
                    last = pe.transpose(bank[2 * h + 1][:, u * P:(u + 1) * P], w_cols[:, h, u:u + 1].to_broadcast([P, P]), ident[:, :])
                last.then_inc(rows_ready, 1)
                hold(pe, "pe", hot_ready, s + 1)
                for u in range(WIDE):
                    last = pe.matmul(bank[4][:, 0:NT], hot_lo[:, h, u, :], hot_hi[:, h, u, :],
                                     start=start and u == 0, stop=stop and u == WIDE - 1)
                last.then_inc(hist_done, 1)

            edge_step(0, 0, start=True)
            edge_step(0, 1)
            with pe.Fori(1, STEPS // 2 - 1) as i:
                edge_step(i, 0)
                edge_step(i, 1)
            edge_step(STEPS // 2 - 1, 0)
            edge_step(STEPS // 2 - 1, 1, stop=True)

            pe.wait_ge(small_ready, 3)
            pe.matmul(bank[6][:, 0:NT], upto[:, :], cnt[:, :], start=True, stop=True)
            pe.matmul(bank[6][:, NT:2 * NT], ones[:, :], cnt[:, :], start=True, stop=True)
            pe.transpose(bank[7][:, 0:P], whole_mask[:, 0:1].to_broadcast([P, P]), ident[:, :]).then_inc(sums_ready, 1)

            def turn_one(src, c, j, r):
                g = NT * r + GT * c + j
                pe.wait_ge(tp_free, g if j else g + 1)
                for f in range(FH):
                    last = pe.transpose(bank[6 + j % 2][:, f * P:(f + 1) * P], src(j, f), ident[:, :])
                last.then_inc(tp_ready, 1)

            def turn(src, c, r):
                for j in range(GT):
                    turn_one(src, c, j, r)

            def tile_of(X, c):
                return lambda j, f: X[:, c * GT + j, f * P:(f + 1) * P]

            def tile_h(c):
                return lambda j, f: XC[:, c * GT + j, f, :]

            def aggregate(c, layer):
                pe.wait_ge(y_out, 4 * (NG * layer + c) + y_start)
                for k in range(NG):
                    m = layer * NT + NG * c + k
                    if c == 0:
                        pe.wait_ge(lo_ready, NG * layer + k + 1)
                    for j in range(GT):
                        pe.wait_ge(split_ready, m * GT + j + 1)
                        first, final = k == 0 and j == 0, k == NG - 1 and j == GT - 1
                        a_hi = [hi_ring[:, j, o * PIECE:(o + 1) * PIECE] for o in range(2)]
                        a_lo = [lo_ring[:, j, o * PIECE:(o + 1) * PIECE] for o in range(2)]
                        for f in range(FH):
                            x_hi = x_hi_ring[:, j, f * P:(f + 1) * P]
                            x_lo = X_LO[layer][:, k * GT + j, f * P:(f + 1) * P]
                            for o in range(2):
                                pe.matmul(bank[2 * f + o][:, 0:PIECE], x_hi, a_hi[o], start=first, stop=False)
                            for o in range(2):
                                pe.matmul(bank[2 * f + o][:, 0:PIECE], x_hi, a_lo[o], start=False, stop=False)
                            for o in range(2):
                                last = pe.matmul(bank[2 * f + o][:, 0:PIECE], x_lo, a_hi[o], start=False, stop=final)
                        last.then_inc(a_used, 1)

            y_start = 1
            pe.sem_inc(y_out, 1)

            def product(c, stage, terms, j):
                pe.wait_ge(z_free, z_out(stage, c, j))
                for n, (lhs, rhs) in enumerate(terms):
                    last = pe.matmul(z_bank(stage, j)[:, 0:D], lhs, rhs, start=n == 0, stop=n == len(terms) - 1)
                last.then_inc(z_ready, 1)

            def nodes(B, c, j, f):
                return B[:, f, bass.ds(c * GC + j * P, P)]

            def dense0(c):
                pe.wait_ge(y_out, 4 * (NG * 0 + c) + 4 + y_start)
                for j in range(GT):
                    product(c, "L0", [(nodes(AT, c, j, f), W0s[:, f, :]) for f in range(FH)], j)

            def dense1(c):
                pe.wait_ge(y_out, 4 * (NG * 1 + c) + 4 + y_start)
                pe.wait_ge(tp_free, 1 + NT * TP["L1"] + GT * c + GT)
                for j in range(GT):
                    product(c, "L1", [(nodes(B, c, j, f), W1Ls[:, FH * n + f, :]) for n, B in enumerate((xT, AT)) for f in range(FH)], j)

            def block_product(c, n, w):
                for f in range(FH):
                    for o in range(2):
                        g = 4 * (NG * n + c) + 2 * f + o
                        pe.wait_ge(t_free, g - 1 if n and (c or f) else g + 1)
                        for k in range(FH):
                            last = pe.matmul(t_bank(n, f, o)[:, 0:PIECE], w[:, k, f * P:(f + 1) * P],
                                             HT[:, k, bass.ds(c * GC + o * PIECE, PIECE)], start=k == 0, stop=k == FH - 1)
                        last.then_inc(t_ready, 1)

            pe.wait_ge(x_in, 32)
            pe.wait_ge(weights_in, 16 * N_WEIGHT_LOADS)
            pe.wait_ge(small_ready, 4)
            aggregate(0, 0)
            for c in range(1, NG):
                aggregate(c, 0)
                dense0(c - 1)
            dense0(NG - 1)

            pe.wait_ge(x_ready, 1)
            turn(tile_of(XB, 0), 0, TP["L1"])
            aggregate(0, 1)
            for c in range(1, NG):
                turn(tile_of(XB, c), c, TP["L1"])
                aggregate(c, 1)
                dense1(c - 1)
            dense1(NG - 1)

            def dense2(c):
                pe.wait_ge(y_out, 4 * (NG * 2 + c) + 4 + y_start)
                block_product(c, 0, W1s)

            pe.wait_ge(x_ready, NG + 1)
            pe.wait_ge(z_free, 1 + 2 * NT)
            turn(tile_h(0), 0, TP["L2"])
            pe.wait_ge(tp_free, 1 + NT * TP["L2"] + GT)
            aggregate(0, 2)
            for c in range(1, NG):
                turn(tile_h(c), c, TP["L2"])
                pe.wait_ge(tp_free, 1 + NT * TP["L2"] + GT * c + GT)
                aggregate(c, 2)
                dense2(c - 1)
            dense2(NG - 1)
            for c in range(NG):
                pe.wait_ge(r_ready, c + 1)
                block_product(c, 1, W2s)
            pe.wait_ge(t_free, 2 + 8 * NG)
            for c in range(NG + 1):
                if c < NG:
                    pe.wait_ge(r_ready, NG + c + 1)
                    for j in range(GT):
                        g = GT * c + j
                        pe.wait_ge(back_free, max(1, g + (1, -3, -3, -3, -2)[j]))
                        for f in range(FH):
                            last = pe.transpose(bank[j % 4][:, f * P:(f + 1) * P], nodes(HT, c, j, f), ident[:, :])
                        last.then_inc(back_ready, 1)
                if c:
                    pe.wait_ge(x_ready, NG * XR["L2"] + c)
                    turn(tile_of(XB, c - 1), c - 1, TP["prep"])
                    pe.wait_ge(tp_free, 1 + NT * TP["prep"] + GT * c)
                    for j in range(GT):
                        product(c - 1, "prep", [(nodes(xT, c - 1, j, f), Wps[:, f, :]) for f in range(FH)]
                                + [(row0[:, :], rows["bp"][0][:, :])], j)

            for l, Wm in enumerate((Wm1s, Wm2s, Wm3s)):
                for c in range(NG):
                    if l:
                        pe.wait_ge(x_ready, NG * XR[f"post{l - 1}"] + c + 1)
                    for j in range(GT):
                        if l:
                            turn_one(tile_of(XD, c), c, j, TP[f"part{l}"])
                            pe.wait_ge(tp_free, 1 + NT * TP[f"part{l}"] + GT * c + j + 1)
                        product(c, f"part{l}", [(nodes(xT, c, j, f), Wm[:, f, :]) for f in range(FH)]
                                + [(row0[:, :], rows[f"bm{l + 1}"][0][:, :])], j)
                pe.wait_ge(max_done, RING + CH * (l + 1))
                for f in range(FH):
                    last = pe.transpose(bank[0][:, f * P:(f + 1) * P], s_ring[:, RING - 1, f * P:(f + 1) * P], ident[:, :])
                last.then_inc(fix_T, 1)
                pe.wait_ge(fix_scan, l + 1)
                for f in range(FH):
                    last = pe.transpose(bank[1][:, f * P:(f + 1) * P], RT[:, f, 0:P], ident[:, :])
                last.then_inc(fix_back, 1)
                pe.wait_ge(z_free, 1 + NT * (Z[f"part{l}"] + 1))

                def turn_pooled(t):
                    c, j = divmod(t, GT)
                    g = NT * TP[f"post{l}"] + t
                    pe.wait_ge(pooled[j], 16 * (NG * l + c + 1))
                    pe.wait_ge(tp_free, g if j else g + 1)
                    for f in range(FH):
                        last = pe.transpose(bank[6 + j % 2][:, f * P:(f + 1) * P], p_ring[:, j, f * P:(f + 1) * P], ident[:, :])
                    last.then_inc(tp_ready, 1)

                turn_pooled(0)
                for t in range(NT):
                    if t + 1 < NT:
                        turn_pooled(t + 1)
                    c, j = divmod(t, GT)
                    pe.wait_ge(tp_free, NT * TP[f"post{l}"] + t + 2)
                    product(c, f"post{l}", [(pT[:, j, f, :], Wm[:, FH + f, :]) for f in range(FH)], j)


def kernel(**inputs):
    import concourse.bacc as _bacc
    from concourse.bass_utils import run_bass_kernel_spmd as _run

    def arr(name):
        return np.asarray(inputs[name])

    def padded(a, fill, n=EP):
        return np.concatenate([a, np.full(n - a.shape[0], fill, a.dtype)])

    def in_steps(a):
        return np.ascontiguousarray(a.reshape(BLOCKS, STREAMS, RUN, P).transpose(3, 0, 2, 1).reshape(P, CH))

    src, w = padded(arr("src"), 0), padded(arr("edge_weight"), 0)
    dst = padded(arr("dst"), PAD_DST)
    given = {
        "src_steps": in_steps(src), "dst_steps": in_steps(dst), "w_steps": in_steps(w),
        "src_chunks": src.reshape(P, CH), "dst_flat": padded(dst, END_DST, EP + FAR),
        "x": arr("x"), "W0": arr("L0_gnn_weight"), "b0": arr("L0_gnn_bias"), "W1L": arr("L1_gnn_W"), "b1L": arr("L1_gnn_b"),
        "eps": arr("L2_gnn_eps"), "W1": arr("L2_gnn_W1"), "b1": arr("L2_gnn_b1"), "g1": arr("L2_gnn_g1"), "be1": arr("L2_gnn_be1"),
        "W2": arr("L2_gnn_W2"), "b2": arr("L2_gnn_b2"), "g2": arr("L2_gnn_g2"), "be2": arr("L2_gnn_be2"),
        "Wp": arr("L3_gnn_Wp1").T, "bp": arr("L3_gnn_bp1"), "Wm1": arr("L3_gnn_Wm1").T, "bm1": arr("L3_gnn_bm1"),
        "Wm2": arr("L3_gnn_Wm2").T, "bm2": arr("L3_gnn_bm2"), "Wm3": arr("L3_gnn_Wm3").T, "bm3": arr("L3_gnn_bm3"),
        "lg2": arr("L3_gnn_ln2_g"), "lb2": arr("L3_gnn_ln2_b"), "lg3": arr("L3_gnn_ln3_g"), "lb3": arr("L3_gnn_ln3_b"),
    }
    nc = _bacc.Bacc("TRN2", target_bir_lowering=False, num_devices=1)
    arrays, args = {}, []
    for name, a in given.items():
        a = np.ascontiguousarray(a)
        arrays[f"in_{name}"] = a
        args.append(nc.dram_tensor(f"in_{name}", a.shape, mybir.dt.from_np(a.dtype), kind="ExternalInput").ap())
    args.append(nc.dram_tensor("out_0", (N, D), F32, kind="ExternalOutput").ap())
    build(nc, *args)
    r = _run(nc, [arrays], core_ids=[0])
    return r.results[0]["out_0"]
```
